# Optimizing a Trainium2 kernel written in Bass

```python
import numpy as np
import jax
import jax.numpy as jnp

def _softmax(x, axis=-1):
    return jax.nn.softmax(x, axis=axis)

def _gelu(x):
    return jax.nn.gelu(x, approximate=True)

def _silu(x):
    return jax.nn.silu(x)

def _sigmoid(x):
    return jax.nn.sigmoid(x)

def _layernorm(x, axis=-1, eps=1e-05):
    m = jnp.mean(x, axis=axis, keepdims=True)
    v = jnp.var(x, axis=axis, keepdims=True)
    return (x - m) / jnp.sqrt(v + eps)

def _scatter_add(tgt, idx, src, axis=0):
    return tgt.at[idx].add(src)

def _segment_sum(src, seg, n):
    return jax.ops.segment_sum(src, seg, n)
kernel_name = 'mk_recurrent_d2_jaxref_r8_8d0fa4'

def setup_inputs(seed: int=0):
    np.random.seed(seed)
    _w = jnp.asarray

    def _L0_attn_setup():
        import jax, jax.numpy as jnp
        import numpy as np
        B, N, D, H = (2, 256, 128, 8)
        HD = D // H
        EPS = 1e-06

        def _interleave(a, b):
            return jnp.stack([a, b], axis=2).reshape(a.shape[0], 2 * a.shape[1], a.shape[2], a.shape[3])

        def _l2norm(x):
            return x / jnp.sqrt(jnp.sum(x * x, axis=-1, keepdims=True) + EPS)

        def _dense_rnn(x, Wq, Wk, Wv, Wf1, Wf2, Wbeta, Wog1, Wog2, norm_w, Wo):
            b, n, d = x.shape
            q = jax.nn.silu(x @ Wq)
            k = jax.nn.silu(x @ Wk)
            v = jax.nn.silu(x @ Wv)
            f = x @ Wf1 @ Wf2
            log_f = jax.nn.log_sigmoid(f)
            beta = jax.nn.sigmoid(x @ Wbeta) * 2.0
            shp = (b, n, H, HD)
            q, k, v, log_f = (t.reshape(shp) for t in (q, k, v, log_f))
            k = _l2norm(k)
            k_ = -beta[..., None] * k
            zero = jnp.zeros(shp, x.dtype)
            gk = _interleave(log_f, zero)
            a = _interleave(k_ * jnp.exp(log_f), k_)
            bb = _interleave(k, k)
            kk = _interleave(zero, k)
            vv = _interleave(zero, v)
            qq = _interleave(zero, q)
            seq = tuple((jnp.moveaxis(t, 1, 0) for t in (gk, a, bb, kk, vv, qq)))
            S0 = jnp.zeros((b, H, HD, HD), x.dtype)

            def step(S, inp):
                g, a_t, b_t, k_t, v_t, q_t = inp
                bS = jnp.einsum('bhk,bhkv->bhv', b_t, S)
                S = jnp.exp(g)[..., None] * S + a_t[..., None] * bS[:, :, None, :] + k_t[..., None] * v_t[:, :, None, :]
                o = jnp.einsum('bhk,bhkv->bhv', q_t, S)
                return (S, o)
            _, o = jax.lax.scan(step, S0, seq)
            o = jnp.moveaxis(o, 0, 1)[:, 1::2]
            out = o.reshape(b, n, d)
            gate = x @ Wog1 @ Wog2
            y = out * jax.nn.sigmoid(gate)
            yh = y.reshape(b, n, H, HD)
            yh = yh / jnp.sqrt(jnp.mean(yh * yh, axis=-1, keepdims=True) + EPS)
            y = yh.reshape(b, n, d) * norm_w
            return y @ Wo
        key = jax.random.key(seed)
        ks = jax.random.split(key, 11)
        std = 0.02
        w = lambda k, shape: jax.random.normal(k, shape, dtype=jnp.float32) * std
        return {'x': jax.random.normal(ks[0], (B, N, D), dtype=jnp.float32), 'Wq': w(ks[1], (D, D)), 'Wk': w(ks[2], (D, D)), 'Wv': w(ks[3], (D, D)), 'Wf1': w(ks[4], (D, HD)), 'Wf2': w(ks[5], (HD, D)), 'Wbeta': w(ks[6], (D, H)), 'Wog1': w(ks[7], (D, HD)), 'Wog2': w(ks[8], (HD, D)), 'norm_w': jnp.ones((D,), dtype=jnp.float32), 'Wo': w(ks[9], (D, D))}
    _L0_attn_in = _L0_attn_setup()

    def _L0_ffn_setup():
        import jax, jax.numpy as jnp
        import numpy as np
        B, S, H = (2, 256, 128)
        E, F, K = (64, 64, 8)
        G, TG = (8, 4)
        SCALE = 2.5
        F_SH = 64

        def _gate(x, gate_w, gate_bias):
            scores = jax.nn.sigmoid(x @ gate_w.T)
            sc = scores + gate_bias[None, :]
            T = x.shape[0]
            group_scores = jax.lax.top_k(sc.reshape(T, G, E // G), 2)[0].sum(-1)
            _, gidx = jax.lax.top_k(group_scores, TG)
            gmask = jnp.zeros((T, G), sc.dtype).at[jnp.arange(T)[:, None], gidx].set(1.0)
            smask = jnp.repeat(gmask, E // G, axis=1)
            masked = jnp.where(smask > 0, sc, -jnp.inf)
            _, tidx = jax.lax.top_k(masked, K)
            tw = jnp.take_along_axis(scores, tidx, axis=1)
            tw = tw / (tw.sum(-1, keepdims=True) + 1e-20)
            return (tidx, tw * SCALE)
        key = jax.random.key(seed)
        ks = jax.random.split(key, 9)

        def w(k, shape, fan_in):
            return jax.random.normal(k, shape, jnp.float32) / np.float32(np.sqrt(fan_in))
        return {'hidden_states': jax.random.normal(ks[0], (B, S, H), jnp.float32), 'gate_w': w(ks[1], (E, H), H), 'gate_bias': jax.random.normal(ks[2], (E,), jnp.float32) * 0.01, 'We_gate': w(ks[3], (E, H, F), H), 'We_up': w(ks[4], (E, H, F), H), 'We_down': w(ks[5], (E, F, H), F), 'Ws_gate': w(ks[6], (H, F_SH), H), 'Ws_up': w(ks[7], (H, F_SH), H), 'Ws_down': w(ks[8], (F_SH, H), F_SH)}
    _L0_ffn_in = _L0_ffn_setup()

    def _L1_attn_setup():
        import jax, jax.numpy as jnp
        import numpy as np
        import math
        B, S, E = (2, 256, 128)
        H, DC, DR = (16, 32, 128)
        HD = E // H

        def _linear_params(key, din, dout):
            k1, k2 = jax.random.split(key)
            bound = 1.0 / math.sqrt(din)
            w = jax.random.uniform(k1, (din, dout), minval=-bound, maxval=bound, dtype=jnp.float32)
            b = jax.random.uniform(k2, (dout,), minval=-bound, maxval=bound, dtype=jnp.float32)
            return (w, b)

        def _gelu(x):
            return jax.nn.gelu(x, approximate=False)

        def _rope_cos_sin(seq_len, d_rope):
            inv_freq = 1.0 / 10000.0 ** (jnp.arange(0, d_rope, 2, dtype=jnp.float32) / d_rope)
            t = jnp.arange(seq_len, dtype=jnp.float32)
            freqs = t[:, None] * inv_freq[None, :]
            emb = jnp.concatenate([freqs, freqs], axis=-1)
            return (jnp.cos(emb), jnp.sin(emb))

        def _apply_rope(x, cos, sin):
            d = x.shape[-1]
            x1, x2 = (x[..., :d // 2], x[..., d // 2:])
            rot = jnp.concatenate([-x2, x1], axis=-1)
            return x * cos + rot * sin
        key = jax.random.key(seed)
        ks = jax.random.split(key, 10)
        x = jax.random.normal(ks[0], (B, S, E), dtype=jnp.float32)
        wq, bq = _linear_params(ks[1], E, DC)
        wqc, bqc = _linear_params(ks[2], DC, E - DR)
        wqr, bqr = _linear_params(ks[3], E, DR)
        wkv, bkv = _linear_params(ks[4], E, DC)
        wkr, bkr = _linear_params(ks[5], E, DR)
        wkc, bkc = _linear_params(ks[6], DC, E - DR)
        wv, bv = _linear_params(ks[7], DC, E)
        wo, bo = _linear_params(ks[8], E, E)
        return dict(x=x, wq=wq, bq=bq, wqc=wqc, bqc=bqc, wqr=wqr, bqr=bqr, wkv=wkv, bkv=bkv, wkr=wkr, bkr=bkr, wkc=wkc, bkc=bkc, wv=wv, bv=bv, wo=wo, bo=bo)
    _L1_attn_in = _L1_attn_setup()

    def _L1_ffn_setup():
        import jax, jax.numpy as jnp
        import numpy as np
        N_EXPERTS = 16
        TOP_K = int(N_EXPERTS * 0.2)
        EPS = 1e-12
        key = jax.random.key(seed)
        ks = jax.random.split(key, 6)
        B, T, D, H, E = (4, 128, 128, 256, N_EXPERTS)
        x = jax.random.normal(ks[0], (B, T, D), dtype=jnp.float32)
        gate = jax.random.normal(ks[1], (D, E), dtype=jnp.float32)
        W1 = jax.random.normal(ks[2], (E, D, H), dtype=jnp.float32) * (1.0 / np.sqrt(D))
        b1 = jax.random.normal(ks[3], (E, H), dtype=jnp.float32) * 0.02
        W2 = jax.random.normal(ks[4], (E, H, D), dtype=jnp.float32) * (1.0 / np.sqrt(H))
        b2 = jax.random.normal(ks[5], (E, D), dtype=jnp.float32) * 0.02
        return {'x': x, 'gate': gate, 'W1': W1, 'b1': b1, 'W2': W2, 'b2': b2}
    _L1_ffn_in = _L1_ffn_setup()
    _d = {'L0_attn_x': _L0_attn_in['x'], 'L0_attn_Wq': _L0_attn_in['Wq'], 'L0_attn_Wk': _L0_attn_in['Wk'], 'L0_attn_Wv': _L0_attn_in['Wv'], 'L0_attn_Wf1': _L0_attn_in['Wf1'], 'L0_attn_Wf2': _L0_attn_in['Wf2'], 'L0_attn_Wbeta': _L0_attn_in['Wbeta'], 'L0_attn_Wog1': _L0_attn_in['Wog1'], 'L0_attn_Wog2': _L0_attn_in['Wog2'], 'L0_attn_norm_w': _L0_attn_in['norm_w'], 'L0_attn_Wo': _L0_attn_in['Wo'], 'L0_ffn_gate_w': _L0_ffn_in['gate_w'], 'L0_ffn_gate_bias': _L0_ffn_in['gate_bias'], 'L0_ffn_We_gate': _L0_ffn_in['We_gate'], 'L0_ffn_We_up': _L0_ffn_in['We_up'], 'L0_ffn_We_down': _L0_ffn_in['We_down'], 'L0_ffn_Ws_gate': _L0_ffn_in['Ws_gate'], 'L0_ffn_Ws_up': _L0_ffn_in['Ws_up'], 'L0_ffn_Ws_down': _L0_ffn_in['Ws_down'], 'L1_attn_wq': _L1_attn_in['wq'], 'L1_attn_bq': _L1_attn_in['bq'], 'L1_attn_wqc': _L1_attn_in['wqc'], 'L1_attn_bqc': _L1_attn_in['bqc'], 'L1_attn_wqr': _L1_attn_in['wqr'], 'L1_attn_bqr': _L1_attn_in['bqr'], 'L1_attn_wkv': _L1_attn_in['wkv'], 'L1_attn_bkv': _L1_attn_in['bkv'], 'L1_attn_wkr': _L1_attn_in['wkr'], 'L1_attn_bkr': _L1_attn_in['bkr'], 'L1_attn_wkc': _L1_attn_in['wkc'], 'L1_attn_bkc': _L1_attn_in['bkc'], 'L1_attn_wv': _L1_attn_in['wv'], 'L1_attn_bv': _L1_attn_in['bv'], 'L1_attn_wo': _L1_attn_in['wo'], 'L1_attn_bo': _L1_attn_in['bo'], 'L1_ffn_gate': _L1_ffn_in['gate'], 'L1_ffn_W1': _L1_ffn_in['W1'], 'L1_ffn_b1': _L1_ffn_in['b1'], 'L1_ffn_W2': _L1_ffn_in['W2'], 'L1_ffn_b2': _L1_ffn_in['b2']}
    _x0 = _d['L0_attn_x']
    _d['L0_attn_x'] = jax.random.normal(jax.random.fold_in(jax.random.key(seed), 1), (16, 256, 128), dtype=_x0.dtype)
    del _x0
    return _d

def reference(L0_attn_x, L0_attn_Wq, L0_attn_Wk, L0_attn_Wv, L0_attn_Wf1, L0_attn_Wf2, L0_attn_Wbeta, L0_attn_Wog1, L0_attn_Wog2, L0_attn_norm_w, L0_attn_Wo, L0_ffn_gate_w, L0_ffn_gate_bias, L0_ffn_We_gate, L0_ffn_We_up, L0_ffn_We_down, L0_ffn_Ws_gate, L0_ffn_Ws_up, L0_ffn_Ws_down, L1_attn_wq, L1_attn_bq, L1_attn_wqc, L1_attn_bqc, L1_attn_wqr, L1_attn_bqr, L1_attn_wkv, L1_attn_bkv, L1_attn_wkr, L1_attn_bkr, L1_attn_wkc, L1_attn_bkc, L1_attn_wv, L1_attn_bv, L1_attn_wo, L1_attn_bo, L1_ffn_gate, L1_ffn_W1, L1_ffn_b1, L1_ffn_W2, L1_ffn_b2):

    def _L0_attn_ref(x, Wq, Wk, Wv, Wf1, Wf2, Wbeta, Wog1, Wog2, norm_w, Wo):
        import jax, jax.numpy as jnp
        import numpy as np
        B, N, D, H = (2, 256, 128, 8)
        HD = D // H
        EPS = 1e-06

        def _interleave(a, b):
            return jnp.stack([a, b], axis=2).reshape(a.shape[0], 2 * a.shape[1], a.shape[2], a.shape[3])

        def _l2norm(x):
            return x / jnp.sqrt(jnp.sum(x * x, axis=-1, keepdims=True) + EPS)

        def _dense_rnn(x, Wq, Wk, Wv, Wf1, Wf2, Wbeta, Wog1, Wog2, norm_w, Wo):
            b, n, d = x.shape
            q = jax.nn.silu(x @ Wq)
            k = jax.nn.silu(x @ Wk)
            v = jax.nn.silu(x @ Wv)
            f = x @ Wf1 @ Wf2
            log_f = jax.nn.log_sigmoid(f)
            beta = jax.nn.sigmoid(x @ Wbeta) * 2.0
            shp = (b, n, H, HD)
            q, k, v, log_f = (t.reshape(shp) for t in (q, k, v, log_f))
            k = _l2norm(k)
            k_ = -beta[..., None] * k
            zero = jnp.zeros(shp, x.dtype)
            gk = _interleave(log_f, zero)
            a = _interleave(k_ * jnp.exp(log_f), k_)
            bb = _interleave(k, k)
            kk = _interleave(zero, k)
            vv = _interleave(zero, v)
            qq = _interleave(zero, q)
            seq = tuple((jnp.moveaxis(t, 1, 0) for t in (gk, a, bb, kk, vv, qq)))
            S0 = jnp.zeros((b, H, HD, HD), x.dtype)

            def step(S, inp):
                g, a_t, b_t, k_t, v_t, q_t = inp
                bS = jnp.einsum('bhk,bhkv->bhv', b_t, S)
                S = jnp.exp(g)[..., None] * S + a_t[..., None] * bS[:, :, None, :] + k_t[..., None] * v_t[:, :, None, :]
                o = jnp.einsum('bhk,bhkv->bhv', q_t, S)
                return (S, o)
            _, o = jax.lax.scan(step, S0, seq)
            o = jnp.moveaxis(o, 0, 1)[:, 1::2]
            out = o.reshape(b, n, d)
            gate = x @ Wog1 @ Wog2
            y = out * jax.nn.sigmoid(gate)
            yh = y.reshape(b, n, H, HD)
            yh = yh / jnp.sqrt(jnp.mean(yh * yh, axis=-1, keepdims=True) + EPS)
            y = yh.reshape(b, n, d) * norm_w
            return y @ Wo
        return _dense_rnn(x, Wq, Wk, Wv, Wf1, Wf2, Wbeta, Wog1, Wog2, norm_w, Wo)

    def _L0_ffn_ref(hidden_states, gate_w, gate_bias, We_gate, We_up, We_down, Ws_gate, Ws_up, Ws_down):
        import jax, jax.numpy as jnp
        import numpy as np
        B, S, H = (2, 256, 128)
        E, F, K = (64, 64, 8)
        G, TG = (8, 4)
        SCALE = 2.5
        F_SH = 64

        def _gate(x, gate_w, gate_bias):
            scores = jax.nn.sigmoid(x @ gate_w.T)
            sc = scores + gate_bias[None, :]
            T = x.shape[0]
            group_scores = jax.lax.top_k(sc.reshape(T, G, E // G), 2)[0].sum(-1)
            _, gidx = jax.lax.top_k(group_scores, TG)
            gmask = jnp.zeros((T, G), sc.dtype).at[jnp.arange(T)[:, None], gidx].set(1.0)
            smask = jnp.repeat(gmask, E // G, axis=1)
            masked = jnp.where(smask > 0, sc, -jnp.inf)
            _, tidx = jax.lax.top_k(masked, K)
            tw = jnp.take_along_axis(scores, tidx, axis=1)
            tw = tw / (tw.sum(-1, keepdims=True) + 1e-20)
            return (tidx, tw * SCALE)
        b, s, h = hidden_states.shape
        x = hidden_states.reshape(-1, h).astype(jnp.float32)
        tidx, tw = _gate(x, gate_w, gate_bias)
        T = x.shape[0]
        w_dense = jnp.zeros((T, E), tw.dtype).at[jnp.arange(T)[:, None], tidx].add(tw)

        def body(acc, ws):
            wg, wu, wdn, cw = ws
            hmid = jax.nn.silu(x @ wg) * (x @ wu)
            return (acc + cw[:, None] * (hmid @ wdn), None)
        y, _ = jax.lax.scan(body, jnp.zeros_like(x), (We_gate, We_up, We_down, w_dense.T))
        y = y.reshape(b, s, h)
        shared = jax.nn.silu(hidden_states @ Ws_gate) * (hidden_states @ Ws_up) @ Ws_down
        return y + shared

    def _L1_attn_ref(x, wq, bq, wqc, bqc, wqr, bqr, wkv, bkv, wkr, bkr, wkc, bkc, wv, bv, wo, bo):
        import jax, jax.numpy as jnp
        import numpy as np
        import math
        B, S, E = (2, 256, 128)
        H, DC, DR = (16, 32, 128)
        HD = E // H

        def _linear_params(key, din, dout):
            k1, k2 = jax.random.split(key)
            bound = 1.0 / math.sqrt(din)
            w = jax.random.uniform(k1, (din, dout), minval=-bound, maxval=bound, dtype=jnp.float32)
            b = jax.random.uniform(k2, (dout,), minval=-bound, maxval=bound, dtype=jnp.float32)
            return (w, b)

        def _gelu(x):
            return jax.nn.gelu(x, approximate=False)

        def _rope_cos_sin(seq_len, d_rope):
            inv_freq = 1.0 / 10000.0 ** (jnp.arange(0, d_rope, 2, dtype=jnp.float32) / d_rope)
            t = jnp.arange(seq_len, dtype=jnp.float32)
            freqs = t[:, None] * inv_freq[None, :]
            emb = jnp.concatenate([freqs, freqs], axis=-1)
            return (jnp.cos(emb), jnp.sin(emb))

        def _apply_rope(x, cos, sin):
            d = x.shape[-1]
            x1, x2 = (x[..., :d // 2], x[..., d // 2:])
            rot = jnp.concatenate([-x2, x1], axis=-1)
            return x * cos + rot * sin
        b, s, _ = x.shape
        cq = _gelu(x @ wq + bq)
        q_c = cq @ wqc + bqc
        q_r = x @ wqr + bqr
        ckv = _gelu(x @ wkv + bkv)
        k_r = x @ wkr + bkr
        k_c = ckv @ wkc + bkc
        v = (ckv @ wv + bv).reshape(b, s, H, HD).transpose(0, 2, 1, 3)
        cos, sin = _rope_cos_sin(s, DR)
        q_r = _apply_rope(q_r, cos, sin)
        k_r = _apply_rope(k_r, cos, sin)
        q = _gelu(jnp.concatenate([q_c, q_r], axis=-1)).reshape(b, s, H, HD).transpose(0, 2, 1, 3)
        k = _gelu(jnp.concatenate([k_c, k_r], axis=-1)).reshape(b, s, H, HD).transpose(0, 2, 1, 3)
        scale = 1.0 / math.sqrt(HD)
        scores = jnp.einsum('bhqd,bhkd->bhqk', q, k) * scale
        causal = jnp.triu(jnp.ones((s, s), dtype=bool), k=1)
        scores = jnp.where(causal[None, None], -jnp.inf, scores)
        attn = jax.nn.softmax(scores, axis=-1)
        out = jnp.einsum('bhqk,bhkd->bhqd', attn, v)
        out = out.transpose(0, 2, 1, 3).reshape(b, s, E)
        return out @ wo + bo

    def _L1_ffn_ref(x, gate, W1, b1, W2, b2):
        import jax, jax.numpy as jnp
        import numpy as np
        N_EXPERTS = 16
        TOP_K = int(N_EXPERTS * 0.2)
        EPS = 1e-12
        raw_gate = jax.nn.softmax(jnp.einsum('btd,de->bte', x, gate), axis=-1)
        _, topk_idx = jax.lax.top_k(raw_gate, TOP_K)
        mask = jax.nn.one_hot(topk_idx, raw_gate.shape[-1], dtype=raw_gate.dtype).sum(axis=2)
        gate_topk = mask * raw_gate
        gate_topk = gate_topk / jnp.maximum(jnp.sum(jnp.abs(gate_topk), axis=-1, keepdims=True), EPS)
        hidden = jax.nn.relu(jnp.einsum('btd,edh->bteh', x, W1) + b1)
        expert_out = jnp.einsum('bteh,ehd->bted', hidden, W2) + b2
        return jnp.einsum('bte,bted->btd', gate_topk, expert_out)
    x = L0_attn_x
    xn = _layernorm(x, axis=-1)
    s = _L0_attn_ref(xn, L0_attn_Wq, L0_attn_Wk, L0_attn_Wv, L0_attn_Wf1, L0_attn_Wf2, L0_attn_Wbeta, L0_attn_Wog1, L0_attn_Wog2, L0_attn_norm_w, L0_attn_Wo)
    g = _silu(_L0_ffn_ref(xn, L0_ffn_gate_w, L0_ffn_gate_bias, L0_ffn_We_gate, L0_ffn_We_up, L0_ffn_We_down, L0_ffn_Ws_gate, L0_ffn_Ws_up, L0_ffn_Ws_down))
    x = x + s * g
    xn = _layernorm(x, axis=-1)
    s = _L1_attn_ref(xn, L1_attn_wq, L1_attn_bq, L1_attn_wqc, L1_attn_bqc, L1_attn_wqr, L1_attn_bqr, L1_attn_wkv, L1_attn_bkv, L1_attn_wkr, L1_attn_bkr, L1_attn_wkc, L1_attn_bkc, L1_attn_wv, L1_attn_bv, L1_attn_wo, L1_attn_bo)
    g = _silu(_L1_ffn_ref(xn, L1_ffn_gate, L1_ffn_W1, L1_ffn_b1, L1_ffn_W2, L1_ffn_b2))
    x = x + s * g
    return x

_drawn_inputs = setup_inputs


def setup_inputs(seed=0):
    import zlib

    import numpy as np

    out = dict(_drawn_inputs(seed))
    spreads = {'L0_attn_norm_w': (1.0, 0.6)}
    factors = {'L0_attn_Wf1': 8.0,
     'L0_attn_Wf2': 8.0,
     'L0_attn_Wbeta': 8.0,
     'L0_attn_Wog1': 8.0,
     'L0_attn_Wog2': 8.0,
     'L0_ffn_gate_bias': 3.32,
     'L1_attn_wqr': 8.0,
     'L1_attn_bqr': 8.0,
     'L1_attn_wkv': 8.0,
     'L1_attn_bkv': 8.0,
     'L1_attn_wkr': 8.0,
     'L1_attn_bkr': 8.0,
     'L1_attn_wv': 3.653,
     'L1_attn_bo': 3.173,
     'L1_ffn_b1': 8.0,
     'L1_ffn_b2': 8.0,
     'L1_attn_bv': 3.69}
    for name, (base, spread) in spreads.items():
        noise = np.random.default_rng([zlib.crc32(name.encode()), seed]).standard_normal(out[name].shape)
        drawn = base * np.exp(spread * noise) if base else spread * noise
        out[name] = jnp.asarray(drawn.astype(out[name].dtype))
    for name, factor in factors.items():
        out[name] = (out[name] * factor).astype(out[name].dtype)
    return out
```

```python
from contextlib import ExitStack

import numpy as np

import concourse.bass as bass
from concourse import mybir

F32 = mybir.dt.float32
F32R = mybir.dt.float32r
ALU = mybir.AluOpType
ACT = mybir.ActivationFunctionType
AX = mybir.AxisListType

P = 128
B, N, D = 16, 256, 128
TP = 32
NT = N // TP
TOK = B * TP
NS = TOK // P
BS = P // TP
LN_EPS = 1e-5

H0, HD0 = 8, 16
ZC = 5 * HD0 + 1
ZW = H0 * ZC
ZQ, ZK, ZV, ZF, ZG, ZB = 0, 16, 32, 48, 64, 80
RNN_EPS = 1e-6
E0, F0, K0, G0, TG0 = 64, 64, 8, 8, 4
EG0 = E0 // G0
PAIRS = E0 // 2
ROUTE_SCALE = 2.5
NEG = -1e30
SLOTS = 3 * PAIRS + 2
STEPS = 13

H1, HD1, DC1 = 16, 8, 32
E1, F1, K1 = 16, 256, 3


class Count:

    def __init__(self, tile, per_tile):
        self.base, self.per_tile, self.n = tile * per_tile, per_tile, 0

    def next(self, k=1):
        self.n += k
        return self.base + self.n

    def check(self):
        assert self.n == self.per_tile, (self.n, self.per_tile)


def layer0(nc, d, scratch, sem):
    z_dram, y_dram, g_dram = scratch
    with ExitStack() as ctx:
        def sb(name, shape, dt=F32):
            return ctx.enter_context(nc.sbuf_tensor(name, shape, dt))

        ident = sb("ident", [P, P])
        onehot = sb("onehot", [P, E0])
        tri = sb("tri", [P, G0 * G0])
        bias64 = sb("bias64", [P, E0])
        eps = sb("eps", [P, 2])
        carrier = sb("carrier", [P, 1])
        wf1 = sb("wf1", [P, 2, HD0])
        wf1T = sb("wf1T", [HD0, 2, P])
        wf2 = sb("wf2", [HD0, 2, D])
        wbeta = sb("wbeta", [P, H0])
        gate_w = sb("gate_w", [E0, D])
        wp = sb("wp", [P, H0, ZC])
        wp_hi, wp_lo = sb("wp_hi", [P, ZW], F32R), sb("wp_lo", [P, ZW], F32R)
        wr_hi, wr_lo = sb("wr_hi", [P, E0], F32R), sb("wr_lo", [P, E0], F32R)
        wg_hi, wg_lo = sb("wg_hi", [P, (E0 + 1) * F0], F32R), sb("wg_lo", [P, (E0 + 1) * F0], F32R)
        wu_hi, wu_lo = sb("wu_hi", [P, (E0 + 1) * F0], F32R), sb("wu_lo", [P, (E0 + 1) * F0], F32R)
        wd = sb("wd", [P, PAIRS + 1, D])
        sel = sb("sel", [P, E0, F0], F32R)
        x_sb = sb("x_sb", [P, NT * NS, D])
        xc = sb("xc", [P, NS, D])
        xn = sb("xn", [P, NS, D])
        stat = sb("stat", [P, 5, NS])
        xt_hi, xt_lo = sb("xt_hi", [P, TOK], F32R), sb("xt_lo", [P, TOK], F32R)
        zs = sb("zs", [P, NS, ZW])
        scores = sb("scores", [P, NS, E0])
        biased = sb("biased", [P, NS, E0])
        top_of_group = sb("top_of_group", [P, NS * G0, 8])
        group_score = sb("group_score", [P, NS, G0])
        cmp_gt = sb("cmp_gt", [P, NS, G0, G0])
        cmp_eq = sb("cmp_eq", [P, NS, G0, G0])
        penalty = sb("penalty", [P, NS, G0])
        masked = sb("masked", [P, NS, E0])
        top8 = sb("top8", [P, NS, 8])
        replaced = sb("replaced", [P, NS, E0])
        cw = sb("cw", [P, NS, E0])
        cw_sum = sb("cw_sum", [P, NS])
        cws = sb("cws", [P, NS, 2 * E0], F32R)
        cwt = sb("cwt", [P, TOK], F32R)
        RING = 3
        act_g = sb("act_g", [P, RING, TOK])
        act_u = sb("act_u", [P, RING, TOK])
        act_c = sb("act_c", [P, RING, TOK])
        hid1 = sb("hid1", [P, TOK])
        hid = sb("hid", [P, 2, TOK])
        yt = act_g[:, 0, :]
        g_out = act_u[:, 0, :].rearrange("p (s c) -> p s c", s=NS)
        zr = sb("zr", [P, TP, ZC])
        am = sb("am", [P, TP, HD0])
        prod = sb("prod", [P, TP, HD0])
        coef = sb("coef", [P, 6, TP])
        wh = sb("wh", [P, TP, 4, HD0])
        x1 = sb("x1", [P, HD0, HD0])
        x2 = sb("x2", [P, HD0, HD0])
        yo = sb("yo", [P, TP, HD0])
        ra = ctx.enter_context(nc.psum_tensor("ra", [P, 4, HD0, HD0], F32))
        rs = ctx.enter_context(nc.psum_tensor("rs", [P, 2, HD0, HD0], F32))
        pb = ctx.enter_context(nc.psum_tensor("pb", [P, 5, 512], F32))
        pbf = pb[:, :, :].rearrange("p a b -> p (a b)")

        s_x = sem("x_loaded")
        s_small = sem("small_weights_loaded")
        s_stage = [sem(f"stage_loaded{i}") for i in range(3)]
        s_wd = sem("down_weights_loaded")
        s_eps = sem("eps_set")
        s_sel = sem("selectors_ready")
        s_w1t_ps = sem("transposed_small_in_psum")
        s_w1t = sem("transposed_small_copied")
        s_w12_ps = sem("products_in_psum")
        s_w12 = sem("products_copied")
        s_wp = sem("projection_weights_split")
        s_split = sem("expert_weights_split")
        s_hi_tmp = sem("expert_weight_hi_written")
        s_xc = sem("centred")
        s_sq = sem("squared")
        s_var = sem("variance_summed")
        s_std = sem("std_ready")
        s_xn = sem("normalised")
        s_ln = sem("ln_chain")
        s_xt_ps = sem("xT_in_psum")
        s_xth = sem("xT_hi_ready")
        s_xtl = sem("xT_lo_ready")
        s_zp = sem("z_in_psum")
        s_zc = sem("z_copied")
        s_zst = sem("z_stored")
        s_zld = sem("z_loaded")
        s_lg = sem("router_logits_in_psum")
        s_sc = sem("router_scores_ready")
        s_rt = sem("router_chain")
        s_cws = sem("router_weights_split")
        s_cwt_ps = sem("router_weightsT_in_psum")
        s_cwt = sem("router_weightsT_ready")
        s_slot = sem("moe_slot_filled")
        s_ev = sem("moe_slot_copied")
        s_h1 = sem("moe_product_ready")
        s_h = sem("moe_hidden_ready")
        s_dn = sem("moe_hidden_used")
        s_s0 = sem("state_zeroed")
        s_y_ps = sem("moe_out_in_psum")
        s_y = sem("moe_out_copied")
        s_g_ps = sem("moe_outT_in_psum")
        s_g = sem("gate_ready")
        s_gst = sem("gate_stored")
        s_sig = sem("z_sigmoid_done")
        s_silu = sem("z_silu_done")
        s_kk = sem("k_squares_summed")
        s_kn = sem("k_norm_ready")
        s_pr = sem("prep_chain")
        s_st = sem("recurrence_step")
        s_po = sem("post_chain")
        s_yy = sem("y_squares_summed")
        s_yn = sem("y_norm_ready")
        s_yo = sem("y_ready")
        s_yst = sem("y_stored")

        LN, PREP, POST, ROUTE = 3, 13, 7, 57
        SMALL = 13

        stages = [r[:, 0:2, :].rearrange("p a b -> p (a b)") for r in (act_g, act_u, act_c)]
        CH = 16
        chunks = [(w, c) for c in range(E0 // CH) for w in (0, 1)] + [(2, 0)]

        block = ctx.enter_context(nc.Block())

        @block.sync
        def _(sp):
            xr = d["L0_attn_x"].rearrange("(s b) (t n) d -> t b n s d", b=BS, n=TP)

            def load_x(t):
                for b in range(BS):
                    src = xr[bass.ds(t, 1), b].rearrange("o n s d -> (o n) s d")
                    sp.dma_start(x_sb[TP * b:TP * (b + 1), bass.ds(t * NS, NS), :], src).then_inc(s_x, 16)

            load_x(0)
            sp.dma_start(ident[:, :], d["c_ident"]).then_inc(s_small, 16)
            sp.dma_start(onehot[:, :], d["c_onehot"]).then_inc(s_small, 16)
            sp.dma_start(tri[:, :], d["c_tri"].rearrange("(o c) -> o c", o=1).to_broadcast([P, G0 * G0])).then_inc(s_small, 16)
            sp.dma_start(bias64[:, :], d["L0_ffn_gate_bias"].rearrange("(o c) -> o c", o=1).to_broadcast([P, E0])).then_inc(s_small, 16)
            sp.dma_start(wf1[:, 0, :], d["L0_attn_Wf1"]).then_inc(s_small, 16)
            sp.dma_start(wf1[:, 1, :], d["L0_attn_Wog1"]).then_inc(s_small, 16)
            sp.dma_start(wf2[:, 0, :], d["L0_attn_Wf2"]).then_inc(s_small, 16)
            sp.dma_start(wf2[:, 1, :], d["L0_attn_Wog2"]).then_inc(s_small, 16)
            sp.dma_start(gate_w[:, :], d["L0_ffn_gate_w"]).then_inc(s_small, 16)
            for at, name in ((ZQ, "L0_attn_Wq"), (ZK, "L0_attn_Wk"), (ZV, "L0_attn_Wv")):
                sp.dma_start(wp[:, :, at:at + HD0], d[name].rearrange("i (h c) -> i h c", h=H0)).then_inc(s_small, 16)
            sp.dma_start(wbeta[:, :], d["L0_attn_Wbeta"]).then_inc(s_small, 16)
            names = ("L0_ffn_We_gate", "L0_ffn_We_up")
            for k, (w, c) in enumerate(chunks):
                if k >= 3:
                    sp.wait_ge(s_split, k - 2)
                dst = stages[k % 3]
                if w < 2:
                    src = d[names[w]][c * CH:(c + 1) * CH].rearrange("e i f -> i e f")
                    sp.dma_start(dst[:, 0:CH * F0].rearrange("p (e f) -> p e f", e=CH), src).then_inc(s_stage[k % 3], 16)
                else:
                    sp.dma_start(dst[:, 0:F0], d["L0_ffn_Ws_gate"]).then_inc(s_stage[k % 3], 16)
                    sp.dma_start(dst[:, F0:2 * F0], d["L0_ffn_Ws_up"]).then_inc(s_stage[k % 3], 16)
            sp.dma_start(wd[:, 0:PAIRS, :], d["L0_ffn_We_down"].rearrange("(p a) f n -> (a f) p n", a=2)).then_inc(s_wd, 16)
            sp.dma_start(wd[0:F0, PAIRS, :], d["L0_ffn_Ws_down"]).then_inc(s_wd, 16)

            def tile(t, last):
                for s in range(NS):
                    sp.wait_ge(s_zc, t * NS + (s + 1))
                    for b in range(BS):
                        sp.dma_start(z_dram[bass.ds(t, 1), s, b].rearrange("o h n c -> (o n) h c"),
                                     zs[TP * b:TP * (b + 1), s, :].rearrange("p (h c) -> p h c", h=H0)).then_inc(s_zst, 16)
                sp.wait_ge(s_zst, (t + 1) * (16 * NS * BS))
                sp.wait_ge(s_yo, t)
                sp.dma_start(zr[:, :, :], z_dram[bass.ds(t, 1)].rearrange("o s b h n c -> (o s b h) n c")).then_inc(s_zld, 16)
                if not last:
                    load_x(t + 1)
                sp.wait_ge(s_g, t + 1)
                sp.dma_start(g_dram[bass.ds(t, 1)].rearrange("o s p c -> (o p) s c"), g_out).then_inc(s_gst, 16)
                sp.wait_ge(s_yo, t + 1)
                sp.dma_start(y_dram[bass.ds(t, 1)].rearrange("o q n c -> (o q) n c"), yo[:, :, :]).then_inc(s_yst, 16)

            with sp.Fori(0, NT - 1) as t:
                tile(t, False)
            tile(NT - 1, True)
            sp.wait_ge(s_yst, NT * 16)
            sp.wait_ge(s_gst, NT * 16)

        @block.gpsimd
        def _(pool):
            pool.memset(eps[:, 0:1], LN_EPS).then_inc(s_eps, 1)
            pool.memset(eps[:, 1:2], RNN_EPS).then_inc(s_eps, 1)
            for k, (w, c) in enumerate(chunks):
                pool.wait_ge(s_stage[k % 3], 16 * (k // 3 + 1) if w < 2 else 16 * (k // 3 + 2))
                parts = ([((wg_hi, wg_lo), (wu_hi, wu_lo))[w] + (c * CH * F0, CH * F0, 0)] if w < 2 else
                         [(wg_hi, wg_lo, E0 * F0, F0, 0), (wu_hi, wu_lo, E0 * F0, F0, F0)])
                for m, (hi, lo, at, n, off) in enumerate(parts):
                    src = stages[k % 3][:, off:off + n]
                    pool.tensor_scalar(hi[:, at:at + n], src, 1.0, 1.0, ALU.mult, ALU.mult).then_inc(s_hi_tmp, 1)
                    pool.wait_ge(s_hi_tmp, k + 1 + m)
                    pool.tensor_tensor(lo[:, at:at + n], src, hi[:, at:at + n].bitcast(F32), ALU.subtract).then_inc(s_split, 1)

            with pool.Fori(0, NT) as t:
                for p in range(PAIRS + 1):
                    pool.wait_ge(s_ev, t * SLOTS + min(3 * p + 3, SLOTS))
                    g, u, c = act_g[:, p % RING, :], act_u[:, p % RING, :], act_c[:, p % RING, :]
                    if p < PAIRS:
                        if p > 0:
                            pool.wait_ge(s_h, t * (PAIRS + 1) + p)
                        pool.tensor_tensor(hid1[:, :], g, u, ALU.mult).then_inc(s_h1, 1)
                        pool.wait_ge(s_h1, t * PAIRS + (p + 1))
                        if p >= 2:
                            pool.wait_ge(s_dn, t * (PAIRS + 1) + (p - 1))
                        pool.tensor_tensor(hid[:, p % 2, :], hid1[:, :], c, ALU.mult).then_inc(s_h, 1)
                    else:
                        pool.wait_ge(s_dn, t * (PAIRS + 1) + (p - 1))
                        pool.tensor_tensor(hid[0:F0, p % 2, :], g[0:F0], u[0:F0], ALU.mult).then_inc(s_h, 1)

        @block.scalar
        def _(act):
            act.wait_ge(s_eps, 2)
            act.wait_ge(s_small, SMALL * 16)
            act.activation(wp[:, :, ZB], wbeta[:, :], ACT.Copy).then_inc(s_w12, 1)
            act.wait_ge(s_w1t_ps, 1)
            act.activation(wf1T[:, :, :], pb[0:HD0, 0, 0:2 * P].rearrange("p (a b) -> p a b", a=2), ACT.Copy).then_inc(s_w1t, 1)
            act.wait_ge(s_w12_ps, 1)
            for a, at in ((0, ZF), (1, ZG)):
                act.activation(wp[:, :, at:at + HD0], pb[:, 2, D * a:D * (a + 1)].rearrange("p (h c) -> p h c", h=H0),
                               ACT.Copy).then_inc(s_w12, 1)

            with act.Fori(0, NT) as t:
                act.wait_ge(s_xc, t + 1)
                act.activation(xn[:, :, :], xc[:, :, :], ACT.Square).then_inc(s_sq, 1)
                act.wait_ge(s_var, t + 1)
                act.activation(stat[:, 3, :], stat[:, 2, :], ACT.Sqrt, bias=eps[:, 0:1], scale=1.0 / D).then_inc(s_std, 1)
                act.wait_ge(s_xt_ps, t + 1)
                act.activation(xt_hi[:, :], pb[:, 0, :], ACT.Copy).then_inc(s_xth, 1)
                act.wait_ge(s_zst, t * (16 * NS * BS))
                for s in range(NS):
                    act.wait_ge(s_zp, t * NS + (s + 1))
                    at = 512 * (1 + 2 * (s % 2))
                    act.activation(zs[:, s, :], pbf[:, at:at + ZW], ACT.Copy).then_inc(s_zc, 1)
                act.wait_ge(s_lg, t + 1)
                act.activation(scores[:, :, :], pb[:, 0, 0:NS * E0].rearrange("p (s e) -> p s e", s=NS),
                               ACT.Sigmoid).then_inc(s_sc, 1)
                act.wait_ge(s_zld, t * 16 + 16)
                act.activation(zr[:, :, ZF:ZC], zr[:, :, ZF:ZC], ACT.Sigmoid).then_inc(s_sig, 1)
                act.activation(zr[:, :, ZQ:ZF], zr[:, :, ZQ:ZF], ACT.Silu).then_inc(s_silu, 1)
                act.wait_ge(s_kk, t + 1)
                act.activation(coef[:, 0, :], coef[:, 0, :], ACT.Sqrt, bias=eps[:, 1:2]).then_inc(s_kn, 1)
                act.wait_ge(s_cwt_ps, t + 1)
                act.activation(cwt[:, :], pb[:, 1, :], ACT.Copy).then_inc(s_cwt, 1)
                act.wait_ge(s_gst, t * 16)
                act.wait_ge(s_split, len(chunks) + 1)
                for r in range(SLOTS):
                    p, what = r // 3, r % 3
                    n = P if p < PAIRS else F0
                    act.wait_ge(s_slot, t * SLOTS + (r + 1))
                    if what == 0 and p >= RING:
                        act.wait_ge(s_h, t * (PAIRS + 1) + (p - RING + 1))
                    dst = (act_g, act_u, act_c)[what][0:n, p % RING, :]
                    act.activation(dst, pb[0:n, r % 4, :], ACT.Silu if what == 0 else ACT.Copy).then_inc(s_ev, 1)
                act.wait_ge(s_dn, (t + 1) * (PAIRS + 1))
                act.activation(yt, pb[:, 4, :], ACT.Copy).then_inc(s_y, 1)
                act.wait_ge(s_g_ps, t + 1)
                act.activation(g_out, pb[:, 0, :].rearrange("p (s c) -> p s c", s=NS), ACT.Silu).then_inc(s_g, 1)
                act.wait_ge(s_yy, t + 1)
                act.activation(coef[:, 5, :], coef[:, 5, :], ACT.Sqrt, bias=eps[:, 1:2], scale=1.0 / HD0).then_inc(s_yn, 1)

        @block.tensor
        def _(pe):
            def split3(out, l_hi, l_lo, r_hi, r_lo, first=True):
                pe.matmul(out, l_hi, r_hi, start=first, stop=False, skip_group_check=True)
                pe.matmul(out, l_hi, r_lo, start=False, stop=False, skip_group_check=True)
                return pe.matmul(out, l_lo, r_hi, start=False, stop=True, skip_group_check=True)

            pe.wait_ge(s_small, SMALL * 16)
            for a in range(2):
                pe.transpose(pb[0:HD0, 0, P * a:P * (a + 1)], wf1[:, a, :], ident[:, :])
            last = pe.transpose(pb[:, 1, 0:E0], gate_w[:, :], ident[0:E0, 0:E0])
            last.then_inc(s_w1t_ps, 1)
            pe.wait_ge(s_w1t, 1)
            for a in range(2):
                last = pe.matmul(pb[:, 2, D * a:D * (a + 1)], wf1T[:, a, :], wf2[:, a, :], start=(a == 0), stop=(a == 1), skip_group_check=True)
            last.then_inc(s_w12_ps, 1)
            pe.wait_ge(s_wp, 4)

            with pe.Fori(0, NT) as t:
                pe.wait_ge(s_xn, t + 1)
                pe.wait_ge(s_g, t)
                for s in range(NS):
                    last = pe.transpose(pb[:, 0, P * s:P * (s + 1)], xn[:, s, :], ident[:, :])
                last.then_inc(s_xt_ps, 1)
                pe.wait_ge(s_xtl, t + 1)
                for s in range(NS):
                    if s >= 2:
                        pe.wait_ge(s_zc, t * NS + (s - 1))
                    xs = slice(P * s, P * (s + 1))
                    at = 512 * (1 + 2 * (s % 2))
                    for lo, hi in ((0, 512), (512, ZW)):
                        last = split3(pbf[:, at + lo:at + hi], xt_hi[:, xs], xt_lo[:, xs], wp_hi[:, lo:hi], wp_lo[:, lo:hi])
                    last.then_inc(s_zp, 1)
                for s in range(NS):
                    xs = slice(P * s, P * (s + 1))
                    last = split3(pb[:, 0, E0 * s:E0 * (s + 1)], xt_hi[:, xs], xt_lo[:, xs], wr_hi[:, :], wr_lo[:, :], first=(s == 0))
                last.then_inc(s_lg, 1)
                pe.wait_ge(s_cws, t + 1)
                pe.wait_ge(s_zc, t * NS + NS)
                for s in range(NS):
                    last = pe.transpose(pb[:, 1, P * s:P * (s + 1)], cws[:, s, :].bitcast(F32), ident[:, :])
                last.then_inc(s_cwt_ps, 1)
                pe.wait_ge(s_cwt, t + 1)
                pe.wait_ge(s_sel, 1)
                pe.wait_ge(s_wd, 32)

                def down(p):
                    n = P if p < PAIRS else F0
                    pe.wait_ge(s_h, t * (PAIRS + 1) + (p + 1))
                    last = pe.matmul(pb[:, 4, :], wd[0:n, p, :], hid[0:n, p % 2, :], start=(p == 0), stop=(p == PAIRS), skip_group_check=True)
                    last.then_inc(s_dn, 1)
                    return last

                def slot_free(r):
                    if r >= 4:
                        pe.wait_ge(s_ev, t * SLOTS + (r - 3))

                LAG = 2
                for p in range(PAIRS + 1):
                    pe.wait_ge(s_split, 2 * (2 * p // CH + 1))
                    for what, (w_hi, w_lo) in enumerate(((wg_hi, wg_lo), (wu_hi, wu_lo))):
                        r = 3 * p + what
                        slot_free(r)
                        if p < PAIRS:
                            at = slice(2 * F0 * p, 2 * F0 * (p + 1))
                            last = split3(pb[:, r % 4, :], w_hi[:, at], w_lo[:, at], xt_hi[:, :], xt_lo[:, :])
                        else:
                            at = slice(E0 * F0, (E0 + 1) * F0)
                            last = split3(pb[0:F0, r % 4, :], w_hi[:, at], w_lo[:, at], xt_hi[:, :], xt_lo[:, :])
                        last.then_inc(s_slot, 1)
                    if p < PAIRS:
                        r = 3 * p + 2
                        slot_free(r)
                        pe.matmul(pb[:, r % 4, :], sel[:, 2 * p:2 * p + 2, :].rearrange("p a b -> p (a b)"), cwt[:, :], start=True, stop=True).then_inc(s_slot, 1)
                    if p >= LAG:
                        down(p - LAG)
                for p in range(PAIRS + 1 - LAG, PAIRS + 1):
                    last = down(p)
                pe.wait_ge(s_y, t + 1)
                for s in range(NS):
                    last = pe.transpose(pb[:, 0, P * s:P * (s + 1)], yt[:, P * s:P * (s + 1)], ident[:, :])
                last.then_inc(s_g_ps, 1)

        @block.vector
        def _(dve):
            def over(ap, n):
                return ap.unsqueeze(len(ap.shape)).to_broadcast([*ap.shape, n])

            dve.memset(rs[:, :, :, :], 0.0).then_inc(s_s0, 1)
            dve.wait_ge(s_small, SMALL * 16)
            dve.tensor_copy(sel[:, :, :], over(onehot[:, :], F0)).then_inc(s_sel, 1)
            dve.wait_ge(s_w12, 3)
            wpf = wp[:, :, :].rearrange("p h c -> p (h c)")
            dve.tensor_copy(wp_hi[:, :], wpf).then_inc(s_wp, 1)
            dve.tensor_copy(wr_hi[:, :], pb[:, 1, 0:E0]).then_inc(s_wp, 1)
            dve.wait_ge(s_wp, 2)
            dve.tensor_tensor(wp_lo[:, :], wpf, wp_hi[:, :].bitcast(F32), ALU.subtract).then_inc(s_wp, 1)
            dve.tensor_tensor(wr_lo[:, :], pb[:, 1, 0:E0], wr_hi[:, :].bitcast(F32), ALU.subtract).then_inc(s_wp, 1)
            dve.wait_ge(s_s0, 1)

            def layer_norm(t):
                dve.wait_ge(s_x, (t + 1) * (16 * BS))
                xin = x_sb[:, bass.ds(t * NS, NS), :]
                c = Count(t, LN)
                dve.tensor_reduce(stat[:, 0, :], xin, AX.X, ALU.add).then_inc(s_ln, 1)
                dve.wait_ge(s_ln, c.next())
                dve.tensor_scalar(stat[:, 1, :], stat[:, 0, :], -1.0 / D, None, ALU.mult).then_inc(s_ln, 1)
                dve.wait_ge(s_ln, c.next())
                dve.tensor_tensor(xc[:, :, :], xin, over(stat[:, 1, :], D), ALU.add).then_inc(s_xc, 1)
                dve.wait_ge(s_sq, t + 1)
                dve.tensor_reduce(stat[:, 2, :], xn[:, :, :], AX.X, ALU.add).then_inc(s_var, 1)
                dve.wait_ge(s_std, t + 1)
                dve.reciprocal(stat[:, 4, :], stat[:, 3, :]).then_inc(s_ln, 1)
                dve.wait_ge(s_ln, c.next())
                dve.tensor_tensor(xn[:, :, :], xc[:, :, :], over(stat[:, 4, :], D), ALU.mult).then_inc(s_xn, 1)
                c.check()
                dve.wait_ge(s_xth, t + 1)
                dve.tensor_tensor(xt_lo[:, :], pb[:, 0, :], xt_hi[:, :].bitcast(F32), ALU.subtract).then_inc(s_xtl, 1)

            def route(t):
                c = Count(t, ROUTE)
                dve.wait_ge(s_sc, t + 1)
                dve.tensor_tensor(biased[:, :, :], scores[:, :, :], bias64[:, :].unsqueeze(1).to_broadcast([P, NS, E0]), ALU.add).then_inc(s_rt, 1)
                dve.wait_ge(s_rt, c.next())
                dve.memset(carrier[:, :], 0.0)
                groups = biased[:, :, :].rearrange("p s (g e) -> p (s g) e", g=G0)
                for i in range(NS * G0):
                    dve.max(top_of_group[:, i, :], groups[:, i, :]).then_inc(s_rt, 1)
                dve.wait_ge(s_rt, c.next(NS * G0))
                tog = top_of_group[:, :, :].rearrange("p (s g) e -> p s g e", s=NS)
                dve.tensor_tensor(group_score[:, :, :], tog[:, :, :, 0], tog[:, :, :, 1], ALU.add).then_inc(s_rt, 1)
                dve.wait_ge(s_rt, c.next())
                mine = over(group_score[:, :, :], G0)
                other = group_score[:, :, :].unsqueeze(2).to_broadcast([P, NS, G0, G0])
                dve.tensor_tensor(cmp_gt[:, :, :, :], other, mine, ALU.is_gt).then_inc(s_rt, 1)
                dve.tensor_tensor(cmp_eq[:, :, :, :], other, mine, ALU.is_equal).then_inc(s_rt, 1)
                dve.wait_ge(s_rt, c.next(2))
                eq = cmp_eq[:, :, :, :].rearrange("p s g h -> p s (g h)")
                dve.tensor_tensor(eq, eq, tri[:, :].unsqueeze(1).to_broadcast([P, NS, G0 * G0]), ALU.mult).then_inc(s_rt, 1)
                dve.wait_ge(s_rt, c.next())
                dve.tensor_tensor(cmp_gt[:, :, :, :], cmp_gt[:, :, :, :], cmp_eq[:, :, :, :], ALU.add).then_inc(s_rt, 1)
                dve.wait_ge(s_rt, c.next())
                dve.tensor_reduce(penalty[:, :, :], cmp_gt[:, :, :, :], AX.X, ALU.add).then_inc(s_rt, 1)
                dve.wait_ge(s_rt, c.next())
                dve.tensor_scalar(penalty[:, :, :], penalty[:, :, :], float(TG0), NEG, ALU.is_ge, ALU.mult).then_inc(s_rt, 1)
                dve.wait_ge(s_rt, c.next())
                m4 = masked[:, :, :].rearrange("p s (g e) -> p s g e", g=G0)
                dve.tensor_tensor(m4, biased[:, :, :].rearrange("p s (g e) -> p s g e", g=G0), over(penalty[:, :, :], EG0), ALU.add).then_inc(s_rt, 1)
                dve.wait_ge(s_rt, c.next())
                dve.memset(carrier[:, :], 0.0)
                for s in range(NS):
                    dve.max(top8[:, s, :], masked[:, s, :]).then_inc(s_rt, 1)
                dve.wait_ge(s_rt, c.next(NS))
                dve.memset(carrier[:, :], 0.0)
                for s in range(NS):
                    dve.match_replace(replaced[:, s, :], top8[:, s, :], masked[:, s, :], 2 * NEG).then_inc(s_rt, 1)
                dve.wait_ge(s_rt, c.next(NS))
                dve.tensor_tensor(replaced[:, :, :], replaced[:, :, :], masked[:, :, :], ALU.not_equal).then_inc(s_rt, 1)
                dve.wait_ge(s_rt, c.next())
                dve.tensor_tensor(cw[:, :, :], replaced[:, :, :], scores[:, :, :], ALU.mult).then_inc(s_rt, 1)
                dve.wait_ge(s_rt, c.next())
                dve.tensor_reduce(cw_sum[:, :], cw[:, :, :], AX.X, ALU.add).then_inc(s_rt, 1)
                dve.wait_ge(s_rt, c.next())
                dve.tensor_scalar(cw_sum[:, :], cw_sum[:, :], 1e-20, None, ALU.add).then_inc(s_rt, 1)
                dve.wait_ge(s_rt, c.next())
                dve.reciprocal(cw_sum[:, :], cw_sum[:, :]).then_inc(s_rt, 1)
                dve.wait_ge(s_rt, c.next())
                dve.tensor_scalar(cw_sum[:, :], cw_sum[:, :], ROUTE_SCALE, None, ALU.mult).then_inc(s_rt, 1)
                dve.wait_ge(s_rt, c.next())
                dve.tensor_tensor(cw[:, :, :], cw[:, :, :], over(cw_sum[:, :], E0), ALU.mult).then_inc(s_rt, 1)
                dve.wait_ge(s_rt, c.next())
                dve.tensor_copy(cws[:, :, 0:E0], cw[:, :, :]).then_inc(s_rt, 1)
                dve.wait_ge(s_rt, c.next())
                dve.tensor_tensor(cws[:, :, E0:2 * E0], cw[:, :, :], cws[:, :, 0:E0].bitcast(F32), ALU.subtract).then_inc(s_cws, 1)
                c.check()

            q, k, v, f, g = (zr[:, :, a:a + HD0] for a in (ZQ, ZK, ZV, ZF, ZG))
            knorm, neg_beta, w1_to_r, w1_to_o, r_to_o, ynorm = (coef[:, i, :] for i in range(6))

            def prepare(t):
                c = Count(t, PREP)
                dve.wait_ge(s_silu, t + 1)
                dve.tensor_tensor(prod[:, :, :], k, k, ALU.mult).then_inc(s_pr, 1)
                dve.wait_ge(s_pr, c.next())
                dve.tensor_reduce(knorm, prod[:, :, :], AX.X, ALU.add).then_inc(s_kk, 1)
                dve.wait_ge(s_sig, t + 1)
                dve.tensor_scalar(neg_beta, zr[:, :, ZB], -2.0, None, ALU.mult).then_inc(s_pr, 1)
                dve.wait_ge(s_kn, t + 1)
                dve.reciprocal(knorm, knorm).then_inc(s_pr, 1)
                dve.wait_ge(s_pr, c.next(2))
                dve.tensor_tensor(k, k, over(knorm, HD0), ALU.mult).then_inc(s_pr, 1)
                dve.wait_ge(s_pr, c.next())
                dve.tensor_tensor(prod[:, :, :], f, k, ALU.mult).then_inc(s_pr, 1)
                dve.wait_ge(s_pr, c.next())
                dve.tensor_tensor(am[:, :, :], prod[:, :, :], over(neg_beta, HD0), ALU.mult).then_inc(s_pr, 1)
                dve.wait_ge(s_pr, c.next())
                for out, a, b in ((w1_to_r, am[:, :, :], k), (w1_to_o, am[:, :, :], q), (r_to_o, k, q)):
                    dve.tensor_tensor(prod[:, :, :], a, b, ALU.mult).then_inc(s_pr, 1)
                    dve.wait_ge(s_pr, c.next())
                    dve.tensor_reduce(out, prod[:, :, :], AX.X, ALU.add).then_inc(s_pr, 1)
                    dve.wait_ge(s_pr, c.next())
                dve.tensor_tensor(w1_to_r, w1_to_r, neg_beta, ALU.mult).then_inc(s_pr, 1)
                dve.wait_ge(s_pr, c.next())
                c.check()

            fs, ks, kfs, qfs = (ra[:, j] for j in range(4))
            state, part = rs[:, 0], rs[:, 1]

            def step(t, n):
                at = t * (STEPS * TP) + STEPS * n
                row = lambda ap: ap[:, n:n + 1, :].to_broadcast([P, HD0, HD0])
                w1, w2, w3, r = (wh[:, n, j, :] for j in range(4))
                dve.wait_ge(s_st, at - 1 if n else at)
                dve.tensor_tensor(fs, row(f), state, ALU.mult).then_inc(s_st, 1)
                dve.tensor_tensor(ks, row(k), state, ALU.mult).then_inc(s_st, 1)
                dve.wait_ge(s_st, at + 1)
                dve.tensor_tensor(kfs, row(k), fs, ALU.mult).then_inc(s_st, 1)
                dve.wait_ge(s_st, at + 2)
                dve.tensor_reduce(w1, ks, AX.X, ALU.add).then_inc(s_st, 1)
                dve.wait_ge(s_st, at + 3)
                dve.tensor_reduce(w2, kfs, AX.X, ALU.add).then_inc(s_st, 1)
                dve.wait_ge(s_st, at + 4)
                dve.scalar_tensor_tensor(out=r, in0=w1, scalar=w1_to_r[:, n:n + 1], in1=v[:, n, :],
                                         op0=ALU.mult, op1=ALU.add).then_inc(s_st, 1)
                dve.tensor_tensor(x1[:, :, :], row(am), over(w1, HD0), ALU.mult).then_inc(s_st, 1)
                dve.wait_ge(s_st, at + 6)
                dve.scalar_tensor_tensor(out=r, in0=w2, scalar=neg_beta[:, n:n + 1], in1=r,
                                         op0=ALU.mult, op1=ALU.add).then_inc(s_st, 1)
                dve.wait_ge(s_st, at + 7)
                dve.tensor_tensor(part, fs, x1[:, :, :], ALU.add).then_inc(s_st, 1)
                dve.wait_ge(s_st, at + 8)
                dve.tensor_tensor(x2[:, :, :], row(k), over(r, HD0), ALU.mult).then_inc(s_st, 1)
                dve.tensor_tensor(qfs, row(q), fs, ALU.mult).then_inc(s_st, 1)
                dve.wait_ge(s_st, at + 10)
                dve.tensor_tensor(state, part, x2[:, :, :], ALU.add).then_inc(s_st, 1)
                dve.wait_ge(s_st, at + 11)
                dve.tensor_reduce(w3, qfs, AX.X, ALU.add).then_inc(s_st, 1)

            def finish(t):
                c = Count(t, POST)
                w1, w3, r = (wh[:, :, j, :] for j in (0, 2, 3))
                dve.wait_ge(s_st, (t + 1) * (STEPS * TP))
                dve.tensor_tensor(prod[:, :, :], w1, over(w1_to_o, HD0), ALU.mult).then_inc(s_po, 1)
                dve.wait_ge(s_po, c.next())
                dve.wait_ge(s_yst, t * 16)
                dve.tensor_tensor(yo[:, :, :], prod[:, :, :], w3, ALU.add).then_inc(s_po, 1)
                dve.tensor_tensor(am[:, :, :], r, over(r_to_o, HD0), ALU.mult).then_inc(s_po, 1)
                dve.wait_ge(s_po, c.next(2))
                dve.tensor_tensor(yo[:, :, :], yo[:, :, :], am[:, :, :], ALU.add).then_inc(s_po, 1)
                dve.wait_ge(s_po, c.next())
                dve.tensor_tensor(yo[:, :, :], yo[:, :, :], g, ALU.mult).then_inc(s_po, 1)
                dve.wait_ge(s_po, c.next())
                dve.tensor_tensor(prod[:, :, :], yo[:, :, :], yo[:, :, :], ALU.mult).then_inc(s_po, 1)
                dve.wait_ge(s_po, c.next())
                dve.tensor_reduce(ynorm, prod[:, :, :], AX.X, ALU.add).then_inc(s_yy, 1)
                dve.wait_ge(s_yn, t + 1)
                dve.reciprocal(ynorm, ynorm).then_inc(s_po, 1)
                dve.wait_ge(s_po, c.next())
                dve.tensor_tensor(yo[:, :, :], yo[:, :, :], over(ynorm, HD0), ALU.mult).then_inc(s_yo, 1)
                c.check()

            with dve.Fori(0, NT) as t:
                layer_norm(t)
                route(t)
                prepare(t)
                for n in range(TP):
                    step(t, n)
                finish(t)


def layer1(nc, d, scratch, out_dram, sem):
    y_dram, g_dram, x2_dram, g1_dram = scratch
    with ExitStack() as ctx:
        def sb(name, shape, dt=F32):
            return ctx.enter_context(nc.sbuf_tensor("l1_" + name, shape, dt))

        NB = B + 1
        ident = sb("ident", [P, P])
        ident_r = sb("ident_r", [P, P], F32R)
        mask_r = sb("mask_r", [P, P], F32R)
        rot = sb("rot", [P, P])
        rows = sb("rows", [2 * E1 + 4, P])
        cols = sb("cols", [P, 2 * E1 + 4])
        rcols = sb("rcols", [P, 2])
        eps = sb("eps", [P, 2])
        carrier = sb("carrier", [P, 1])
        wo0 = sb("wo0", [P, D])
        wproj = sb("wproj", [P, 2, D])
        wqk = sb("wqk", [P, 2, 4, D], F32R)
        wqk_hi, wqk_lo = wqk[:, 0], wqk[:, 1]
        wkv = sb("wkv", [P, P])
        wkv_hi, wkv_lo = sb("wkv_hi", [P, P], F32R), sb("wkv_lo", [P, P], F32R)
        gate = sb("gate", [P, E1])
        gate_hi, gate_lo = sb("gate_hi", [P, E1], F32R), sb("gate_lo", [P, E1], F32R)
        b2 = sb("b2", [E1, D])
        wv = sb("wv", [DC1 + 1, D])
        wo = sb("wo", [P, D])
        bo = sb("bo", [1, D])
        ones = sb("ones", [1, P])
        cosT, sinT = sb("cosT", [P, N]), sb("sinT", [P, N])
        big0 = sb("big0", [P, E1 * F1], F32R)
        big1 = sb("big1", [P, E1 * F1], F32R)
        big2 = sb("big2", [P, E1 * F1])
        w1_hi, w1_lo = big0, big1
        w2 = big2[:, :].rearrange("p (e a n) -> p e a n", e=E1, a=2)
        qh, ql = sb("qh", [P, B, N], F32R), sb("ql", [P, B, N], F32R)
        kh, kl = sb("kh", [P, B, N], F32R), sb("kl", [P, B, N], F32R)
        ckvT = sb("ckvT", [P, B, N])
        xs = sb("xs", [P, NS, D])
        ys = sb("ys", [P, NS, D])
        gs = sb("gs", [P, NS, D])
        yT = sb("yT", [P, TOK])
        xc = sb("xc", [P, NS, D])
        xn = sb("xn", [P, NS, D])
        stat = sb("stat", [P, 5, NS])
        xt = sb("xt", [P, 2, TOK], F32R)
        xt_hi, xt_lo = xt[:, 0, :], xt[:, 1, :]
        rope = sb("rope", [P, 3, TOK])
        logits = sb("logits", [P, NS, E1])
        raw = sb("raw", [P, NS, E1])
        top8 = sb("top8", [P, NS, 8])
        replaced = sb("replaced", [P, NS, E1])
        row1 = sb("row1", [P, 2, NS])
        gtok = sb("gtok", [P, NS, E1])
        gT = sb("gT", [E1, TOK])
        HR = 4
        hid = sb("hid", [P, HR, TOK])
        acc = sb("acc", [P, NS, D])
        qb = [b[:, :].rearrange("p (h n) -> p h n", h=H1) for b in (big0, big1)]
        kr = xt[:, :, :].rearrange("p a n -> p (a n)"), wqk[:, :, :, :].rearrange("p a j n -> p (a j n)")
        rep = sb("rep", [P, 4, 4, P], F32R)
        rep_stage = hid[:, :, :].rearrange("p a b -> p (a b)")
        esel = sb("esel", [2 * H1, H1, P], F32R)
        qmask = sb("qmask", [P, 4])
        mrow = sb("mrow", [P, 2, H1])
        mhl = sb("mhl", [P, 2, 2 * H1], F32R)
        mT = [sb(f"mT{i}", [2 * H1, N], F32R) for i in range(2)]
        place = 0

        def carve(pattern, **sizes):
            nonlocal place
            n = int(np.prod(list(sizes.values())))
            place += n
            assert place <= E1 * F1
            return big2[:, place - n:place].rearrange(pattern, **sizes)

        ckv_b = carve("p (o n) -> p o n", o=1, n=N)[:, 0, :]
        vp = [carve("p (k h c) -> p k h c", k=2, h=H1, c=HD1 + 1) for _ in range(2)]
        pt = carve("p (a n) -> p a n", a=2, n=3 * N)
        rec = carve("p (k h) -> p k h", k=2, h=H1)
        o_tok = carve("p (k c) -> p k c", k=2, c=D)
        oT = carve("p (o n) -> p o n", o=1, n=N)[:, 0, :]
        x2b = xs[:, 0:2, :], xs[:, 2:4, :]
        g1b = gs[:, 0:2, :], gs[:, 2:4, :]
        prodb = ys[:, 0:2, :]
        outb = ys[:, 2:4, :]
        pb = ctx.enter_context(nc.psum_tensor("l1_pb", [P, 8, 512], F32))
        pbf = pb[:, :, :].rearrange("p a b -> p (a b)")

        s_w = sem("m_weights_loaded")
        s_w1 = sem("m_w1_loaded")
        s_w1b = sem("m_w1_second_half_loaded")
        s_w2 = sem("m_w2_loaded")
        s_init = sem("m_constants_set")
        s_cols_ps = sem("m_columns_in_psum")
        s_cols = sem("m_columns_ready")
        s_prep = sem("m_weights_split")
        s_w1s = sem("m_w1_split")
        s_x = sem("m_x_loaded")
        s_yld = sem("m_y_loaded")
        s_gld = sem("m_gate_loaded")
        s_yt_ps = sem("m_yT_in_psum")
        s_yt = sem("m_yT_ready")
        s_s_ps = sem("m_mixed_in_psum")
        s_ln = sem("m_ln_chain")
        s_x2 = sem("m_x2_ready")
        s_x2st = sem("m_x2_stored")
        s_xc, s_sq, s_var, s_std, s_xn = (sem("m_" + n) for n in ("centred", "squared", "variance_summed", "std_ready", "normalised"))
        s_xt_ps, s_xth, s_xtl = sem("m_xT_in_psum"), sem("m_xT_hi_ready"), sem("m_xT_lo_ready")
        s_lg = sem("m_logits_in_psum")
        s_rt = sem("m_router_chain")
        s_cen = sem("m_logits_centred")
        s_exp = sem("m_logits_exp")
        s_gt = sem("m_gate_weights_ready")
        s_kv_ps, s_kv = sem("m_kv_in_psum"), sem("m_kv_ready")
        s_qk_ps = sem("m_qk_in_psum")
        s_rope = sem("m_rope_chain")
        s_rope_done = sem("m_rope_ready")
        s_gelu = sem("m_gelu_done")
        s_qkh = sem("m_qk_hi_ready")
        s_qkl = sem("m_qk_lo_ready")
        s_gT_ps, s_gT = sem("m_gate_weightsT_in_psum"), sem("m_gate_weightsT_ready")
        s_b2 = sem("m_gate_bias_in_psum")
        s_acc0 = sem("m_sum_started")
        s_w1o = sem("m_hidden_in_psum")
        s_hid = sem("m_hidden_ready")
        s_w2o = sem("m_expert_out_in_psum")
        s_acc = sem("m_expert_summed")
        s_g1, s_g1st = sem("m_gate1_ready"), sem("m_gate1_stored")
        s_rep_ld = sem("a_selectors_loaded")
        s_rep = sem("a_selectors_ready")
        s_x2l = [sem(f"a_x2_loaded{i}") for i in range(2)]
        s_g1l = [sem(f"a_gate1_loaded{i}") for i in range(2)]
        s_ckb = sem("a_latent_copied")
        s_ua = sem("a_unit_in_psum")
        s_ua_act = sem("a_unit_read_by_act")
        s_ua_dve = sem("a_unit_read_by_dve")
        s_mc = sem("a_max_chain")
        s_mhl = sem("a_max_split")
        s_st = sem("a_scoresT_in_psum")
        s_pt = sem("a_probs_ready")
        s_pv = sem("a_probs_used")
        s_rec = sem("a_sums_inverted")
        s_ot = sem("a_out_ready")
        s_oT_ps, s_oT = sem("a_outT_in_psum"), sem("a_outT_ready")
        s_wo = sem("a_wo_in_psum")
        s_fin = sem("a_final_chain")
        s_done = sem("a_out_final")
        s_ost = sem("a_out_stored")

        NW = 21
        LN, ROPE, ROUTE = 4, 4, NS + 11
        PREP = 18
        UNITS = ["k"] * 2 + ["q_dve", "q_act", "v"] + ["max0"] * 4 + ["max1"] * 8 + ["mT"]
        NU = len(UNITS)
        BY_ACT = [u in ("k", "q_act", "v", "mT") for u in UNITS]
        N_ACT, N_DVE = sum(BY_ACT), NU - sum(BY_ACT)
        XU = H1 // 2

        def read(b, i):
            if BY_ACT[i]:
                return s_ua_act, b * N_ACT + sum(BY_ACT[:i + 1])
            return s_ua_dve, b * N_DVE + (i + 1 - sum(BY_ACT[:i + 1]))

        block = ctx.enter_context(nc.Block())

        @block.sync
        def _(sp):
            def w(dst, src):
                sp.dma_start(dst, src).then_inc(s_w, 16)

            row = lambda name: d[name].rearrange("(o c) -> o c", o=1)
            w(ident[:, :], d["c_ident"])
            w(rot[:, :], d["c_rot"])
            w(qmask[:, :], d["c_qmask"])
            w(rope[:, 1, 0:P], d["c_mask"])
            sp.wait_ge(s_init, 1)
            w(rows[0:2 * E1, :], d["L1_ffn_b1"].rearrange("e (a p) -> (e a) p", a=2))
            w(rows[2 * E1:2 * E1 + 1, :], row("L1_attn_bqr"))
            w(rows[2 * E1 + 1:2 * E1 + 2, :], row("L1_attn_bkr"))
            w(rows[2 * E1 + 2:2 * E1 + 3, :], row("L0_attn_norm_w"))
            w(rows[2 * E1 + 3:2 * E1 + 4, 0:DC1], row("L1_attn_bkv"))
            w(wo0[:, :], d["L0_attn_Wo"])
            w(wproj[:, 0, :], d["L1_attn_wqr"])
            w(wproj[:, 1, :], d["L1_attn_wkr"])
            w(gate[:, :], d["L1_ffn_gate"])
            w(b2[:, :], d["L1_ffn_b2"])
            w(wv[0:DC1, :], d["L1_attn_wv"])
            w(wv[DC1:DC1 + 1, :], row("L1_attn_bv"))
            w(wo[:, :], d["L1_attn_wo"])
            w(bo[:, :], row("L1_attn_bo"))
            w(cosT[:, :], d["c_cosT"])
            w(sinT[:, :], d["c_sinT"])
            sp.wait_ge(s_init, 2)
            w(wkv[:, 0:DC1], d["L1_attn_wkv"])

            xr = d["L0_attn_x"].rearrange("(s b) (t n) d -> t b n s d", b=BS, n=TP)

            def load(t):
                for b in range(BS):
                    sp.dma_start(xs[TP * b:TP * (b + 1), :, :], xr[bass.ds(t, 1), b].rearrange("o n s d -> (o n) s d")).then_inc(s_x, 16)
                for s in range(NS):
                    for b in range(BS):
                        src = y_dram[bass.ds(t, 1), (s * BS + b) * H0:(s * BS + b + 1) * H0]
                        sp.dma_start(ys[TP * b:TP * (b + 1), s, :].rearrange("p (h c) -> p h c", h=H0),
                                     src.rearrange("o h n c -> (o n) h c")).then_inc(s_yld, 16)
                sp.dma_start(gs[:, :, :], g_dram[bass.ds(t, 1)].rearrange("o s p c -> (o p) s c")).then_inc(s_gld, 16)

            load(0)
            for half, ready in enumerate((s_w1, s_w1b)):
                at = slice(half * (E1 // 2), (half + 1) * (E1 // 2))
                sp.dma_start(ckvT[:, at, :], d["L1_ffn_W1"][at].rearrange("e i f -> i e f")).then_inc(ready, 16)
            for a in range(2):
                sp.dma_start(w2[:, :, a, :], d["L1_ffn_W2"].rearrange("e (a f) n -> a f e n", a=2)[a]).then_inc(s_w2, 16)

            def store_tile(dst, src, t, signal):
                r = dst.rearrange("(s b) (t n) d -> t b n s d", b=BS, n=TP)
                for b in range(BS):
                    sp.dma_start(r[bass.ds(t, 1), b].rearrange("o n s d -> (o n) s d"), src[TP * b:TP * (b + 1)]).then_inc(signal, 16)

            def tile(t, last):
                sp.wait_ge(s_x2, t + 1)
                store_tile(x2_dram, xs[:, :, :], t, s_x2st)
                sp.wait_ge(s_x2st, (t + 1) * (16 * BS))
                if not last:
                    sp.wait_ge(s_xc, t + 1)
                    load(t + 1)
                sp.wait_ge(s_g1, t + 1)
                store_tile(g1_dram, acc[:, :, :], t, s_g1st)

            with sp.Fori(0, NT - 1) as t:
                tile(t, False)
            tile(NT - 1, True)
            sp.wait_ge(s_hid, NT * 2 * E1)
            sp.wait_ge(s_w2o, NT * E1)
            sp.dma_start(rep_stage, d["c_rep"]).then_inc(s_rep_ld, 16)
            sp.wait_ge(s_rep, 1)
            sp.dma_start(rep_stage[0:2 * H1, :], d["c_esel"]).then_inc(s_rep_ld, 16)

            sp.wait_ge(s_g1st, NT * 16 * BS)

            def load_b(b, par):
                view = lambda dram: dram[bass.ds(b, 1)].rearrange("o (k n) d -> n (o k) d", k=2)
                sp.dma_start(x2b[par], view(x2_dram)).then_inc(s_x2l[par], 16)
                sp.dma_start(g1b[par], view(g1_dram)).then_inc(s_g1l[par], 16)

            load_b(0, 0)
            load_b(1, 1)

            def finish(b, par, more):
                sp.wait_ge(s_done, b + 1)
                sp.dma_start(out_dram[bass.ds(b, 1)].rearrange("o (k n) d -> n (o k) d", k=2), outb).then_inc(s_ost, 16)
                if more:
                    load_b(b + 2, par)

            with sp.Fori(0, B // 2 - 1) as i:
                for par in range(2):
                    finish(i * 2 + par, par, True)
            finish(B - 2, 0, False)
            finish(B - 1, 1, False)
            sp.wait_ge(s_ost, B * 16)

        @block.gpsimd
        def _(pool):
            pool.memset(rows[:, :], 0.0).then_inc(s_init, 1)
            for i, (buffer, value) in enumerate(((wkv[:, :], 0.0), (eps[:, 0:1], LN_EPS), (ones[:, :], 1.0))):
                pool.wait_ge(s_init, i + 1)
                pool.memset(buffer, value).then_inc(s_init, 1)
            pool.wait_ge(s_init, 4)
            pool.wait_ge(s_w1s, 4)
            pool.memset(ckvT[DC1:DC1 + 1, :, :], 1.0).then_inc(s_init, 1)
            pool.wait_ge(s_init, 5)
            with pool.Fori(0, NT) as t:
                at = bass.ds(t * TP, TP)
                for j, (hi, lo) in enumerate(((qh, ql), (kh, kl))):
                    pool.wait_ge(s_qkh, t * 2 + (j + 1))
                    pool.tensor_tensor(lo[:, :, at], rope[:, 2 * j, :].rearrange("p (b n) -> p b n", n=TP), hi[:, :, at].bitcast(F32), ALU.subtract).then_inc(s_qkl, 1)
            pool.wait_ge(s_w2o, NT * E1)
            for i in range(2):
                pool.wait_ge(s_init, 5 + i)
                pool.memset(vp[i], 1.0).then_inc(s_init, 1)

        @block.scalar
        def _(act):
            act.wait_ge(s_w, NW * 16)
            act.wait_ge(s_cols_ps, 1)
            act.activation(cols[:, :], pb[:, 0, 0:2 * E1 + 4], ACT.Copy).then_inc(s_cols, 1)
            act.wait_ge(s_cols_ps, 2)
            act.activation(rcols[:, :], pb[:, 1, 0:2], ACT.Copy).then_inc(s_cols, 1)
            act.wait_ge(s_cols, 2)
            act.wait_ge(s_init, 4)

            with act.Fori(0, NT) as t:
                act.wait_ge(s_yt_ps, t + 1)
                act.activation(yT[:, :], pb[:, 0, :], ACT.Copy, scale=cols[:, 2 * E1 + 2:2 * E1 + 3]).then_inc(s_yt, 1)
                act.wait_ge(s_xc, t + 1)
                act.activation(xn[:, :, :], xc[:, :, :], ACT.Square).then_inc(s_sq, 1)
                act.wait_ge(s_var, t + 1)
                act.activation(stat[:, 3, :], stat[:, 2, :], ACT.Sqrt, bias=eps[:, 0:1], scale=1.0 / D).then_inc(s_std, 1)
                act.wait_ge(s_xt_ps, t + 1)
                act.activation(xt_hi[:, :], pb[:, 0, :], ACT.Copy).then_inc(s_xth, 1)
                act.wait_ge(s_cen, t + 1)
                act.activation(raw[:, :, :], logits[:, :, :], ACT.Exp).then_inc(s_exp, 1)
                act.wait_ge(s_kv_ps, t + 1)
                act.wait_ge(s_w1s, 4)
                at = bass.ds(t * TP, TP)
                act.activation(ckvT[0:DC1, :, at], pb[0:DC1, 0, :].rearrange("p (b n) -> p b n", n=TP), ACT.Gelu,
                               bias=cols[0:DC1, 2 * E1 + 3:2 * E1 + 4]).then_inc(s_kv, 1)
                for j, hi in enumerate((qh, kh)):
                    act.wait_ge(s_rope_done, t * 2 + (j + 1))
                    act.activation(rope[:, 2 * j, :], rope[:, 2 * j, :], ACT.Gelu).then_inc(s_gelu, 1)
                for j, hi in enumerate((qh, kh)):
                    act.wait_ge(s_gelu, t * 2 + (j + 1))
                    act.activation(hi[:, :, at], rope[:, 2 * j, :].rearrange("p (b n) -> p b n", n=TP), ACT.Copy).then_inc(s_qkh, 1)
                act.wait_ge(s_gT_ps, t + 1)
                act.activation(gT[:, :], pb[0:E1, 1, :], ACT.Copy).then_inc(s_gT, 1)
                act.wait_ge(s_b2, t + 1)
                act.wait_ge(s_g1st, t * (16 * BS))
                act.activation(acc[:, :, :], pb[:, 7, :].rearrange("p (s c) -> p s c", s=NS), ACT.Copy).then_inc(s_acc0, 1)
                for r in range(2 * E1):
                    act.wait_ge(s_w1o, t * (2 * E1) + (r + 1))
                    if r >= HR:
                        act.wait_ge(s_w2o, t * E1 + ((r - HR) // 2 + 1))
                    act.activation(hid[:, r % HR, :], pb[:, 2 + r % 3, :], ACT.Relu, bias=cols[:, r:r + 1]).then_inc(s_hid, 1)
                act.wait_ge(s_acc, t * (NS * E1) + NS * E1)
                act.activation(acc[:, :, :], acc[:, :, :], ACT.Silu).then_inc(s_g1, 1)


            def a_unit(b, par, i):
                if i == 0:
                    act.activation(ckv_b[0:DC1 + 1, :], ckvT[0:DC1 + 1, bass.ds(b, 1), :].rearrange("p o n -> p (o n)"), ACT.Copy).then_inc(s_ckb, 1)
                if not BY_ACT[i]:
                    return
                src = pb[:, i % 2, :]
                act.wait_ge(s_ua, b * NU + (i + 1))
                if UNITS[i] == "k":
                    act.activation(kr[par][:, 512 * i:512 * (i + 1)], src, ACT.Copy).then_inc(s_ua_act, 1)
                elif UNITS[i] == "q_act":
                    for h in range(H1 // 2, H1):
                        g, j = h // 4 - 2, h % 4
                        last = act.activation(qb[par][:, h, :], src[:, N * g:N * (g + 1)], ACT.Copy, scale=qmask[:, j:j + 1])
                    last.then_inc(s_ua_act, 1)
                elif UNITS[i] == "v":
                    act.activation(vp[par][:, :, :, 0:HD1], src[:, 0:2 * D].rearrange("p (k h c) -> p k h c", k=2, h=H1),
                                   ACT.Copy).then_inc(s_ua_act, 1)
                else:
                    act.activation(mT[par][:, :], src[0:2 * H1, 0:N], ACT.Copy).then_inc(s_ua_act, 1)

            def x_unit(b, par, u):
                act.wait_ge(s_st, b * XU + (u + 1))
                act.wait_ge(s_pv, b * XU + max(u - 1, 0))
                at = 512 * (2 + 2 * (u % 2))
                act.activation(pt[:, u % 2, :], pbf[:, at:at + 3 * N], ACT.Exp, scale=float(1.0 / np.sqrt(HD1))).then_inc(s_pt, 1)

            def both(ba, bx, pa, px):
                for i in range(NU):
                    if ba is not None:
                        a_unit(ba, pa, i)
                    if bx is not None and i % 2 == 0 and i // 2 < XU:
                        x_unit(bx, px, i // 2)
                if bx is not None:
                    act.wait_ge(s_oT_ps, bx + 1)
                    act.activation(oT[:, :], pb[:, 7, 0:N], ACT.Copy).then_inc(s_oT, 1)

            act.wait_ge(s_init, 7)
            act.wait_ge(s_w2o, NT * E1)
            act.wait_ge(s_kv, NT)
            act.wait_ge(s_rep, 2)
            both(0, None, 0, None)
            with act.Fori(0, B // 2 - 1) as i:
                both(i * 2 + 1, i * 2, 1, 0)
                both(i * 2 + 2, i * 2 + 1, 0, 1)
            both(B - 1, B - 2, 1, 0)
            both(None, B - 1, None, 1)

        @block.tensor
        def _(pe):
            def mm(out, l, r, start=True, stop=True):
                return pe.matmul(out, l, r, start=start, stop=stop, skip_group_check=True)

            def split3(out, l_hi, l_lo, r_hi, r_lo):
                mm(out, l_hi, r_hi, stop=False)
                mm(out, l_hi, r_lo, start=False, stop=False)
                return mm(out, l_lo, r_hi, start=False)

            pe.wait_ge(s_w, NW * 16)
            pe.transpose(pb[:, 0, 0:2 * E1 + 4], rows[:, :], ident[0:2 * E1 + 4, 0:2 * E1 + 4]).then_inc(s_cols_ps, 1)
            pe.wait_ge(s_cols, 1)
            mm(pb[:, 1, 0:2], rot[:, :], cols[:, 2 * E1:2 * E1 + 2]).then_inc(s_cols_ps, 1)
            pe.wait_ge(s_cols, 2)
            pe.wait_ge(s_prep, PREP)

            with pe.Fori(0, NT) as t:
                sub = [slice(P * s, P * (s + 1)) for s in range(NS)]
                pe.wait_ge(s_yld, (t + 1) * (16 * NS * BS))
                pe.wait_ge(s_kv, t)
                pe.wait_ge(s_acc, t * (NS * E1))
                for s in range(NS):
                    last = pe.transpose(pb[:, 0, sub[s]], ys[:, s, :], ident[:, :])
                last.then_inc(s_yt_ps, 1)
                pe.wait_ge(s_yt, t + 1)
                pe.wait_ge(s_gT, t)
                for s in range(NS):
                    last = mm(pb[:, 1, sub[s]], yT[:, sub[s]], wo0[:, :])
                last.then_inc(s_s_ps, 1)
                pe.wait_ge(s_xn, t + 1)
                for s in range(NS):
                    last = pe.transpose(pb[:, 0, sub[s]], xn[:, s, :], ident[:, :])
                last.then_inc(s_xt_ps, 1)
                pe.wait_ge(s_xtl, t + 1)
                for s in range(NS):
                    last = split3(pb[:, 1, E1 * s:E1 * (s + 1)], xt_hi[:, sub[s]], xt_lo[:, sub[s]], gate_hi[:, :], gate_lo[:, :])
                last.then_inc(s_lg, 1)
                split3(pb[:, 0, :], wkv_hi[:, :], wkv_lo[:, :], xt_hi[:, :], xt_lo[:, :]).then_inc(s_kv_ps, 1)
                for j in range(4):
                    split3(pb[:, 2 + j, :], wqk_hi[:, j, :], wqk_lo[:, j, :], xt_hi[:, :], xt_lo[:, :]).then_inc(s_qk_ps, 1)
                pe.wait_ge(s_gt, t + 1)
                for s in range(NS):
                    last = pe.transpose(pb[0:E1, 1, sub[s]], gtok[:, s, :], ident[:, :])
                last.then_inc(s_gT_ps, 1)
                pe.wait_ge(s_gT, t + 1)
                for s in range(NS):
                    last = mm(pb[:, 7, sub[s]], gT[:, sub[s]], b2[:, :])
                last.then_inc(s_b2, 1)
                pe.wait_ge(s_rope_done, t * 2 + 2)
                pe.wait_ge(s_w1s, 4)
                pe.wait_ge(s_w2, 32)
                for e in range(E1 + 1):
                    if e < E1:
                        for a in range(2):
                            r = 2 * e + a
                            if r >= 3:
                                pe.wait_ge(s_hid, t * (2 * E1) + (r - 2))
                            at = slice(P * r, P * (r + 1))
                            split3(pb[:, 2 + r % 3, :], w1_hi[:, at], w1_lo[:, at], xt_hi[:, :], xt_lo[:, :]).then_inc(s_w1o, 1)
                    if e > 0:
                        x = e - 1
                        pe.wait_ge(s_hid, t * (2 * E1) + (2 * x + 2))
                        if x >= 2:
                            pe.wait_ge(s_acc, t * (NS * E1) + NS * (x - 1))
                        for s in range(NS):
                            for a in range(2):
                                last = mm(pb[:, 5 + x % 2, sub[s]], hid[:, (2 * x + a) % HR, sub[s]], w2[:, x, a, :],
                                          start=(a == 0), stop=(a == 1))
                        last.then_inc(s_w2o, 1)

            def a_unit(b, par, i):
                u, bank = UNITS[i], pb[:, i % 2, :]
                if i >= 2:
                    pe.wait_ge(*read(b, i - 2))
                elif i == 0:
                    pe.wait_ge(s_ua_dve, b * N_DVE)
                else:
                    pe.wait_ge(s_ua_act, b * N_ACT)
                if u == "k" or u[0] == "q":
                    hi, lo, kind = (kh, kl, 2) if u == "k" else (qh, ql, 0)
                    for g in range(2):
                        group = 2 * (i % 2) + g
                        out = bank[:, N * g:N * (g + 1)]
                        mm(out, rep[:, kind, group, :], hi[:, bass.ds(b, 1), :].rearrange("p o n -> p (o n)"), stop=False)
                        last = mm(out, rep[:, kind + 1, group, :], lo[:, bass.ds(b, 1), :].rearrange("p o n -> p (o n)"), start=False)
                elif u == "v":
                    pe.wait_ge(s_ckb, b + 1)
                    for k in range(2):
                        last = mm(bank[:, D * k:D * (k + 1)], ckv_b[0:DC1 + 1, P * k:P * (k + 1)], wv[:, :])
                elif u == "max0":
                    j = i - UNITS.index(u)
                    pe.wait_ge(*read(b, 3))
                    for m in range(4):
                        h, out = 4 * j + m, bank[:, P * m:P * (m + 1)]
                        mm(out, qb[par][:, h, 0:P], kr[par][:, N * (h // 4):N * (h // 4) + P], stop=False)
                        last = mm(out, ident_r[:, :], mask_r[:, :], start=False)
                elif u == "max1":
                    j = i - UNITS.index(u)
                    for m in range(2):
                        h, out = 2 * j + m, bank[:, N * m:N * (m + 1)]
                        mm(out, qb[par][:, h, P:N], kr[par][:, N * (h // 4):N * (h // 4 + 1)], stop=False)
                        last = mm(out[:, P:N], ident_r[:, :], mask_r[:, :], start=False)
                else:
                    pe.wait_ge(s_mhl, b + 1)
                    for k in range(2):
                        last = pe.transpose(bank[0:2 * H1, P * k:P * (k + 1)], mhl[:, k, :].bitcast(F32), ident[:, :])
                last.then_inc(s_ua, 1)

            def scores_t(b, par, u):
                if u == 0:
                    pe.wait_ge(s_ua_act, (b + 1) * N_ACT)
                    pe.wait_ge(s_pt, b * XU)
                elif u >= 2:
                    pe.wait_ge(s_pt, b * XU + (u - 1))
                for m in range(2):
                    h = 2 * u + m
                    keys = N * (h // 4)
                    for k, lo in ((0, N * m), (1, 2 * N + P * m)):
                        width = N - P * k
                        at = 512 * (2 + 2 * (u % 2)) + lo
                        out = pbf[:, at:at + width]
                        mm(out, kr[par][:, keys + P * k:keys + P * (k + 1)], qb[par][:, h, P * k:N], stop=False)
                        mm(out, esel[:, h, :], mT[par][:, P * k:N], start=False, stop=False)
                        last = mm(out[:, 0:P], mask_r[:, :], ident_r[:, :], start=False)
                last.then_inc(s_st, 1)

            def values(b, par, u):
                pe.wait_ge(s_pt, b * XU + (u + 1))
                if u == 0:
                    pe.wait_ge(s_ot, b)
                out = pb[:, 6, 0:2 * H1 * (HD1 + 1)].rearrange("p (k h c) -> p k h c", k=2, h=H1)
                for m in range(2):
                    h = 2 * u + m
                    v0, v1 = vp[par][:, 0, h, :], vp[par][:, 1, h, :]
                    mm(out[:, 0, h, :], pt[:, u % 2, N * m:N * m + P], v0)
                    mm(out[:, 1, h, :], pt[:, u % 2, N * m + P:N * (m + 1)], v0, stop=False)
                    last = mm(out[:, 1, h, :], pt[:, u % 2, 2 * N + P * m:2 * N + P * (m + 1)], v1, start=False)
                last.then_inc(s_pv, 1)

            def both(ba, bx, pa, px):
                for i in range(NU):
                    if bx is not None and i % 2 == 0:
                        u = i // 2
                        if u < XU:
                            scores_t(bx, px, u)
                        if 0 < u <= XU:
                            values(bx, px, u - 1)
                    if ba is not None:
                        a_unit(ba, pa, i)
                if bx is not None:
                    pe.wait_ge(s_ot, bx + 1)
                    pe.wait_ge(s_done, bx)
                    for k in range(2):
                        last = pe.transpose(pb[:, 7, P * k:P * (k + 1)], o_tok[:, k, :], ident[:, :])
                    last.then_inc(s_oT_ps, 1)
                    pe.wait_ge(s_oT, bx + 1)
                    for k in range(2):
                        out = pb[:, 7, N + D * k:N + D * (k + 1)]
                        mm(out, oT[:, P * k:P * (k + 1)], wo[:, :], stop=False)
                        last = mm(out, ones[:, :], bo[:, :], start=False)
                    last.then_inc(s_wo, 1)

            pe.wait_ge(s_rep, 2)
            pe.wait_ge(s_qkl, NT * 2)
            both(0, None, 0, None)
            with pe.Fori(0, B // 2 - 1) as i:
                both(i * 2 + 1, i * 2, 1, 0)
                both(i * 2 + 2, i * 2 + 1, 0, 1)
            both(B - 1, B - 2, 1, 0)
            both(None, B - 1, None, 1)

        @block.vector
        def _(dve):
            def over(ap, n):
                return ap.unsqueeze(len(ap.shape)).to_broadcast([*ap.shape, n])

            half = D // 2
            dve.wait_ge(s_w, NW * 16)
            dve.wait_ge(s_init, 2)
            for j in range(2):
                w, hi = wproj[:, j, :], wqk_hi[:, 2 * j, :]
                dve.tensor_copy(hi, w).then_inc(s_prep, 1)
                dve.tensor_scalar(wqk_hi[:, 2 * j + 1, 0:half], w[:, half:D], -1.0, None, ALU.mult).then_inc(s_prep, 1)
                dve.tensor_copy(wqk_hi[:, 2 * j + 1, half:D], w[:, 0:half]).then_inc(s_prep, 1)
                dve.wait_ge(s_prep, 6 * j + 3)
                whole = hi.bitcast(F32)
                dve.tensor_tensor(wqk_lo[:, 2 * j, :], w, whole, ALU.subtract).then_inc(s_prep, 1)
                dve.tensor_tensor(wqk_lo[:, 2 * j + 1, 0:half], whole[:, half:D], w[:, half:D], ALU.subtract).then_inc(s_prep, 1)
                dve.tensor_tensor(wqk_lo[:, 2 * j + 1, half:D], w[:, 0:half], whole[:, 0:half], ALU.subtract).then_inc(s_prep, 1)
            dve.tensor_copy(wkv_hi[:, :], wkv[:, :]).then_inc(s_prep, 1)
            dve.tensor_copy(gate_hi[:, :], gate[:, :]).then_inc(s_prep, 1)
            dve.tensor_copy(ident_r[:, :], ident[:, :]).then_inc(s_prep, 1)
            dve.tensor_copy(mask_r[:, :], rope[:, 1, 0:P]).then_inc(s_prep, 1)
            dve.wait_ge(s_prep, 16)
            dve.tensor_tensor(wkv_lo[:, :], wkv[:, :], wkv_hi[:, :].bitcast(F32), ALU.subtract).then_inc(s_prep, 1)
            dve.tensor_tensor(gate_lo[:, :], gate[:, :], gate_hi[:, :].bitcast(F32), ALU.subtract).then_inc(s_prep, 1)
            for i, ready in enumerate((s_w1, s_w1b)):
                dve.wait_ge(ready, 16)
                n = E1 * F1 // 2
                src = ckvT[:, i * (E1 // 2):(i + 1) * (E1 // 2), :].rearrange("p e f -> p (e f)")
                at = slice(n * i, n * (i + 1))
                dve.tensor_copy(w1_hi[:, at], src).then_inc(s_w1s, 1)
                dve.wait_ge(s_w1s, 2 * i + 1)
                dve.tensor_tensor(w1_lo[:, at], src, w1_hi[:, at].bitcast(F32), ALU.subtract).then_inc(s_w1s, 1)
            dve.wait_ge(s_cols, 2)

            def mix(t):
                c = Count(t, LN)
                dve.wait_ge(s_gld, t * 16 + 16)
                dve.wait_ge(s_x, (t + 1) * (16 * BS))
                dve.wait_ge(s_s_ps, t + 1)
                dve.tensor_tensor(xc[:, :, :], pb[:, 1, :].rearrange("p (s c) -> p s c", s=NS), gs[:, :, :], ALU.mult).then_inc(s_ln, 1)
                dve.wait_ge(s_ln, c.next())
                dve.tensor_tensor(xs[:, :, :], xs[:, :, :], xc[:, :, :], ALU.add).then_inc(s_x2, 1)
                dve.wait_ge(s_x2, t + 1)
                dve.tensor_reduce(stat[:, 0, :], xs[:, :, :], AX.X, ALU.add).then_inc(s_ln, 1)
                dve.wait_ge(s_ln, c.next())
                dve.tensor_scalar(stat[:, 1, :], stat[:, 0, :], -1.0 / D, None, ALU.mult).then_inc(s_ln, 1)
                dve.wait_ge(s_ln, c.next())
                dve.tensor_tensor(xc[:, :, :], xs[:, :, :], over(stat[:, 1, :], D), ALU.add).then_inc(s_xc, 1)
                dve.wait_ge(s_sq, t + 1)
                dve.tensor_reduce(stat[:, 2, :], xn[:, :, :], AX.X, ALU.add).then_inc(s_var, 1)
                dve.wait_ge(s_std, t + 1)
                dve.reciprocal(stat[:, 4, :], stat[:, 3, :]).then_inc(s_ln, 1)
                dve.wait_ge(s_ln, c.next())
                dve.tensor_tensor(xn[:, :, :], xc[:, :, :], over(stat[:, 4, :], D), ALU.mult).then_inc(s_xn, 1)
                c.check()
                dve.wait_ge(s_xth, t + 1)
                dve.tensor_tensor(xt_lo[:, :], pb[:, 0, :], xt_hi[:, :].bitcast(F32), ALU.subtract).then_inc(s_xtl, 1)

            def turn(t):
                dve.wait_ge(s_qkl, t * 2)
                at = bass.ds(t * TP, TP)
                for j in range(2):
                    for m, (bias, table) in enumerate(((cols[:, 2 * E1 + j:2 * E1 + j + 1], cosT), (rcols[:, j:j + 1], sinT))):
                        dve.wait_ge(s_qk_ps, t * 4 + (2 * j + m + 1))
                        if (j, m) == (1, 1):
                            dve.wait_ge(s_rope_done, t * 2 + 1)
                        dst = rope[:, (2 * j, 1)[m], :].rearrange("p (b n) -> p b n", n=TP)
                        dve.scalar_tensor_tensor(out=dst, in0=pb[:, 2 + 2 * j + m, :].rearrange("p (b n) -> p b n", n=TP), scalar=bias,
                                                 in1=table[:, at].unsqueeze(1).to_broadcast([P, B, TP]),
                                                 op0=ALU.add, op1=ALU.mult).then_inc(s_rope, 1)
                    dve.wait_ge(s_rope, t * ROPE + 2 * (j + 1))
                    dve.tensor_tensor(rope[:, 2 * j, :], rope[:, 2 * j, :], rope[:, 1, :], ALU.add).then_inc(s_rope_done, 1)

            def route(t):
                c = Count(t, ROUTE)
                lg = pb[:, 1, 0:NS * E1].rearrange("p (s e) -> p s e", s=NS)
                peak, total = row1[:, 0, :], row1[:, 1, :]
                dve.wait_ge(s_lg, t + 1)
                dve.tensor_reduce(peak, lg, AX.X, ALU.max).then_inc(s_rt, 1)
                dve.wait_ge(s_rt, c.next())
                dve.tensor_tensor(logits[:, :, :], lg, over(peak, E1), ALU.subtract).then_inc(s_cen, 1)
                dve.wait_ge(s_exp, t + 1)
                dve.tensor_reduce(total, raw[:, :, :], AX.X, ALU.add).then_inc(s_rt, 1)
                dve.wait_ge(s_rt, c.next())
                dve.reciprocal(total, total).then_inc(s_rt, 1)
                dve.wait_ge(s_rt, c.next())
                dve.tensor_tensor(raw[:, :, :], raw[:, :, :], over(total, E1), ALU.mult).then_inc(s_rt, 1)
                dve.wait_ge(s_rt, c.next())
                dve.memset(carrier[:, :], 0.0)
                for s in range(NS):
                    dve.max(top8[:, s, :], raw[:, s, :]).then_inc(s_rt, 1)
                dve.wait_ge(s_rt, c.next(NS))
                dve.memset(top8[:, :, K1:8], -1.0).then_inc(s_rt, 1)
                dve.wait_ge(s_rt, c.next())
                dve.memset(carrier[:, :], 0.0)
                for s in range(NS):
                    last = dve.match_replace(replaced[:, s, :], top8[:, s, :], raw[:, s, :], -2.0)
                last.then_inc(s_rt, 1)
                dve.wait_ge(s_rt, c.next())
                dve.tensor_tensor(replaced[:, :, :], replaced[:, :, :], raw[:, :, :], ALU.not_equal).then_inc(s_rt, 1)
                dve.wait_ge(s_rt, c.next())
                dve.tensor_tensor(raw[:, :, :], replaced[:, :, :], raw[:, :, :], ALU.mult).then_inc(s_rt, 1)
                dve.wait_ge(s_rt, c.next())
                dve.tensor_reduce(total, raw[:, :, :], AX.X, ALU.add).then_inc(s_rt, 1)
                dve.wait_ge(s_rt, c.next())
                dve.tensor_scalar(total, total, 1e-12, None, ALU.max).then_inc(s_rt, 1)
                dve.wait_ge(s_rt, c.next())
                dve.reciprocal(total, total).then_inc(s_rt, 1)
                dve.wait_ge(s_rt, c.next())
                dve.tensor_tensor(gtok[:, :, :], raw[:, :, :], over(total, E1), ALU.mult).then_inc(s_gt, 1)
                c.check()

            def experts(t):
                dve.wait_ge(s_gt, t + 1)
                dve.wait_ge(s_acc0, t + 1)
                for e in range(E1):
                    dve.wait_ge(s_w2o, t * E1 + (e + 1))
                    for s in range(NS):
                        sub = slice(P * s, P * (s + 1))
                        if e:
                            dve.wait_ge(s_acc, t * (NS * E1) + (NS * (e - 1) + s + 1))
                        dve.scalar_tensor_tensor(out=acc[:, s, :], in0=pb[:, 5 + e % 2, sub], scalar=gtok[:, s, e:e + 1],
                                                 in1=acc[:, s, :], op0=ALU.mult, op1=ALU.add).then_inc(s_acc, 1)

            with dve.Fori(0, NT) as t:
                mix(t)
                route(t)
                turn(t)
                experts(t)

            dve.wait_ge(s_rep_ld, 16)
            dve.tensor_copy(rep[:, :, :, :].rearrange("p k g r -> p (k g r)"), rep_stage).then_inc(s_rep, 1)
            dve.wait_ge(s_rep_ld, 32)
            dve.tensor_copy(esel[:, :, :], rep_stage[0:2 * H1, :].rearrange("p (h m) -> p h m", h=H1)).then_inc(s_rep, 1)

            def a_unit(b, par, i):
                if BY_ACT[i]:
                    return
                src, u = pb[:, i % 2, :], UNITS[i]
                dve.wait_ge(s_ua, b * NU + (i + 1))
                if u == "q_dve":
                    for g in range(2):
                        q = src[:, N * g:N * (g + 1)].unsqueeze(1).to_broadcast([P, 4, N])
                        last = dve.tensor_tensor(qb[par][:, 4 * g:4 * (g + 1), :], q, over(qmask[:, :], N), ALU.mult)
                    last.then_inc(s_ua_dve, 1)
                    return
                j = i - UNITS.index(u)
                k, heads = (0, 4) if u == "max0" else (1, 2)
                dve.tensor_reduce(mrow[:, k, heads * j:heads * (j + 1)], src.rearrange("p (h n) -> p h n", h=heads), AX.X, ALU.max).then_inc(s_ua_dve, 1)
                if i == NU - 2:
                    dve.wait_ge(s_ua_dve, (b + 1) * N_DVE)
                    dve.tensor_copy(mhl[:, :, 0:H1], mrow[:, :, :]).then_inc(s_mc, 1)
                    dve.wait_ge(s_mc, b + 1)
                    dve.tensor_tensor(mhl[:, :, H1:2 * H1], mrow[:, :, :], mhl[:, :, 0:H1].bitcast(F32), ALU.subtract).then_inc(s_mhl, 1)

            def output(b, par, n):
                pv = pb[:, 6, 0:2 * H1 * (HD1 + 1)].rearrange("p (k h c) -> p k h c", k=2, h=H1)
                dve.wait_ge(s_pv, (b + 1) * XU)
                dve.reciprocal(rec, pv[:, :, :, HD1]).then_inc(s_rec, 1)
                dve.wait_ge(s_rec, b + 1)
                o = o_tok.rearrange("p k (h c) -> p k h c", h=H1)
                for k in range(2):
                    last = dve.tensor_tensor(o[:, k], pv[:, k, :, 0:HD1], over(rec[:, k, :], HD1), ALU.mult)
                last.then_inc(s_ot, 1)
                dve.wait_ge(s_wo, b + 1)
                dve.wait_ge(s_g1l[par], n * 16 + 16)
                dve.tensor_tensor(prodb, pb[:, 7, N:2 * N].rearrange("p (k c) -> p k c", k=2), g1b[par], ALU.mult).then_inc(s_fin, 1)
                dve.wait_ge(s_fin, b + 1)
                dve.wait_ge(s_x2l[par], n * 16 + 16)
                dve.wait_ge(s_ost, b * 16)
                dve.tensor_tensor(outb, prodb, x2b[par], ALU.add).then_inc(s_done, 1)

            for i in range(NU):
                a_unit(0, 0, i)
            with dve.Fori(0, B // 2 - 1) as n:
                for par in range(2):
                    for i in range(NU):
                        a_unit(n * 2 + (par + 1), 1 - par, i)
                    output(n * 2 + par, par, n)
            for i in range(NU):
                a_unit(B - 1, 1, i)
            output(B - 2, 0, B // 2 - 1)
            output(B - 1, 1, B // 2 - 1)


def build(nc, d, out):
    def scratch(name, *shape):
        return nc.dram_tensor(name, shape, F32).ap()

    z = scratch("z_scratch", NT, NS, BS, H0, TP, ZC)
    y = scratch("y_scratch", NT, P, TP, HD0)
    g0 = scratch("g0_scratch", NT, NS, P, D)
    x2 = scratch("x2_scratch", B, N, D)
    g1 = scratch("g1_scratch", B, N, D)
    with ExitStack() as ctx:
        def sem(name):
            return ctx.enter_context(nc.semaphore(name))

        layer0(nc, d, (z, y, g0), sem)
        layer1(nc, d, (y, g0, x2, g1), out, sem)


def constants():
    f = np.float32
    c = {
        "c_ident": np.eye(P, dtype=f),
        "c_onehot": np.tile(np.eye(E0, dtype=f), (2, 1)),
        "c_tri": np.tril(np.ones((G0, G0), f), -1).reshape(-1),
        "c_rot": np.roll(np.eye(P, dtype=f), D // 2, axis=1) * np.where(np.arange(P) < D // 2, 1, -1).astype(f)[:, None],
        "c_qmask": np.repeat(np.eye(4, dtype=f), P // 4, axis=0),
        "c_mask": np.where(np.arange(P)[None, :] > np.arange(P)[:, None], f(NEG), f(0)),
    }
    freq = (1.0 / 10000.0 ** (np.arange(0, D, 2, dtype=f) / f(D))).astype(f)
    angle = np.arange(N, dtype=f)[:, None] * freq[None, :]
    angle = np.concatenate([angle, angle], -1)
    c["c_cosT"] = np.ascontiguousarray(np.cos(angle).T)
    c["c_sinT"] = np.ascontiguousarray(np.sin(angle).T)
    rep = np.zeros((P, 4, 4, P), f)
    for kind, parts in enumerate(((0, 1), (2,), (0, 2), (1,))):
        for h in range(H1):
            for part in parts:
                for i in range(HD1):
                    rep[h * HD1 + i, kind, h // 4, 32 * (h % 4) + HD1 * part + i] = 1
    c["c_rep"] = rep.reshape(P, -1)
    esel = np.zeros((2, H1, H1, P), f)
    for h in range(H1):
        esel[:, h, h, :] = -1
    c["c_esel"] = esel.reshape(2 * H1, -1)
    return c


UNUSED = ("L1_attn_wq", "L1_attn_bq", "L1_attn_wqc", "L1_attn_bqc", "L1_attn_wkc", "L1_attn_bkc")


def kernel(**inputs):
    import concourse.bacc as _bacc
    from concourse.bass_utils import run_bass_kernel_spmd as _run

    nc = _bacc.Bacc("TRN2", target_bir_lowering=False, num_devices=1)
    arrays, d = {}, {}
    for name, a in {**inputs, **constants()}.items():
        if name in UNUSED:
            continue
        a = np.ascontiguousarray(a)
        arrays[f"in_{name}_dram"] = a
        d[name] = nc.dram_tensor(f"in_{name}_dram", a.shape, mybir.dt.from_np(a.dtype), kind="ExternalInput").ap()
    out = nc.dram_tensor("out_0_dram", (B, N, D), F32, kind="ExternalOutput").ap()
    build(nc, d, out)
    r = _run(nc, [arrays], core_ids=[0])
    return r.results[0]["out_0_dram"]
```

```python
from contextlib import ExitStack

import numpy as np

import concourse.bass as bass
from concourse import mybir

F32 = mybir.dt.float32
F32R = mybir.dt.float32r
BF16 = mybir.dt.bfloat16
ALU = mybir.AluOpType
ACT = mybir.ActivationFunctionType
AX = mybir.AxisListType

P = 128
B, N, D = 16, 256, 128
TP = 32
NT = N // TP
TOK = B * TP
NS = TOK // P
BS = P // TP
LN_EPS = 1e-5

H0, HD0 = 8, 16
ZC = 5 * HD0 + 1
ZW = H0 * ZC
ZQ, ZK, ZV, ZF, ZG, ZB = 0, 16, 32, 48, 64, 80
RNN_EPS = 1e-6
E0, F0, K0, G0, TG0 = 64, 64, 8, 8, 4
EG0 = E0 // G0
PAIRS = E0 // 2
ROUTE_SCALE = 2.5
NEG = -1e30
SLOTS = 3 * PAIRS + 2
STEPS = 13

H1, HD1, DC1 = 16, 8, 32
E1, F1, K1 = 16, 256, 3


class Count:

    def __init__(self, tile, per_tile):
        self.base, self.per_tile, self.n = tile * per_tile, per_tile, 0

    def next(self, k=1):
        self.n += k
        return self.base + self.n

    def check(self):
        assert self.n == self.per_tile, (self.n, self.per_tile)


def layer0(nc, d, scratch, sem):
    z_dram, y_dram, g_dram = scratch
    with ExitStack() as ctx:
        def sb(name, shape, dt=F32):
            return ctx.enter_context(nc.sbuf_tensor(name, shape, dt))

        ident = sb("ident", [P, P])
        onehot = sb("onehot", [P, E0])
        tri = sb("tri", [P, G0 * G0])
        bias64 = sb("bias64", [P, E0])
        eps = sb("eps", [P, 2])
        carrier = sb("carrier", [P, 1])
        wf1 = sb("wf1", [P, 2, HD0])
        wf1T = sb("wf1T", [HD0, 2, P])
        wf2 = sb("wf2", [HD0, 2, D])
        wbeta = sb("wbeta", [P, H0])
        gate_w = sb("gate_w", [E0, D])
        wp = sb("wp", [P, H0, ZC])
        wp_hi, wp_lo = sb("wp_hi", [P, ZW], F32R), sb("wp_lo", [P, ZW], F32R)
        wr_hi, wr_lo = sb("wr_hi", [P, E0], F32R), sb("wr_lo", [P, E0], F32R)
        wg_hi, wg_lo = sb("wg_hi", [P, (E0 + 1) * F0], F32R), sb("wg_lo", [P, (E0 + 1) * F0], F32R)
        wu_hi, wu_lo = sb("wu_hi", [P, (E0 + 1) * F0], F32R), sb("wu_lo", [P, (E0 + 1) * F0], F32R)
        wd = sb("wd", [P, PAIRS + 1, D])
        sel = sb("sel", [P, E0, F0], F32R)
        x_sb = sb("x_sb", [P, NS, D])
        xc = sb("xc", [P, NS, D])
        xn = sb("xn", [P, NS, D])
        stat = sb("stat", [P, 5, NS])
        xt_hi, xt_lo = ([sb(f"xt_{part}{i}", [P, TOK], F32R) for i in range(2)] for part in ("hi", "lo"))
        zs = sb("zs", [P, NS, ZW])
        scores = sb("scores", [P, NS, E0])
        biased = sb("biased", [P, NS, E0])
        top_of_group = sb("top_of_group", [P, NS * G0, 8])
        group_score = sb("group_score", [P, NS, G0])
        cmp_gt = sb("cmp_gt", [P, NS, G0, G0])
        cmp_eq = sb("cmp_eq", [P, NS, G0, G0])
        penalty = sb("penalty", [P, NS, G0])
        masked = sb("masked", [P, NS, E0])
        top8 = sb("top8", [P, NS, 8])
        replaced = sb("replaced", [P, NS, E0])
        cw = sb("cw", [P, NS, E0])
        cw_sum = sb("cw_sum", [P, NS])
        cws = sb("cws", [P, NS, 2 * E0], F32R)
        cwt = sb("cwt", [P, TOK], F32R)
        RING = 3
        act_g = sb("act_g", [P, RING, TOK])
        act_u = sb("act_u", [P, RING, TOK])
        act_c = sb("act_c", [P, RING, TOK])
        hid1 = sb("hid1", [P, TOK])
        hid = sb("hid", [P, 2, TOK])
        yt = act_g[:, 0, :]
        g_out = act_u[:, 0, :].rearrange("p (s c) -> p s c", s=NS)
        zr = [sb(f"zr{i}", [P, TP, ZC]) for i in range(2)]
        am = sb("am", [P, TP, HD0])
        prod = sb("prod", [P, TP, HD0])
        coef = sb("coef", [P, 6, TP])
        wh = sb("wh", [P, TP, 4, HD0])
        x1 = sb("x1", [P, HD0, HD0])
        x2 = sb("x2", [P, HD0, HD0])
        yo = sb("yo", [P, TP, HD0])
        ra = ctx.enter_context(nc.psum_tensor("ra", [P, 4, HD0, HD0], F32))
        rs = ctx.enter_context(nc.psum_tensor("rs", [P, 2, HD0, HD0], F32))
        pb = ctx.enter_context(nc.psum_tensor("pb", [P, 5, 512], F32))
        pbf = pb[:, :, :].rearrange("p a b -> p (a b)")

        s_x = sem("x_loaded")
        s_small = sem("small_weights_loaded")
        s_stage = [sem(f"stage_loaded{i}") for i in range(3)]
        s_wd = sem("down_weights_loaded")
        s_eps = sem("eps_set")
        s_sel = sem("selectors_ready")
        s_w1t_ps = sem("transposed_small_in_psum")
        s_w1t = sem("transposed_small_copied")
        s_w12_ps = sem("products_in_psum")
        s_w12 = sem("products_copied")
        s_wp = sem("projection_weights_split")
        s_split = sem("expert_weights_split")
        s_hi_tmp = sem("expert_weight_hi_written")
        s_xc = sem("centred")
        s_sq = sem("squared")
        s_var = sem("variance_summed")
        s_std = sem("std_ready")
        s_xn = sem("normalised")
        s_ln = sem("ln_chain")
        s_xt_ps = sem("xT_in_psum")
        s_xth = sem("xT_hi_ready")
        s_xtl = sem("xT_lo_ready")
        s_zp = sem("z_in_psum")
        s_zc = sem("z_copied")
        s_zst = sem("z_stored")
        s_zld = sem("z_loaded")
        s_lg = sem("router_logits_in_psum")
        s_sc = sem("router_scores_ready")
        s_rt = sem("router_chain")
        s_cws = sem("router_weights_split")
        s_cwt_ps = sem("router_weightsT_in_psum")
        s_cwt = sem("router_weightsT_ready")
        s_slot = sem("moe_slot_filled")
        s_ev = sem("moe_slot_copied")
        s_h1 = sem("moe_product_ready")
        s_h = sem("moe_hidden_ready")
        s_dn = sem("moe_hidden_used")
        s_s0 = sem("state_zeroed")
        s_y = sem("moe_out_copied")
        s_g_ps = sem("moe_outT_in_psum")
        s_g = sem("gate_ready")
        s_gst = sem("gate_stored")
        s_sig = sem("z_sigmoid_done")
        s_silu = sem("z_silu_done")
        s_kk = sem("k_squares_summed")
        s_kn = sem("k_norm_ready")
        s_pr = sem("prep_chain")
        s_st = sem("recurrence_step")
        s_po = sem("post_chain")
        s_yy = sem("y_squares_summed")
        s_yn = sem("y_norm_ready")
        s_yo = sem("y_ready")
        s_yst = sem("y_stored")

        LN, PREP, POST, ROUTE = 3, 13, 7, 57
        LN_AT, ROUTE_AT = (3, 6, 7, 12), 20
        PROJECT_PAIR, NORM_SLOT, INPUT_SLOT = 15, 24, 66
        SMALL = 13

        stages = [r[:, 0:2, :].rearrange("p a b -> p (a b)") for r in (act_g, act_u, act_c)]
        CH = 16
        chunks = [(w, c) for c in range(E0 // CH) for w in (0, 1)] + [(2, 0)]

        block = ctx.enter_context(nc.Block())

        @block.sync
        def _(sp):
            xr = d["L0_attn_x"].rearrange("(s b) (t n) d -> t b n s d", b=BS, n=TP)

            def load_x(t):
                for b in range(BS):
                    src = xr[bass.ds(t, 1), b].rearrange("o n s d -> (o n) s d")
                    sp.dma_start(x_sb[TP * b:TP * (b + 1), :, :], src).then_inc(s_x, 16)

            load_x(0)
            sp.dma_start(ident[:, :], d["c_ident"]).then_inc(s_small, 16)
            sp.dma_start(onehot[:, :], d["c_onehot"]).then_inc(s_small, 16)
            sp.dma_start(tri[:, :], d["c_tri"].rearrange("(o c) -> o c", o=1).to_broadcast([P, G0 * G0])).then_inc(s_small, 16)
            sp.dma_start(bias64[:, :], d["L0_ffn_gate_bias"].rearrange("(o c) -> o c", o=1).to_broadcast([P, E0])).then_inc(s_small, 16)
            sp.dma_start(wf1[:, 0, :], d["L0_attn_Wf1"]).then_inc(s_small, 16)
            sp.dma_start(wf1[:, 1, :], d["L0_attn_Wog1"]).then_inc(s_small, 16)
            sp.dma_start(wf2[:, 0, :], d["L0_attn_Wf2"]).then_inc(s_small, 16)
            sp.dma_start(wf2[:, 1, :], d["L0_attn_Wog2"]).then_inc(s_small, 16)
            sp.dma_start(gate_w[:, :], d["L0_ffn_gate_w"]).then_inc(s_small, 16)
            for at, name in ((ZQ, "L0_attn_Wq"), (ZK, "L0_attn_Wk"), (ZV, "L0_attn_Wv")):
                sp.dma_start(wp[:, :, at:at + HD0], d[name].rearrange("i (h c) -> i h c", h=H0)).then_inc(s_small, 16)
            sp.dma_start(wbeta[:, :], d["L0_attn_Wbeta"]).then_inc(s_small, 16)
            names = ("L0_ffn_We_gate", "L0_ffn_We_up")
            def load_chunk(k):
                w, c = chunks[k]
                if k >= 3:
                    sp.wait_ge(s_split, k - 2)
                dst = stages[k % 3]
                if w < 2:
                    src = d[names[w]][c * CH:(c + 1) * CH].rearrange("e i f -> i e f")
                    sp.dma_start(dst[:, 0:CH * F0].rearrange("p (e f) -> p e f", e=CH), src).then_inc(s_stage[k % 3], 16)
                else:
                    sp.dma_start(dst[:, 0:F0], d["L0_ffn_Ws_gate"]).then_inc(s_stage[k % 3], 16)
                    sp.dma_start(dst[:, F0:2 * F0], d["L0_ffn_Ws_up"]).then_inc(s_stage[k % 3], 16)

            for k in range(3):
                load_chunk(k)

            def pass_z(t, par):
                for s in range(NS):
                    sp.wait_ge(s_zc, t * NS + (s + 1))
                    for b in range(BS):
                        sp.dma_start(z_dram[bass.ds(t, 1), s, b].rearrange("o h n c -> (o n) h c"),
                                     zs[TP * b:TP * (b + 1), s, :].rearrange("p (h c) -> p h c", h=H0)).then_inc(s_zst, 16)
                sp.wait_ge(s_zst, (t + 1) * (16 * NS * BS))
                sp.dma_start(zr[par][:, :, :], z_dram[bass.ds(t, 1)].rearrange("o s b h n c -> (o s b h) n c")).then_inc(s_zld, 16)

            def store_gate(t):
                sp.wait_ge(s_g, t + 1)
                sp.dma_start(g_dram[bass.ds(t, 1)].rearrange("o s p c -> (o p) s c"), g_out).then_inc(s_gst, 16)

            def store_y(t):
                sp.wait_ge(s_yo, t + 1)
                sp.dma_start(y_dram[bass.ds(t, 1)].rearrange("o q n c -> (o q) n c"), yo[:, :, :]).then_inc(s_yst, 16)

            pass_z(0, 0)
            for k in range(3, len(chunks)):
                load_chunk(k)
            sp.dma_start(wd[:, 0:PAIRS, :], d["L0_ffn_We_down"].rearrange("(p a) f n -> (a f) p n", a=2)).then_inc(s_wd, 16)
            sp.dma_start(wd[0:F0, PAIRS, :], d["L0_ffn_Ws_down"]).then_inc(s_wd, 16)
            sp.wait_ge(s_xc, 1)
            load_x(1)
            with sp.Fori(0, NT // 2 - 1) as i:
                for par in range(2):
                    t = i * 2 + par
                    sp.wait_ge(s_yo, t)
                    pass_z(t + 1, 1 - par)
                    sp.wait_ge(s_xc, t + 2)
                    load_x(t + 2)
                    store_gate(t)
                    store_y(t)
            pass_z(NT - 1, 1)
            store_gate(NT - 2)
            store_y(NT - 2)
            store_gate(NT - 1)
            store_y(NT - 1)
            sp.wait_ge(s_yst, NT * 16)
            sp.wait_ge(s_gst, NT * 16)

        @block.gpsimd
        def _(pool):
            pool.memset(eps[:, 0:1], LN_EPS).then_inc(s_eps, 1)
            pool.memset(eps[:, 1:2], RNN_EPS).then_inc(s_eps, 1)
            for k, (w, c) in enumerate(chunks):
                pool.wait_ge(s_stage[k % 3], 16 * (k // 3 + 1) if w < 2 else 16 * (k // 3 + 2))
                parts = ([((wg_hi, wg_lo), (wu_hi, wu_lo))[w] + (c * CH * F0, CH * F0, 0)] if w < 2 else
                         [(wg_hi, wg_lo, E0 * F0, F0, 0), (wu_hi, wu_lo, E0 * F0, F0, F0)])
                for m, (hi, lo, at, n, off) in enumerate(parts):
                    src = stages[k % 3][:, off:off + n]
                    pool.tensor_scalar(hi[:, at:at + n], src, 1.0, 1.0, ALU.mult, ALU.mult).then_inc(s_hi_tmp, 1)
                    pool.wait_ge(s_hi_tmp, k + 1 + m)
                    pool.tensor_tensor(lo[:, at:at + n], src, hi[:, at:at + n].bitcast(F32), ALU.subtract).then_inc(s_split, 1)

            with pool.Fori(0, NT) as t:
                for p in range(PAIRS + 1):
                    pool.wait_ge(s_ev, t * SLOTS + min(3 * p + 3, SLOTS))
                    g, u, c = act_g[:, p % RING, :], act_u[:, p % RING, :], act_c[:, p % RING, :]
                    if p < PAIRS:
                        if p > 0:
                            pool.wait_ge(s_h, t * (PAIRS + 1) + p)
                        pool.tensor_tensor(hid1[:, :], g, u, ALU.mult).then_inc(s_h1, 1)
                        pool.wait_ge(s_h1, t * PAIRS + (p + 1))
                        if p >= 2:
                            pool.wait_ge(s_dn, t * (PAIRS + 1) + (p - 1))
                        pool.tensor_tensor(hid[:, p % 2, :], hid1[:, :], c, ALU.mult).then_inc(s_h, 1)
                    else:
                        pool.wait_ge(s_dn, t * (PAIRS + 1) + (p - 1))
                        pool.tensor_tensor(hid[0:F0, p % 2, :], g[0:F0], u[0:F0], ALU.mult).then_inc(s_h, 1)

        @block.scalar
        def _(act):
            act.wait_ge(s_eps, 2)
            act.wait_ge(s_small, SMALL * 16)
            act.activation(wp[:, :, ZB], wbeta[:, :], ACT.Copy).then_inc(s_w12, 1)
            act.wait_ge(s_w1t_ps, 1)
            act.activation(wf1T[:, :, :], pb[0:HD0, 0, 0:2 * P].rearrange("p (a b) -> p a b", a=2), ACT.Copy).then_inc(s_w1t, 1)
            act.wait_ge(s_w12_ps, 1)
            for a, at in ((0, ZF), (1, ZG)):
                act.activation(wp[:, :, at:at + HD0], pb[:, 2, D * a:D * (a + 1)].rearrange("p (h c) -> p h c", h=H0),
                               ACT.Copy).then_inc(s_w12, 1)

            def norm(t):
                act.wait_ge(s_xc, t + 1)
                act.activation(xn[:, :, :], xc[:, :, :], ACT.Square).then_inc(s_sq, 1)
                act.wait_ge(s_var, t + 1)
                act.activation(stat[:, 3, :], stat[:, 2, :], ACT.Sqrt, bias=eps[:, 0:1], scale=1.0 / D).then_inc(s_std, 1)

            def project(t, par):
                act.wait_ge(s_xt_ps, t + 1)
                act.activation(xt_hi[par][:, :], pb[:, 0, :], ACT.Copy).then_inc(s_xth, 1)
                act.wait_ge(s_zst, t * (16 * NS * BS))
                for s in range(NS):
                    act.wait_ge(s_zp, t * NS + (s + 1))
                    at = 1024 * (s % 2)
                    act.activation(zs[:, s, :], pbf[:, at:at + ZW], ACT.Copy).then_inc(s_zc, 1)
                act.wait_ge(s_lg, t + 1)
                act.activation(scores[:, :, :], pb[:, 0, 0:NS * E0].rearrange("p (s e) -> p s e", s=NS),
                               ACT.Sigmoid).then_inc(s_sc, 1)

            def recurrence_inputs(t, par):
                act.wait_ge(s_zld, t * 16 + 16)
                act.activation(zr[par][:, :, ZF:ZC], zr[par][:, :, ZF:ZC], ACT.Sigmoid).then_inc(s_sig, 1)
                act.activation(zr[par][:, :, ZQ:ZF], zr[par][:, :, ZQ:ZF], ACT.Silu).then_inc(s_silu, 1)

            def key_norm(t):
                act.wait_ge(s_kk, t + 1)
                act.activation(coef[:, 0, :], coef[:, 0, :], ACT.Sqrt, bias=eps[:, 1:2]).then_inc(s_kn, 1)

            def tile(t, par, ahead):
                act.wait_ge(s_cwt_ps, t + 1)
                act.activation(cwt[:, :], pb[:, 1, :], ACT.Copy).then_inc(s_cwt, 1)
                act.wait_ge(s_gst, t * 16)
                act.wait_ge(s_split, len(chunks) + 1)
                for r in range(SLOTS):
                    p, what = r // 3, r % 3
                    n = P if p < PAIRS else F0
                    if ahead and r == NORM_SLOT:
                        norm(t + 1)
                    if ahead and r == 3 * PROJECT_PAIR:
                        project(t + 1, 1 - par)
                    if ahead and r == INPUT_SLOT:
                        recurrence_inputs(t + 1, 1 - par)
                    act.wait_ge(s_slot, t * SLOTS + (r + 1))
                    if what == 0 and p >= RING:
                        act.wait_ge(s_h, t * (PAIRS + 1) + (p - RING + 1))
                    dst = (act_g, act_u, act_c)[what][0:n, p % RING, :]
                    act.activation(dst, pb[0:n, r % 4, :], ACT.Silu if what == 0 else ACT.Copy).then_inc(s_ev, 1)
                act.wait_ge(s_dn, (t + 1) * (PAIRS + 1))
                act.activation(yt, pb[:, 4, :], ACT.Copy).then_inc(s_y, 1)
                act.wait_ge(s_g_ps, t + 1)
                act.activation(g_out, pb[:, 0, :].rearrange("p (s c) -> p s c", s=NS), ACT.Silu).then_inc(s_g, 1)
                act.wait_ge(s_yy, t + 1)
                act.activation(coef[:, 5, :], coef[:, 5, :], ACT.Sqrt, bias=eps[:, 1:2], scale=1.0 / HD0).then_inc(s_yn, 1)
                if ahead:
                    key_norm(t + 1)

            norm(0)
            project(0, 0)
            recurrence_inputs(0, 0)
            key_norm(0)
            with act.Fori(0, NT // 2 - 1) as i:
                tile(i * 2, 0, True)
                tile(i * 2 + 1, 1, True)
            tile(NT - 2, 0, True)
            tile(NT - 1, 1, False)

        @block.tensor
        def _(pe):
            def split3(out, l_hi, l_lo, r_hi, r_lo, first=True):
                pe.matmul(out, l_hi, r_hi, start=first, stop=False, skip_group_check=True)
                pe.matmul(out, l_hi, r_lo, start=False, stop=False, skip_group_check=True)
                return pe.matmul(out, l_lo, r_hi, start=False, stop=True, skip_group_check=True)

            pe.wait_ge(s_small, SMALL * 16)
            for a in range(2):
                pe.transpose(pb[0:HD0, 0, P * a:P * (a + 1)], wf1[:, a, :], ident[:, :])
            last = pe.transpose(pb[:, 1, 0:E0], gate_w[:, :], ident[0:E0, 0:E0])
            last.then_inc(s_w1t_ps, 1)
            pe.wait_ge(s_w1t, 1)
            for a in range(2):
                last = pe.matmul(pb[:, 2, D * a:D * (a + 1)], wf1T[:, a, :], wf2[:, a, :], start=(a == 0), stop=(a == 1), skip_group_check=True)
            last.then_inc(s_w12_ps, 1)
            pe.wait_ge(s_wp, 4)

            def project(t, par):
                pe.wait_ge(s_xn, t + 1)
                for s in range(NS):
                    last = pe.transpose(pb[:, 0, P * s:P * (s + 1)], xn[:, s, :], ident[:, :])
                last.then_inc(s_xt_ps, 1)
                pe.wait_ge(s_xtl, t + 1)
                for s in range(NS):
                    if s >= 2:
                        pe.wait_ge(s_zc, t * NS + (s - 1))
                    xs = slice(P * s, P * (s + 1))
                    at = 1024 * (s % 2)
                    for lo, hi in ((0, 512), (512, ZW)):
                        last = split3(pbf[:, at + lo:at + hi], xt_hi[par][:, xs], xt_lo[par][:, xs], wp_hi[:, lo:hi], wp_lo[:, lo:hi])
                    last.then_inc(s_zp, 1)
                pe.wait_ge(s_zc, t * NS + (NS - 1))
                for s in range(NS):
                    xs = slice(P * s, P * (s + 1))
                    last = split3(pb[:, 0, E0 * s:E0 * (s + 1)], xt_hi[par][:, xs], xt_lo[par][:, xs], wr_hi[:, :], wr_lo[:, :], first=(s == 0))
                last.then_inc(s_lg, 1)

            def experts(t, par, ahead):
                pe.wait_ge(s_cws, t + 1)
                pe.wait_ge(s_ev, t * SLOTS)
                pe.wait_ge(s_zc, t * NS + NS)
                pe.wait_ge(s_sc, t + 1)
                pe.wait_ge(s_g, t)
                for s in range(NS):
                    last = pe.transpose(pb[:, 1, P * s:P * (s + 1)], cws[:, s, :].bitcast(F32), ident[:, :])
                last.then_inc(s_cwt_ps, 1)
                pe.wait_ge(s_cwt, t + 1)
                pe.wait_ge(s_sel, 1)
                pe.wait_ge(s_wd, 32)

                def down(p):
                    n = P if p < PAIRS else F0
                    pe.wait_ge(s_h, t * (PAIRS + 1) + (p + 1))
                    last = pe.matmul(pb[:, 4, :], wd[0:n, p, :], hid[0:n, p % 2, :], start=(p == 0), stop=(p == PAIRS), skip_group_check=True)
                    last.then_inc(s_dn, 1)
                    return last

                def slot_free(r):
                    if r >= 4:
                        pe.wait_ge(s_ev, t * SLOTS + (r - 3))

                LAG = 2
                for p in range(PAIRS + 1):
                    if ahead and p == PROJECT_PAIR:
                        pe.wait_ge(s_ev, t * SLOTS + 3 * p)
                        project(t + 1, 1 - par)
                        pe.wait_ge(s_zc, (t + 2) * NS)
                        pe.wait_ge(s_sc, t + 2)
                    pe.wait_ge(s_split, 2 * (2 * p // CH + 1))
                    for what, (w_hi, w_lo) in enumerate(((wg_hi, wg_lo), (wu_hi, wu_lo))):
                        r = 3 * p + what
                        slot_free(r)
                        if p < PAIRS:
                            at = slice(2 * F0 * p, 2 * F0 * (p + 1))
                            last = split3(pb[:, r % 4, :], w_hi[:, at], w_lo[:, at], xt_hi[par][:, :], xt_lo[par][:, :])
                        else:
                            at = slice(E0 * F0, (E0 + 1) * F0)
                            last = split3(pb[0:F0, r % 4, :], w_hi[:, at], w_lo[:, at], xt_hi[par][:, :], xt_lo[par][:, :])
                        last.then_inc(s_slot, 1)
                    if p < PAIRS:
                        r = 3 * p + 2
                        slot_free(r)
                        pe.matmul(pb[:, r % 4, :], sel[:, 2 * p:2 * p + 2, :].rearrange("p a b -> p (a b)"), cwt[:, :], start=True, stop=True).then_inc(s_slot, 1)
                    if p >= LAG:
                        down(p - LAG)
                for p in range(PAIRS + 1 - LAG, PAIRS + 1):
                    last = down(p)
                pe.wait_ge(s_y, t + 1)
                for s in range(NS):
                    last = pe.transpose(pb[:, 0, P * s:P * (s + 1)], yt[:, P * s:P * (s + 1)], ident[:, :])
                last.then_inc(s_g_ps, 1)

            project(0, 0)
            with pe.Fori(0, NT // 2 - 1) as i:
                experts(i * 2, 0, True)
                experts(i * 2 + 1, 1, True)
            experts(NT - 2, 0, True)
            experts(NT - 1, 1, False)

        @block.vector
        def _(dve):
            def over(ap, n):
                return ap.unsqueeze(len(ap.shape)).to_broadcast([*ap.shape, n])

            dve.memset(rs[:, :, :, :], 0.0).then_inc(s_s0, 1)
            dve.wait_ge(s_small, SMALL * 16)
            dve.tensor_copy(sel[:, :, :], over(onehot[:, :], F0)).then_inc(s_sel, 1)
            dve.wait_ge(s_w12, 3)
            wpf = wp[:, :, :].rearrange("p h c -> p (h c)")
            dve.tensor_copy(wp_hi[:, :], wpf).then_inc(s_wp, 1)
            dve.tensor_copy(wr_hi[:, :], pb[:, 1, 0:E0]).then_inc(s_wp, 1)
            dve.wait_ge(s_wp, 2)
            dve.tensor_tensor(wp_lo[:, :], wpf, wp_hi[:, :].bitcast(F32), ALU.subtract).then_inc(s_wp, 1)
            dve.tensor_tensor(wr_lo[:, :], pb[:, 1, 0:E0], wr_hi[:, :].bitcast(F32), ALU.subtract).then_inc(s_wp, 1)
            dve.wait_ge(s_s0, 1)

            def layer_norm(t, par, stage):
                if stage == 0:
                    dve.wait_ge(s_x, (t + 1) * (16 * BS))
                    dve.tensor_reduce(stat[:, 0, :], x_sb[:, :, :], AX.X, ALU.add).then_inc(s_ln, 1)
                    dve.wait_ge(s_ln, t * LN + 1)
                    dve.tensor_scalar(stat[:, 1, :], stat[:, 0, :], -1.0 / D, None, ALU.mult).then_inc(s_ln, 1)
                    dve.wait_ge(s_ln, t * LN + 2)
                    dve.tensor_tensor(xc[:, :, :], x_sb[:, :, :], over(stat[:, 1, :], D), ALU.add).then_inc(s_xc, 1)
                elif stage == 1:
                    dve.wait_ge(s_sq, t + 1)
                    dve.tensor_reduce(stat[:, 2, :], xn[:, :, :], AX.X, ALU.add).then_inc(s_var, 1)
                elif stage == 2:
                    dve.wait_ge(s_std, t + 1)
                    dve.reciprocal(stat[:, 4, :], stat[:, 3, :]).then_inc(s_ln, 1)
                    dve.wait_ge(s_ln, t * LN + 3)
                    dve.tensor_tensor(xn[:, :, :], xc[:, :, :], over(stat[:, 4, :], D), ALU.mult).then_inc(s_xn, 1)
                else:
                    dve.wait_ge(s_xth, t + 1)
                    dve.tensor_tensor(xt_lo[par][:, :], pb[:, 0, :], xt_hi[par][:, :].bitcast(F32), ALU.subtract).then_inc(s_xtl, 1)

            def route(t):
                c = Count(t, ROUTE)
                dve.wait_ge(s_sc, t + 1)
                dve.tensor_tensor(biased[:, :, :], scores[:, :, :], bias64[:, :].unsqueeze(1).to_broadcast([P, NS, E0]), ALU.add).then_inc(s_rt, 1)
                dve.wait_ge(s_rt, c.next())
                dve.memset(carrier[:, :], 0.0)
                groups = biased[:, :, :].rearrange("p s (g e) -> p (s g) e", g=G0)
                for i in range(NS * G0):
                    dve.max(top_of_group[:, i, :], groups[:, i, :]).then_inc(s_rt, 1)
                dve.wait_ge(s_rt, c.next(NS * G0))
                tog = top_of_group[:, :, :].rearrange("p (s g) e -> p s g e", s=NS)
                dve.tensor_tensor(group_score[:, :, :], tog[:, :, :, 0], tog[:, :, :, 1], ALU.add).then_inc(s_rt, 1)
                dve.wait_ge(s_rt, c.next())
                mine = over(group_score[:, :, :], G0)
                other = group_score[:, :, :].unsqueeze(2).to_broadcast([P, NS, G0, G0])
                dve.tensor_tensor(cmp_gt[:, :, :, :], other, mine, ALU.is_gt).then_inc(s_rt, 1)
                dve.tensor_tensor(cmp_eq[:, :, :, :], other, mine, ALU.is_equal).then_inc(s_rt, 1)
                dve.wait_ge(s_rt, c.next(2))
                eq = cmp_eq[:, :, :, :].rearrange("p s g h -> p s (g h)")
                dve.tensor_tensor(eq, eq, tri[:, :].unsqueeze(1).to_broadcast([P, NS, G0 * G0]), ALU.mult).then_inc(s_rt, 1)
                dve.wait_ge(s_rt, c.next())
                dve.tensor_tensor(cmp_gt[:, :, :, :], cmp_gt[:, :, :, :], cmp_eq[:, :, :, :], ALU.add).then_inc(s_rt, 1)
                dve.wait_ge(s_rt, c.next())
                dve.tensor_reduce(penalty[:, :, :], cmp_gt[:, :, :, :], AX.X, ALU.add).then_inc(s_rt, 1)
                dve.wait_ge(s_rt, c.next())
                dve.tensor_scalar(penalty[:, :, :], penalty[:, :, :], float(TG0), NEG, ALU.is_ge, ALU.mult).then_inc(s_rt, 1)
                dve.wait_ge(s_rt, c.next())
                m4 = masked[:, :, :].rearrange("p s (g e) -> p s g e", g=G0)
                dve.tensor_tensor(m4, biased[:, :, :].rearrange("p s (g e) -> p s g e", g=G0), over(penalty[:, :, :], EG0), ALU.add).then_inc(s_rt, 1)
                dve.wait_ge(s_rt, c.next())
                dve.memset(carrier[:, :], 0.0)
                for s in range(NS):
                    dve.max(top8[:, s, :], masked[:, s, :]).then_inc(s_rt, 1)
                dve.wait_ge(s_rt, c.next(NS))
                dve.memset(carrier[:, :], 0.0)
                for s in range(NS):
                    dve.match_replace(replaced[:, s, :], top8[:, s, :], masked[:, s, :], 2 * NEG).then_inc(s_rt, 1)
                dve.wait_ge(s_rt, c.next(NS))
                dve.tensor_tensor(replaced[:, :, :], replaced[:, :, :], masked[:, :, :], ALU.not_equal).then_inc(s_rt, 1)
                dve.wait_ge(s_rt, c.next())
                dve.tensor_tensor(cw[:, :, :], replaced[:, :, :], scores[:, :, :], ALU.mult).then_inc(s_rt, 1)
                dve.wait_ge(s_rt, c.next())
                dve.tensor_reduce(cw_sum[:, :], cw[:, :, :], AX.X, ALU.add).then_inc(s_rt, 1)
                dve.wait_ge(s_rt, c.next())
                dve.tensor_scalar(cw_sum[:, :], cw_sum[:, :], 1e-20, None, ALU.add).then_inc(s_rt, 1)
                dve.wait_ge(s_rt, c.next())
                dve.reciprocal(cw_sum[:, :], cw_sum[:, :]).then_inc(s_rt, 1)
                dve.wait_ge(s_rt, c.next())
                dve.tensor_scalar(cw_sum[:, :], cw_sum[:, :], ROUTE_SCALE, None, ALU.mult).then_inc(s_rt, 1)
                dve.wait_ge(s_rt, c.next())
                dve.tensor_tensor(cw[:, :, :], cw[:, :, :], over(cw_sum[:, :], E0), ALU.mult).then_inc(s_rt, 1)
                dve.wait_ge(s_rt, c.next())
                dve.tensor_copy(cws[:, :, 0:E0], cw[:, :, :]).then_inc(s_rt, 1)
                dve.wait_ge(s_rt, c.next())
                dve.tensor_tensor(cws[:, :, E0:2 * E0], cw[:, :, :], cws[:, :, 0:E0].bitcast(F32), ALU.subtract).then_inc(s_cws, 1)
                c.check()

            def fields(par):
                return (zr[par][:, :, a:a + HD0] for a in (ZQ, ZK, ZV, ZF, ZG))

            knorm, neg_beta, w1_to_r, w1_to_o, r_to_o, ynorm = (coef[:, i, :] for i in range(6))

            def prepare_norm(t, par):
                q, k, v, f, g = fields(par)
                dve.wait_ge(s_silu, t + 1)
                dve.tensor_tensor(prod[:, :, :], k, k, ALU.mult).then_inc(s_pr, 1)
                dve.wait_ge(s_pr, t * PREP + 1)
                dve.tensor_reduce(knorm, prod[:, :, :], AX.X, ALU.add).then_inc(s_kk, 1)
                dve.wait_ge(s_sig, t + 1)
                dve.tensor_scalar(neg_beta, zr[par][:, :, ZB], -2.0, None, ALU.mult).then_inc(s_pr, 1)

            def prepare(t, par):
                q, k, v, f, g = fields(par)
                c = Count(t, PREP)
                c.next(2)
                dve.wait_ge(s_kn, t + 1)
                dve.reciprocal(knorm, knorm).then_inc(s_pr, 1)
                dve.wait_ge(s_pr, c.next())
                dve.tensor_tensor(k, k, over(knorm, HD0), ALU.mult).then_inc(s_pr, 1)
                dve.wait_ge(s_pr, c.next())
                dve.tensor_tensor(prod[:, :, :], f, k, ALU.mult).then_inc(s_pr, 1)
                dve.wait_ge(s_pr, c.next())
                dve.tensor_tensor(am[:, :, :], prod[:, :, :], over(neg_beta, HD0), ALU.mult).then_inc(s_pr, 1)
                dve.wait_ge(s_pr, c.next())
                for out, a, b in ((w1_to_r, am[:, :, :], k), (w1_to_o, am[:, :, :], q), (r_to_o, k, q)):
                    dve.tensor_tensor(prod[:, :, :], a, b, ALU.mult).then_inc(s_pr, 1)
                    dve.wait_ge(s_pr, c.next())
                    dve.tensor_reduce(out, prod[:, :, :], AX.X, ALU.add).then_inc(s_pr, 1)
                    dve.wait_ge(s_pr, c.next())
                dve.tensor_tensor(w1_to_r, w1_to_r, neg_beta, ALU.mult).then_inc(s_pr, 1)
                dve.wait_ge(s_pr, c.next())
                c.check()

            fs, ks, kfs, qfs = (ra[:, j] for j in range(4))
            state, part = rs[:, 0], rs[:, 1]

            def step(t, par, n):
                q, k, v, f, g = fields(par)
                at = t * (STEPS * TP) + STEPS * n
                row = lambda ap: ap[:, n:n + 1, :].to_broadcast([P, HD0, HD0])
                w1, w2, w3, r = (wh[:, n, j, :] for j in range(4))
                dve.wait_ge(s_st, at - 1 if n else at)
                dve.tensor_tensor(fs, row(f), state, ALU.mult).then_inc(s_st, 1)
                dve.tensor_tensor(ks, row(k), state, ALU.mult).then_inc(s_st, 1)
                dve.wait_ge(s_st, at + 1)
                dve.tensor_tensor(kfs, row(k), fs, ALU.mult).then_inc(s_st, 1)
                dve.wait_ge(s_st, at + 2)
                dve.tensor_reduce(w1, ks, AX.X, ALU.add).then_inc(s_st, 1)
                dve.wait_ge(s_st, at + 3)
                dve.tensor_reduce(w2, kfs, AX.X, ALU.add).then_inc(s_st, 1)
                dve.wait_ge(s_st, at + 4)
                dve.scalar_tensor_tensor(out=r, in0=w1, scalar=w1_to_r[:, n:n + 1], in1=v[:, n, :],
                                         op0=ALU.mult, op1=ALU.add).then_inc(s_st, 1)
                dve.tensor_tensor(x1[:, :, :], row(am), over(w1, HD0), ALU.mult).then_inc(s_st, 1)
                dve.wait_ge(s_st, at + 6)
                dve.scalar_tensor_tensor(out=r, in0=w2, scalar=neg_beta[:, n:n + 1], in1=r,
                                         op0=ALU.mult, op1=ALU.add).then_inc(s_st, 1)
                dve.wait_ge(s_st, at + 7)
                dve.tensor_tensor(part, fs, x1[:, :, :], ALU.add).then_inc(s_st, 1)
                dve.wait_ge(s_st, at + 8)
                dve.tensor_tensor(x2[:, :, :], row(k), over(r, HD0), ALU.mult).then_inc(s_st, 1)
                dve.tensor_tensor(qfs, row(q), fs, ALU.mult).then_inc(s_st, 1)
                dve.wait_ge(s_st, at + 10)
                dve.tensor_tensor(state, part, x2[:, :, :], ALU.add).then_inc(s_st, 1)
                dve.wait_ge(s_st, at + 11)
                dve.tensor_reduce(w3, qfs, AX.X, ALU.add).then_inc(s_st, 1)

            def finish(t, par):
                q, k, v, f, g = fields(par)
                c = Count(t, POST)
                w1, w3, r = (wh[:, :, j, :] for j in (0, 2, 3))
                dve.wait_ge(s_st, (t + 1) * (STEPS * TP))
                dve.tensor_tensor(prod[:, :, :], w1, over(w1_to_o, HD0), ALU.mult).then_inc(s_po, 1)
                dve.wait_ge(s_po, c.next())
                dve.wait_ge(s_yst, t * 16)
                dve.tensor_tensor(yo[:, :, :], prod[:, :, :], w3, ALU.add).then_inc(s_po, 1)
                dve.tensor_tensor(am[:, :, :], r, over(r_to_o, HD0), ALU.mult).then_inc(s_po, 1)
                dve.wait_ge(s_po, c.next(2))
                dve.tensor_tensor(yo[:, :, :], yo[:, :, :], am[:, :, :], ALU.add).then_inc(s_po, 1)
                dve.wait_ge(s_po, c.next())
                dve.tensor_tensor(yo[:, :, :], yo[:, :, :], g, ALU.mult).then_inc(s_po, 1)
                dve.wait_ge(s_po, c.next())
                dve.tensor_tensor(prod[:, :, :], yo[:, :, :], yo[:, :, :], ALU.mult).then_inc(s_po, 1)
                dve.wait_ge(s_po, c.next())
                dve.tensor_reduce(ynorm, prod[:, :, :], AX.X, ALU.add).then_inc(s_yy, 1)

            def finish_norm(t):
                dve.wait_ge(s_yn, t + 1)
                dve.reciprocal(ynorm, ynorm).then_inc(s_po, 1)
                dve.wait_ge(s_po, (t + 1) * POST)
                dve.tensor_tensor(yo[:, :, :], yo[:, :, :], over(ynorm, HD0), ALU.mult).then_inc(s_yo, 1)

            def tile(t, par, ahead):
                for n in range(TP):
                    step(t, par, n)
                    if ahead and n in LN_AT:
                        layer_norm(t + 1, 1 - par, LN_AT.index(n))
                    if ahead and n == ROUTE_AT:
                        route(t + 1)
                finish(t, par)
                if ahead:
                    dve.wait_ge(s_yy, t + 1)
                    prepare_norm(t + 1, 1 - par)
                finish_norm(t)
                if ahead:
                    prepare(t + 1, 1 - par)

            for stage in range(4):
                layer_norm(0, 0, stage)
            route(0)
            prepare_norm(0, 0)
            prepare(0, 0)
            with dve.Fori(0, NT // 2 - 1) as i:
                tile(i * 2, 0, True)
                tile(i * 2 + 1, 1, True)
            tile(NT - 2, 0, True)
            tile(NT - 1, 1, False)


def layer1(nc, d, scratch, out_dram, sem):
    y_dram, g_dram, x2_dram, g1_dram = scratch
    with ExitStack() as ctx:
        def sb(name, shape, dt=F32):
            return ctx.enter_context(nc.sbuf_tensor("l1_" + name, shape, dt))

        NB = B + 1
        ident = sb("ident", [P, P])
        ident_b, mask_b = sb("ident_b", [P, P], BF16), sb("mask_b", [P, P], BF16)
        rot = sb("rot", [P, P])
        rows = sb("rows", [2 * E1 + 4, P])
        cols = sb("cols", [P, 2 * E1 + 4])
        rcols = sb("rcols", [P, 2])
        eps = sb("eps", [P, 2])
        carrier = sb("carrier", [P, 1])
        wo0 = sb("wo0", [P, D])
        wproj = sb("wproj", [P, 2, D])
        wqk = sb("wqk", [P, 2, 4, D], F32R)
        wqk_hi, wqk_lo = wqk[:, 0], wqk[:, 1]
        wkv = sb("wkv", [P, P])
        wkv_hi, wkv_lo = sb("wkv_hi", [P, P], F32R), sb("wkv_lo", [P, P], F32R)
        gate = sb("gate", [P, E1])
        gate_hi, gate_lo = sb("gate_hi", [P, E1], F32R), sb("gate_lo", [P, E1], F32R)
        b2 = sb("b2", [P, D])
        wv = sb("wv", [P, D])
        wo = sb("wo", [P, D])
        bo = sb("bo", [P, D])
        ones = sb("ones", [P, P])
        cosT, sinT = sb("cosT", [P, N]), sb("sinT", [P, N])
        big0 = sb("big0", [P, E1 * F1], F32R)
        big1 = sb("big1", [P, E1 * F1], F32R)
        big2 = sb("big2", [P, E1 * F1])
        w1_hi, w1_lo = big0, big1
        w2 = big2[:, :].rearrange("p (e a n) -> p e a n", e=E1, a=2)
        qh, ql = sb("qh", [P, B, N], F32R), sb("ql", [P, B, N], F32R)
        kh, kl = sb("kh", [P, B, N], F32R), sb("kl", [P, B, N], F32R)
        ckvT = sb("ckvT", [P, B, N])
        xs = sb("xs", [P, NS, D])
        ys = sb("ys", [P, NS, D])
        gs = sb("gs", [P, NS, D])
        yT = sb("yT", [P, TOK])
        xc = sb("xc", [P, NS, D])
        xn = sb("xn", [P, NS, D])
        stat = sb("stat", [P, 5, NS])
        xt = [sb(f"xt{i}", [P, 2, TOK], F32R) for i in range(2)]
        rope = sb("rope", [P, 3, TOK])
        logits = sb("logits", [P, NS, E1])
        raw = sb("raw", [P, NS, E1])
        top8 = sb("top8", [P, NS, 8])
        replaced = sb("replaced", [P, NS, E1])
        row1 = sb("row1", [P, 2, NS])
        gtok = [sb(f"gtok{i}", [P, NS, E1]) for i in range(2)]
        gT = sb("gT", [P, TOK])
        HR = 4
        hid = sb("hid", [P, HR, TOK])
        acc = sb("acc", [P, NS, D])
        qb = [b[:, :].rearrange("p (h n) -> p h n", h=H1) for b in (big0, big1)]
        kr = xt[0][:, :, :].rearrange("p a n -> p (a n)"), wqk[:, :, :, :].rearrange("p a j n -> p (a j n)")
        rep = sb("rep", [P, 4, 4, P], F32R)
        STAGED = 2 * TOK
        rep_stage = rope[:, 0:2, :].rearrange("p a b -> p (a b)")
        esel = sb("esel", [P, H1, P], F32R)
        qmask = sb("qmask", [P, 4])
        mrow = sb("mrow", [P, 2, H1])
        mhl = sb("mhl", [P, 2, P], F32R)
        mT = [sb(f"mT{i}", [P, N], F32R) for i in range(2)]
        place = 0

        def carve(pattern, **sizes):
            nonlocal place
            n = int(np.prod(list(sizes.values())))
            place += n
            assert place <= E1 * F1
            return big2[:, place - n:place].rearrange(pattern, **sizes)

        ckv_b = carve("p (o n) -> p o n", o=1, n=N)[:, 0, :]
        VC = P // 4
        vp = [hid[:, 2 * i:2 * i + 2, :].rearrange("p k (h c) -> p k h c", h=H1) for i in range(2)]
        pt = carve("p (a n) -> p a n", a=4, n=3 * N)
        o_raw = rope[:, 0:2, :]
        rec = sb("rec", [P, 2, H1])
        o_tok = carve("p (k c) -> p k c", k=2, c=D)
        oT = carve("p (o n) -> p o n", o=1, n=N)[:, 0, :]
        x2b = xs[:, 0:2, :], xs[:, 2:4, :]
        g1b = gs[:, 0:2, :], gs[:, 2:4, :]
        prodb = ys[:, 0:2, :]
        outb = ys[:, 2:4, :]
        pb = ctx.enter_context(nc.psum_tensor("l1_pb", [P, 8, 512], F32))
        pbf = pb[:, :, :].rearrange("p a b -> p (a b)")

        s_w = sem("m_weights_loaded")
        s_w1 = sem("m_w1_loaded")
        s_w1b = sem("m_w1_second_half_loaded")
        s_w2 = sem("m_w2_loaded")
        s_init = sem("m_constants_set")
        s_cols_ps = sem("m_columns_in_psum")
        s_cols = sem("m_columns_ready")
        s_prep = sem("m_weights_split")
        s_w1s = sem("m_w1_split")
        s_x = sem("m_x_loaded")
        s_yld = sem("m_y_loaded")
        s_gld = sem("m_gate_loaded")
        s_yt_ps = sem("m_yT_in_psum")
        s_yt = sem("m_yT_ready")
        s_s_ps = sem("m_mixed_in_psum")
        s_ln = sem("m_ln_chain")
        s_x2 = sem("m_x2_ready")
        s_x2st = sem("m_x2_stored")
        s_xc, s_sq, s_var, s_std, s_xn = (sem("m_" + n) for n in ("centred", "squared", "variance_summed", "std_ready", "normalised"))
        s_xt_ps, s_xth, s_xtl = sem("m_xT_in_psum"), sem("m_xT_hi_ready"), sem("m_xT_lo_ready")
        s_lg = sem("m_logits_in_psum")
        s_rt = sem("m_router_chain")
        s_peak = sem("m_logits_peak")
        s_cen = sem("m_logits_centred")
        s_exp = sem("m_logits_exp")
        s_gt = sem("m_gate_weights_ready")
        s_kv_ps, s_kv = sem("m_kv_in_psum"), sem("m_kv_ready")
        s_qk_ps = sem("m_qk_in_psum")
        s_rope = sem("m_rope_chain")
        s_rope_done = sem("m_rope_ready")
        s_gelu = sem("m_gelu_done")
        s_qkh = sem("m_qk_hi_ready")
        s_qkl = sem("m_qk_lo_ready")
        s_gT_ps, s_gT = sem("m_gate_weightsT_in_psum"), sem("m_gate_weightsT_ready")
        s_b2 = sem("m_gate_bias_in_psum")
        s_acc0 = sem("m_sum_started")
        s_w1o = sem("m_hidden_in_psum")
        s_hid = sem("m_hidden_ready")
        s_w2o = sem("m_expert_out_in_psum")
        s_acc = sem("m_expert_summed")
        s_g1, s_g1st = sem("m_gate1_ready"), sem("m_gate1_stored")
        s_rep_ld = sem("a_selectors_loaded")
        s_rep = sem("a_selectors_ready")
        s_x2l = [sem(f"a_x2_loaded{i}") for i in range(2)]
        s_g1l = [sem(f"a_gate1_loaded{i}") for i in range(2)]
        s_ckb = sem("a_latent_copied")
        s_ua = sem("a_unit_in_psum")
        s_ua_act = sem("a_unit_read_by_act")
        s_ua_dve = sem("a_unit_read_by_dve")
        s_mc = sem("a_max_chain")
        s_mz = sem("a_max_parts_zeroed")
        s_mhl = sem("a_max_split")
        s_st = sem("a_scoresT_in_psum")
        s_pt = sem("a_probs_ready")
        s_pv = sem("a_probs_used")
        s_rec = sem("a_sums_inverted")
        s_raw = sem("a_raw_out_copied")
        s_tb = sem("a_raw_out_transposed")
        s_ot = sem("a_out_ready")
        s_oT_ps, s_oT = sem("a_outT_in_psum"), sem("a_outT_ready")
        s_wo = sem("a_wo_in_psum")
        s_fin = sem("a_final_chain")
        s_done = sem("a_out_final")
        s_ost = sem("a_out_stored")

        PE_AT = {1: "yT", 3: "mix", 9: "xT", 12: "router"}
        ACT_AT = {5: "yT", 12: "square", 15: "sqrt", 20: "xT", 30: "exp"}
        MIX_AT, CENTRE_AT, SELECT_AT = (3, 5, 6, 9), 13, (8, 10, 12, 14)
        NW = 21
        LN, ROPE, ROUTE = 4, 4, NS + 10
        PREP = 18
        UNITS = ["k"] * 2 + ["q_dve", "q_act"] + ["max0"] * 8 + ["max1"] * 8 + ["v", "mT"]
        NU = len(UNITS)
        BY_ACT = [u in ("k", "q_act", "v", "mT") for u in UNITS]
        N_ACT, N_DVE = sum(BY_ACT), NU - sum(BY_ACT)
        XU = H1 // 2
        O_RAW, O_TB, O_NORM, O_OT, O_WO, O_END = 0, 1, 3, 5, 6, 7

        def read(b, i):
            if BY_ACT[i]:
                return s_ua_act, b * N_ACT + sum(BY_ACT[:i + 1])
            return s_ua_dve, b * N_DVE + (i + 1 - sum(BY_ACT[:i + 1]))

        block = ctx.enter_context(nc.Block())

        @block.sync
        def _(sp):
            def w(dst, src):
                sp.dma_start(dst, src).then_inc(s_w, 16)

            row = lambda name: d[name].rearrange("(o c) -> o c", o=1)
            w(ident[:, :], d["c_ident"])
            w(rot[:, :], d["c_rot"])
            w(qmask[:, :], d["c_qmask"])
            w(rope[:, 1, 0:P], d["c_mask"])
            xr = d["L0_attn_x"].rearrange("(s b) (t n) d -> t b n s d", b=BS, n=TP)

            def load(t):
                for b in range(BS):
                    sp.dma_start(xs[TP * b:TP * (b + 1), :, :], xr[bass.ds(t, 1), b].rearrange("o n s d -> (o n) s d")).then_inc(s_x, 16)
                for s in range(NS):
                    for b in range(BS):
                        src = y_dram[bass.ds(t, 1), (s * BS + b) * H0:(s * BS + b + 1) * H0]
                        sp.dma_start(ys[TP * b:TP * (b + 1), s, :].rearrange("p (h c) -> p h c", h=H0),
                                     src.rearrange("o h n c -> (o n) h c")).then_inc(s_yld, 16)
                sp.dma_start(gs[:, :, :], g_dram[bass.ds(t, 1)].rearrange("o s p c -> (o p) s c")).then_inc(s_gld, 16)

            load(0)
            sp.wait_ge(s_init, 9)
            w(rows[0:2 * E1, :], d["L1_ffn_b1"].rearrange("e (a p) -> (e a) p", a=2))
            w(rows[2 * E1:2 * E1 + 1, :], row("L1_attn_bqr"))
            w(rows[2 * E1 + 1:2 * E1 + 2, :], row("L1_attn_bkr"))
            w(rows[2 * E1 + 2:2 * E1 + 3, :], row("L0_attn_norm_w"))
            w(rows[2 * E1 + 3:2 * E1 + 4, 0:DC1], row("L1_attn_bkv"))
            w(wo0[:, :], d["L0_attn_Wo"])
            w(wproj[:, 0, :], d["L1_attn_wqr"])
            w(wproj[:, 1, :], d["L1_attn_wkr"])
            w(gate[:, :], d["L1_ffn_gate"])
            w(b2[0:E1, :], d["L1_ffn_b2"])
            w(wv[0:DC1, :], d["L1_attn_wv"])
            w(wv[DC1:DC1 + 1, :], row("L1_attn_bv"))
            w(wo[:, :], d["L1_attn_wo"])
            w(bo[0:1, :], row("L1_attn_bo"))
            w(cosT[:, :], d["c_cosT"])
            w(sinT[:, :], d["c_sinT"])
            w(wkv[:, 0:DC1], d["L1_attn_wkv"])
            for half, ready in enumerate((s_w1, s_w1b)):
                at = slice(half * (E1 // 2), (half + 1) * (E1 // 2))
                sp.dma_start(ckvT[:, at, :], d["L1_ffn_W1"][at].rearrange("e i f -> i e f")).then_inc(ready, 16)
            for a in range(2):
                sp.dma_start(w2[:, :, a, :], d["L1_ffn_W2"].rearrange("e (a f) n -> a f e n", a=2)[a]).then_inc(s_w2, 16)

            def store_tile(dst, src, t, signal):
                r = dst.rearrange("(s b) (t n) d -> t b n s d", b=BS, n=TP)
                for b in range(BS):
                    sp.dma_start(r[bass.ds(t, 1), b].rearrange("o n s d -> (o n) s d"), src[TP * b:TP * (b + 1)]).then_inc(signal, 16)

            def pass_x2(t, more):
                sp.wait_ge(s_x2, t + 1)
                store_tile(x2_dram, xs[:, :, :], t, s_x2st)
                if more:
                    sp.wait_ge(s_x2st, (t + 1) * (16 * BS))
                    sp.wait_ge(s_xc, t + 1)
                    load(t + 1)

            def store_gate(t):
                sp.wait_ge(s_g1, t + 1)
                store_tile(g1_dram, acc[:, :, :], t, s_g1st)

            pass_x2(0, True)
            with sp.Fori(0, NT - 2) as t:
                pass_x2(t + 1, True)
                store_gate(t)
            pass_x2(NT - 1, False)
            store_gate(NT - 2)
            sp.wait_ge(s_qkl, NT * 2)
            for i in range(4):
                if i:
                    sp.wait_ge(s_rep, i)
                sp.dma_start(rep_stage, d[("c_rep", "c_esel")[i // 2]][:, STAGED * (i % 2):STAGED * (i % 2 + 1)]).then_inc(s_rep_ld, 16)
            store_gate(NT - 1)
            sp.wait_ge(s_x2st, NT * (16 * BS))
            sp.wait_ge(s_g1st, NT * 16 * BS)

            def load_b(b, par):
                view = lambda dram: dram[bass.ds(b, 1)].rearrange("o (k n) d -> n (o k) d", k=2)
                sp.dma_start(x2b[par], view(x2_dram)).then_inc(s_x2l[par], 16)
                sp.dma_start(g1b[par], view(g1_dram)).then_inc(s_g1l[par], 16)

            load_b(0, 0)
            load_b(1, 1)

            def finish(b, par, more):
                sp.wait_ge(s_done, b + 1)
                sp.dma_start(out_dram[bass.ds(b, 1)].rearrange("o (k n) d -> n (o k) d", k=2), outb).then_inc(s_ost, 16)
                if more:
                    load_b(b + 2, par)

            with sp.Fori(0, B // 2 - 1) as i:
                for par in range(2):
                    finish(i * 2 + par, par, True)
            finish(B - 2, 0, False)
            finish(B - 1, 1, False)
            sp.wait_ge(s_ost, B * 16)

        @block.gpsimd
        def _(pool):
            zeroed = rows[:, :], wkv[:, :], b2[:, :], wv[:, :], bo[:, :], ones[:, :], gT[:, :]
            for i, (buffer, value) in enumerate((*((z, 0.0) for z in zeroed), (eps[:, 0:1], LN_EPS), (ones[0:1, :], 1.0))):
                if i:
                    pool.wait_ge(s_init, i)
                pool.memset(buffer, value).then_inc(s_init, 1)
            pool.wait_ge(s_init, 9)
            pool.wait_ge(s_w1s, 4)
            pool.memset(ckvT[DC1:DC1 + 1, :, :], 1.0).then_inc(s_init, 1)
            pool.wait_ge(s_init, 10)
            with pool.Fori(0, NT) as t:
                at = bass.ds(t * TP, TP)
                for j, (hi, lo) in enumerate(((qh, ql), (kh, kl))):
                    pool.wait_ge(s_qkh, t * 2 + (j + 1))
                    pool.tensor_tensor(lo[:, :, at], rope[:, 2 * j, :].rearrange("p (b n) -> p b n", n=TP), hi[:, :, at].bitcast(F32), ALU.subtract).then_inc(s_qkl, 1)
            pool.wait_ge(s_w2o, NT * E1)
            pool.memset(ckv_b, 0.0).then_inc(s_init, 1)
            for i in range(2):
                pool.wait_ge(s_init, 11 + 2 * i)
                pool.memset(vp[i], 0.0).then_inc(s_init, 1)
                pool.wait_ge(s_init, 12 + 2 * i)
                pool.memset(vp[i][:, :, :, HD1:HD1 + 1], 1.0).then_inc(s_init, 1)

        @block.scalar
        def _(act):
            act.wait_ge(s_w, NW * 16)
            act.wait_ge(s_cols_ps, 1)
            act.activation(cols[:, :], pb[:, 0, 0:2 * E1 + 4], ACT.Copy).then_inc(s_cols, 1)
            act.wait_ge(s_cols_ps, 2)
            act.activation(rcols[:, :], pb[:, 1, 0:2], ACT.Copy).then_inc(s_cols, 1)
            act.wait_ge(s_cols, 2)
            act.wait_ge(s_init, 9)

            def front(t, par, stage):
                if stage == "yT":
                    act.wait_ge(s_yt_ps, t + 1)
                    act.activation(yT[:, :], pb[:, 0, :], ACT.Copy, scale=cols[:, 2 * E1 + 2:2 * E1 + 3]).then_inc(s_yt, 1)
                elif stage == "square":
                    act.wait_ge(s_xc, t + 1)
                    act.activation(xn[:, :, :], xc[:, :, :], ACT.Square).then_inc(s_sq, 1)
                elif stage == "sqrt":
                    act.wait_ge(s_var, t + 1)
                    act.activation(stat[:, 3, :], stat[:, 2, :], ACT.Sqrt, bias=eps[:, 0:1], scale=1.0 / D).then_inc(s_std, 1)
                elif stage == "xT":
                    act.wait_ge(s_xt_ps, t + 1)
                    act.activation(xt[par][:, 0, :], pb[:, 0, :], ACT.Copy).then_inc(s_xth, 1)
                elif stage == "exp":
                    act.wait_ge(s_cen, t + 1)
                    act.activation(raw[:, :, :], logits[:, :, :], ACT.Exp).then_inc(s_exp, 1)

            def tile(t, par, ahead):
                act.wait_ge(s_kv_ps, t + 1)
                act.wait_ge(s_w1s, 4)
                at = bass.ds(t * TP, TP)
                act.activation(ckvT[0:DC1, :, at], pb[0:DC1, 0, :].rearrange("p (b n) -> p b n", n=TP), ACT.Gelu,
                               bias=cols[0:DC1, 2 * E1 + 3:2 * E1 + 4]).then_inc(s_kv, 1)
                act.wait_ge(s_gT_ps, t + 1)
                act.activation(gT[0:E1, :], pb[0:E1, 1, :], ACT.Copy).then_inc(s_gT, 1)
                act.wait_ge(s_b2, t + 1)
                act.wait_ge(s_g1st, t * (16 * BS))
                act.activation(acc[:, :, :], pb[:, 7, :].rearrange("p (s c) -> p s c", s=NS), ACT.Copy).then_inc(s_acc0, 1)
                for r in range(2 * E1):
                    if r == 2:
                        for j in range(2):
                            act.wait_ge(s_rope_done, t * 2 + (j + 1))
                            act.activation(rope[:, 2 * j, :], rope[:, 2 * j, :], ACT.Gelu).then_inc(s_gelu, 1)
                    if r in (6, 8):
                        j = r // 2 - 3
                        act.wait_ge(s_gelu, t * 2 + (j + 1))
                        act.activation((qh, kh)[j][:, :, at], rope[:, 2 * j, :].rearrange("p (b n) -> p b n", n=TP), ACT.Copy).then_inc(s_qkh, 1)
                    if ahead and r in ACT_AT:
                        front(t + 1, 1 - par, ACT_AT[r])
                    act.wait_ge(s_w1o, t * (2 * E1) + (r + 1))
                    if r >= HR:
                        act.wait_ge(s_w2o, t * E1 + ((r - HR) // 2 + 1))
                    act.activation(hid[:, r % HR, :], pb[:, 2 + r % 3, :], ACT.Relu, bias=cols[:, r:r + 1]).then_inc(s_hid, 1)
                act.wait_ge(s_acc, t * (NS * E1) + NS * E1)
                act.activation(acc[:, :, :], acc[:, :, :], ACT.Silu).then_inc(s_g1, 1)

            for stage in ("yT", "square", "sqrt", "xT", "exp"):
                front(0, 0, stage)
            with act.Fori(0, NT // 2 - 1) as i:
                tile(i * 2, 0, True)
                tile(i * 2 + 1, 1, True)
            tile(NT - 2, 0, True)
            tile(NT - 1, 1, False)

            def a_unit(b, par, i):
                if i == 0:
                    act.activation(ckv_b[0:DC1 + 1, :], ckvT[0:DC1 + 1, bass.ds(b, 1), :].rearrange("p o n -> p (o n)"), ACT.Copy).then_inc(s_ckb, 1)
                if not BY_ACT[i]:
                    return
                src = pb[:, i % 2, :]
                act.wait_ge(s_ua, b * NU + (i + 1))
                if UNITS[i] == "k":
                    act.activation(kr[par][:, 512 * i:512 * (i + 1)], src, ACT.Copy).then_inc(s_ua_act, 1)
                elif UNITS[i] == "q_act":
                    for h in range(H1 // 2, H1):
                        g, j = h // 4 - 2, h % 4
                        last = act.activation(qb[par][:, h, :], src[:, N * g:N * (g + 1)], ACT.Copy, scale=qmask[:, j:j + 1])
                    last.then_inc(s_ua_act, 1)
                elif UNITS[i] == "v":
                    act.activation(vp[par][:, :, :, 0:HD1], src[:, 0:2 * D].rearrange("p (k h c) -> p k h c", k=2, h=H1),
                                   ACT.Copy).then_inc(s_ua_act, 1)
                else:
                    act.activation(mT[par][:, :], src[:, 0:N], ACT.Copy).then_inc(s_ua_act, 1)

            def x_unit(b, par, u):
                act.wait_ge(s_st, b * XU + (u + 1))
                act.wait_ge(s_pv, b * (XU // 2) + max(u // 2 - 1, 0))
                at = 512 * (2 + 2 * (u % 2)) + N
                act.activation(pt[:, u % 4, :], pbf[:, at:at + 3 * N], ACT.Exp, scale=float(1.0 / np.sqrt(HD1))).then_inc(s_pt, 1)

            def o_unit(b, i):
                if i == O_RAW:
                    act.wait_ge(s_pv, (b + 1) * (XU // 2))
                    act.activation(o_raw, pb[:, 6:8, :], ACT.Copy).then_inc(s_raw, 1)
                if i == O_WO:
                    act.wait_ge(s_oT_ps, b + 1)
                    act.activation(oT[:, :], pb[:, 6, 0:N], ACT.Copy).then_inc(s_oT, 1)

            def both(ba, bx, bo, pa, px, po):
                for i in range(NU):
                    if bo is not None:
                        o_unit(bo, i)
                    if ba is not None:
                        a_unit(ba, pa, i)
                    if bx is not None and i % 2 == 0 and i // 2 < XU:
                        x_unit(bx, px, i // 2)

            act.wait_ge(s_init, 15)
            act.wait_ge(s_w2o, NT * E1)
            act.wait_ge(s_kv, NT)
            act.wait_ge(s_rep, 4)
            both(0, None, None, 0, None, None)
            both(1, 0, None, 1, 0, None)
            with act.Fori(0, B // 2 - 1) as i:
                both(i * 2 + 2, i * 2 + 1, i * 2, 0, 1, 0)
                both(i * 2 + 3, i * 2 + 2, i * 2 + 1, 1, 0, 1)
            both(None, B - 1, B - 2, None, 1, 0)
            both(None, None, B - 1, None, None, 1)

        @block.tensor
        def _(pe):
            def mm(out, l, r, start=True, stop=True):
                return pe.matmul(out, l, r, start=start, stop=stop, skip_group_check=True)

            def split3(out, l_hi, l_lo, r_hi, r_lo):
                mm(out, l_hi, r_hi, stop=False)
                mm(out, l_hi, r_lo, start=False, stop=False)
                return mm(out, l_lo, r_hi, start=False)

            pe.wait_ge(s_w, NW * 16)
            pe.transpose(pb[:, 0, 0:2 * E1 + 4], rows[:, :], ident[0:2 * E1 + 4, 0:2 * E1 + 4]).then_inc(s_cols_ps, 1)
            pe.wait_ge(s_cols, 1)
            mm(pb[:, 1, 0:2], rot[:, :], cols[:, 2 * E1:2 * E1 + 2]).then_inc(s_cols_ps, 1)
            pe.wait_ge(s_cols, 2)
            pe.wait_ge(s_prep, PREP)

            sub = [slice(P * s, P * (s + 1)) for s in range(NS)]

            def front(t, par, stage):
                hi, lo = xt[par][:, 0, :], xt[par][:, 1, :]
                if stage == "yT":
                    pe.wait_ge(s_yld, (t + 1) * (16 * NS * BS))
                    pe.wait_ge(s_kv, t)
                    for s in range(NS):
                        last = pe.transpose(pb[:, 0, sub[s]], ys[:, s, :], ident[:, :])
                    last.then_inc(s_yt_ps, 1)
                elif stage == "mix":
                    pe.wait_ge(s_yt, t + 1)
                    pe.wait_ge(s_gT, t)
                    for s in range(NS):
                        last = mm(pb[:, 1, sub[s]], yT[:, sub[s]], wo0[:, :])
                    last.then_inc(s_s_ps, 1)
                elif stage == "xT":
                    pe.wait_ge(s_xn, t + 1)
                    for s in range(NS):
                        last = pe.transpose(pb[:, 0, sub[s]], xn[:, s, :], ident[:, :])
                    last.then_inc(s_xt_ps, 1)
                else:
                    pe.wait_ge(s_xtl, t + 1)
                    for s in range(NS):
                        last = split3(pb[:, 1, E1 * s:E1 * (s + 1)], hi[:, sub[s]], lo[:, sub[s]], gate_hi[:, :], gate_lo[:, :])
                    last.then_inc(s_lg, 1)
                    split3(pb[:, 0, :], wkv_hi[:, :], wkv_lo[:, :], hi, lo).then_inc(s_kv_ps, 1)

            def tile(t, par, ahead):
                hi, lo = xt[par][:, 0, :], xt[par][:, 1, :]
                pe.wait_ge(s_acc, t * (NS * E1))
                for j in range(4):
                    split3(pb[:, 2 + j, :], wqk_hi[:, j, :], wqk_lo[:, j, :], hi, lo).then_inc(s_qk_ps, 1)
                pe.wait_ge(s_gt, t + 1)
                for s in range(NS):
                    last = pe.transpose(pb[0:E1, 1, sub[s]], gtok[par][:, s, :], ident[:, :])
                last.then_inc(s_gT_ps, 1)
                pe.wait_ge(s_w1s, 4)
                pe.wait_ge(s_w2, 32)
                for e in range(E1 + 1):
                    if ahead and e in PE_AT:
                        front(t + 1, 1 - par, PE_AT[e])
                    if e < E1:
                        for a in range(2):
                            r = 2 * e + a
                            if r == 0:
                                pe.wait_ge(s_rope_done, t * 2 + 1)
                            elif r == 2:
                                pe.wait_ge(s_rope_done, t * 2 + 2)
                            if r >= 3:
                                pe.wait_ge(s_hid, t * (2 * E1) + (r - 2))
                            at = slice(P * r, P * (r + 1))
                            split3(pb[:, 2 + r % 3, :], w1_hi[:, at], w1_lo[:, at], hi, lo).then_inc(s_w1o, 1)
                    if e == 0:
                        pe.wait_ge(s_gT, t + 1)
                        for s in range(NS):
                            last = mm(pb[:, 7, sub[s]], gT[:, sub[s]], b2[:, :])
                        last.then_inc(s_b2, 1)
                    if e > 0:
                        x = e - 1
                        pe.wait_ge(s_hid, t * (2 * E1) + (2 * x + 2))
                        if x >= 2:
                            pe.wait_ge(s_acc, t * (NS * E1) + NS * (x - 1))
                        for s in range(NS):
                            for a in range(2):
                                last = mm(pb[:, 5 + x % 2, sub[s]], hid[:, (2 * x + a) % HR, sub[s]], w2[:, x, a, :],
                                          start=(a == 0), stop=(a == 1))
                        last.then_inc(s_w2o, 1)

            for stage in PE_AT.values():
                front(0, 0, stage)
            with pe.Fori(0, NT // 2 - 1) as i:
                tile(i * 2, 0, True)
                tile(i * 2 + 1, 1, True)
            tile(NT - 2, 0, True)
            tile(NT - 1, 1, False)

            def a_unit(b, par, i):
                u, bank = UNITS[i], pb[:, i % 2, :]
                if i >= 2:
                    pe.wait_ge(*read(b, i - 2))
                else:
                    pe.wait_ge(s_ua_act, b * N_ACT)
                if u == "k" or u[0] == "q":
                    hi, lo, kind = (kh, kl, 2) if u == "k" else (qh, ql, 0)
                    for g in range(2):
                        group = 2 * (i % 2) + g
                        out = bank[:, N * g:N * (g + 1)]
                        mm(out, rep[:, kind, group, :], hi[:, bass.ds(b, 1), :].rearrange("p o n -> p (o n)"), stop=False)
                        last = mm(out, rep[:, kind + 1, group, :], lo[:, bass.ds(b, 1), :].rearrange("p o n -> p (o n)"), start=False)
                elif u == "v":
                    pe.wait_ge(s_ckb, b + 1)
                    for k in range(2):
                        last = mm(bank[:, D * k:D * (k + 1)], ckv_b[:, P * k:P * (k + 1)], wv[:, :])
                elif u[0:3] == "max":
                    j, k = i - UNITS.index(u), int(u[3])
                    if u == "max0" and j == 0:
                        pe.wait_ge(*read(b, 0))
                        pe.wait_ge(*read(b, 2))
                    elif u == "max0" and j == XU // 2:
                        pe.wait_ge(*read(b, 3))
                    for m in range(2):
                        h, out = 2 * j + m, bank[:, N * m:N * (m + 1)]
                        mm(out, qb[par][:, h, P * k:P * (k + 1)], kr[par][:, N * (h // 4):N * (h // 4 + 1)], stop=False)
                        last = mm(out[:, P * k:P * (k + 1)], ident_b[:, :], mask_b[:, :], start=False)
                else:
                    pe.wait_ge(s_mhl, b + 1)
                    for k in range(2):
                        last = pe.transpose(bank[:, P * k:P * (k + 1)], mhl[:, k, :].bitcast(F32), ident[:, :])
                last.then_inc(s_ua, 1)

            def scores_t(b, par, u):
                if u == 0:
                    pe.wait_ge(s_ua_act, (b + 1) * N_ACT)
                    pe.wait_ge(s_pt, b * XU)
                elif u >= 2:
                    pe.wait_ge(s_pt, b * XU + (u - 1))
                bank = 512 * (2 + 2 * (u % 2))
                for k, m, lo in ((1, 1, N), (1, 0, P), (0, 0, 2 * N), (0, 1, 3 * N)):
                    h = 2 * u + m
                    keys = N * (h // 4) + P * k
                    out = pbf[:, bank + lo:bank + lo + N]
                    mm(out, kr[par][:, keys:keys + P], qb[par][:, h, :], stop=False)
                    mm(out, esel[:, h, :], mT[par][:, :], start=False, stop=False)
                    last = mm(out[:, P * k:P * (k + 1)], mask_b[:, :], ident_b[:, :], start=False)
                last.then_inc(s_st, 1)

            def values(b, par, u):
                pe.wait_ge(s_pt, b * XU + (u + 2))
                if u == 0:
                    pe.wait_ge(s_done, b)
                out = pb[:, 6 + u // 4, N * (u // 2 % 2):N * (u // 2 % 2 + 1)]
                for k in range(2):
                    for m in range(4):
                        p = pt[:, (u + m // 2) % 4, :]
                        p = p[:, P * (m % 2):P * (m % 2 + 1)] if k else p[:, N * (1 + m % 2):N * (2 + m % 2)]
                        last = pe.matmul(out[VC * m:VC * (m + 1), P * k:N], vp[par][:, k, 2 * u + m, :], p, start=(k == 0), stop=(k == 1),
                                         skip_group_check=True, tile_position=(0, VC * m))
                last.then_inc(s_pv, 1)

            def o_unit(b, i):
                if i == O_TB:
                    pe.wait_ge(s_raw, b + 1)
                    for g in range(4):
                        for k in range(2):
                            src = o_raw[:, g // 2, N * (g % 2) + P * k:N * (g % 2) + P * (k + 1)]
                            last = pe.transpose(pb[:, 6 + k, P * g:P * (g + 1)], src, ident[:, :])
                    last.then_inc(s_tb, 1)
                if i == O_OT:
                    pe.wait_ge(s_ot, b + 1)
                    for k in range(2):
                        last = pe.transpose(pb[:, 6, P * k:P * (k + 1)], o_tok[:, k, :], ident[:, :])
                    last.then_inc(s_oT_ps, 1)
                if i == O_WO:
                    pe.wait_ge(s_oT, b + 1)
                    for k in range(2):
                        out = pb[:, 7, D * k:D * (k + 1)]
                        mm(out, oT[:, P * k:P * (k + 1)], wo[:, :], stop=False)
                        last = mm(out, ones[:, :], bo[:, :], start=False)
                    last.then_inc(s_wo, 1)

            def both(ba, bx, bo_, pa, px, po):
                for i in range(NU):
                    if bx is not None and i % 2 == 0:
                        u = i // 2
                        if u < XU:
                            scores_t(bx, px, u)
                        if u % 2 == 0 and 0 <= u - 4 < XU:
                            values(bx, px, u - 4)
                    if bo_ is not None:
                        o_unit(bo_, i)
                    if ba is not None:
                        a_unit(ba, pa, i)
            pe.wait_ge(s_rep, 4)
            pe.wait_ge(s_qkl, NT * 2)
            both(0, None, None, 0, None, None)
            both(1, 0, None, 1, 0, None)
            with pe.Fori(0, B // 2 - 1) as i:
                both(i * 2 + 2, i * 2 + 1, i * 2, 0, 1, 0)
                both(i * 2 + 3, i * 2 + 2, i * 2 + 1, 1, 0, 1)
            both(None, B - 1, B - 2, None, 1, 0)
            both(None, None, B - 1, None, None, 1)

        @block.vector
        def _(dve):
            def over(ap, n):
                return ap.unsqueeze(len(ap.shape)).to_broadcast([*ap.shape, n])

            half = D // 2
            dve.wait_ge(s_w, NW * 16)
            dve.wait_ge(s_init, 9)
            for j in range(2):
                w, hi = wproj[:, j, :], wqk_hi[:, 2 * j, :]
                dve.tensor_copy(hi, w).then_inc(s_prep, 1)
                dve.tensor_scalar(wqk_hi[:, 2 * j + 1, 0:half], w[:, half:D], -1.0, None, ALU.mult).then_inc(s_prep, 1)
                dve.tensor_copy(wqk_hi[:, 2 * j + 1, half:D], w[:, 0:half]).then_inc(s_prep, 1)
                dve.wait_ge(s_prep, 6 * j + 3)
                whole = hi.bitcast(F32)
                dve.tensor_tensor(wqk_lo[:, 2 * j, :], w, whole, ALU.subtract).then_inc(s_prep, 1)
                dve.tensor_tensor(wqk_lo[:, 2 * j + 1, 0:half], whole[:, half:D], w[:, half:D], ALU.subtract).then_inc(s_prep, 1)
                dve.tensor_tensor(wqk_lo[:, 2 * j + 1, half:D], w[:, 0:half], whole[:, 0:half], ALU.subtract).then_inc(s_prep, 1)
            dve.tensor_copy(wkv_hi[:, :], wkv[:, :]).then_inc(s_prep, 1)
            dve.tensor_copy(gate_hi[:, :], gate[:, :]).then_inc(s_prep, 1)
            dve.tensor_copy(ident_b[:, :], ident[:, :]).then_inc(s_prep, 1)
            dve.tensor_copy(mask_b[:, :], rope[:, 1, 0:P]).then_inc(s_prep, 1)
            dve.wait_ge(s_prep, 16)
            dve.tensor_tensor(wkv_lo[:, :], wkv[:, :], wkv_hi[:, :].bitcast(F32), ALU.subtract).then_inc(s_prep, 1)
            dve.tensor_tensor(gate_lo[:, :], gate[:, :], gate_hi[:, :].bitcast(F32), ALU.subtract).then_inc(s_prep, 1)
            dve.memset(mhl[:, :, :].bitcast(F32), 0.0).then_inc(s_mz, 1)
            dve.wait_ge(s_mz, 1)
            dve.wait_ge(s_cols, 2)

            def mix(t, par, stage):
                if stage == 0:
                    dve.wait_ge(s_gld, t * 16 + 16)
                    dve.wait_ge(s_x, (t + 1) * (16 * BS))
                    dve.wait_ge(s_s_ps, t + 1)
                    dve.tensor_tensor(xc[:, :, :], pb[:, 1, :].rearrange("p (s c) -> p s c", s=NS), gs[:, :, :], ALU.mult).then_inc(s_ln, 1)
                    dve.wait_ge(s_ln, t * LN + 1)
                    dve.tensor_tensor(xs[:, :, :], xs[:, :, :], xc[:, :, :], ALU.add).then_inc(s_x2, 1)
                    dve.wait_ge(s_x2, t + 1)
                    dve.tensor_reduce(stat[:, 0, :], xs[:, :, :], AX.X, ALU.add).then_inc(s_ln, 1)
                    dve.wait_ge(s_ln, t * LN + 2)
                    dve.tensor_scalar(stat[:, 1, :], stat[:, 0, :], -1.0 / D, None, ALU.mult).then_inc(s_ln, 1)
                    dve.wait_ge(s_ln, t * LN + 3)
                    dve.tensor_tensor(xc[:, :, :], xs[:, :, :], over(stat[:, 1, :], D), ALU.add).then_inc(s_xc, 1)
                elif stage == 1:
                    dve.wait_ge(s_sq, t + 1)
                    dve.tensor_reduce(stat[:, 2, :], xn[:, :, :], AX.X, ALU.add).then_inc(s_var, 1)
                elif stage == 2:
                    dve.wait_ge(s_std, t + 1)
                    dve.reciprocal(stat[:, 4, :], stat[:, 3, :]).then_inc(s_ln, 1)
                    dve.wait_ge(s_ln, t * LN + 4)
                    dve.tensor_tensor(xn[:, :, :], xc[:, :, :], over(stat[:, 4, :], D), ALU.mult).then_inc(s_xn, 1)
                else:
                    dve.wait_ge(s_xth, t + 1)
                    dve.tensor_tensor(xt[par][:, 1, :], pb[:, 0, :], xt[par][:, 0, :].bitcast(F32), ALU.subtract).then_inc(s_xtl, 1)

            def turn(t):
                dve.wait_ge(s_qkl, t * 2)
                at = bass.ds(t * TP, TP)
                for j in range(2):
                    for m, (bias, table) in enumerate(((cols[:, 2 * E1 + j:2 * E1 + j + 1], cosT), (rcols[:, j:j + 1], sinT))):
                        dve.wait_ge(s_qk_ps, t * 4 + (2 * j + m + 1))
                        if (j, m) == (1, 1):
                            dve.wait_ge(s_rope_done, t * 2 + 1)
                        dst = rope[:, (2 * j, 1)[m], :].rearrange("p (b n) -> p b n", n=TP)
                        dve.scalar_tensor_tensor(out=dst, in0=pb[:, 2 + 2 * j + m, :].rearrange("p (b n) -> p b n", n=TP), scalar=bias,
                                                 in1=table[:, at].unsqueeze(1).to_broadcast([P, B, TP]),
                                                 op0=ALU.add, op1=ALU.mult).then_inc(s_rope, 1)
                    dve.wait_ge(s_rope, t * ROPE + 2 * (j + 1))
                    dve.tensor_tensor(rope[:, 2 * j, :], rope[:, 2 * j, :], rope[:, 1, :], ALU.add).then_inc(s_rope_done, 1)

            peak, total = row1[:, 0, :], row1[:, 1, :]

            def centre(t):
                lg = pb[:, 1, 0:NS * E1].rearrange("p (s e) -> p s e", s=NS)
                dve.wait_ge(s_lg, t + 1)
                dve.tensor_reduce(peak, lg, AX.X, ALU.max).then_inc(s_peak, 1)
                dve.wait_ge(s_peak, t + 1)
                dve.tensor_tensor(logits[:, :, :], lg, over(peak, E1), ALU.subtract).then_inc(s_cen, 1)

            def route(t, par):
                c = Count(t, ROUTE)
                dve.wait_ge(s_exp, t + 1)
                dve.tensor_reduce(total, raw[:, :, :], AX.X, ALU.add).then_inc(s_rt, 1)
                dve.wait_ge(s_rt, c.next())
                dve.reciprocal(total, total).then_inc(s_rt, 1)
                dve.wait_ge(s_rt, c.next())
                dve.tensor_tensor(raw[:, :, :], raw[:, :, :], over(total, E1), ALU.mult).then_inc(s_rt, 1)
                dve.wait_ge(s_rt, c.next())
                dve.memset(carrier[:, :], 0.0)
                for s in range(NS):
                    dve.max(top8[:, s, :], raw[:, s, :]).then_inc(s_rt, 1)
                dve.wait_ge(s_rt, c.next(NS))
                dve.memset(top8[:, :, K1:8], -1.0).then_inc(s_rt, 1)
                dve.wait_ge(s_rt, c.next())
                dve.memset(carrier[:, :], 0.0)
                for s in range(NS):
                    last = dve.match_replace(replaced[:, s, :], top8[:, s, :], raw[:, s, :], -2.0)
                last.then_inc(s_rt, 1)
                dve.wait_ge(s_rt, c.next())
                dve.tensor_tensor(replaced[:, :, :], replaced[:, :, :], raw[:, :, :], ALU.not_equal).then_inc(s_rt, 1)
                dve.wait_ge(s_rt, c.next())
                dve.tensor_tensor(raw[:, :, :], replaced[:, :, :], raw[:, :, :], ALU.mult).then_inc(s_rt, 1)
                dve.wait_ge(s_rt, c.next())
                dve.tensor_reduce(total, raw[:, :, :], AX.X, ALU.add).then_inc(s_rt, 1)
                dve.wait_ge(s_rt, c.next())
                dve.tensor_scalar(total, total, 1e-12, None, ALU.max).then_inc(s_rt, 1)
                dve.wait_ge(s_rt, c.next())
                dve.reciprocal(total, total).then_inc(s_rt, 1)
                dve.wait_ge(s_rt, c.next())
                dve.tensor_tensor(gtok[par][:, :, :], raw[:, :, :], over(total, E1), ALU.mult).then_inc(s_gt, 1)
                c.check()

            def selectors(i):
                dst = (rep[:, :, :, :].rearrange("p k g r -> p (k g r)"), esel[:, :, :].rearrange("p h m -> p (h m)"))[i // 2]
                dve.wait_ge(s_rep_ld, 16 * (i + 1))
                dve.tensor_copy(dst[:, STAGED * (i % 2):STAGED * (i % 2 + 1)], rep_stage).then_inc(s_rep, 1)

            def experts(t, par, ahead):
                dve.wait_ge(s_gt, t + 1)
                dve.wait_ge(s_acc0, t + 1)
                for e in range(E1):
                    if ahead and e in MIX_AT:
                        mix(t + 1, 1 - par, MIX_AT.index(e))
                    if ahead and e == CENTRE_AT:
                        centre(t + 1)
                    if not ahead and e in SELECT_AT:
                        selectors(SELECT_AT.index(e))
                    dve.wait_ge(s_w2o, t * E1 + (e + 1))
                    for s in range(NS):
                        sub = slice(P * s, P * (s + 1))
                        if e:
                            dve.wait_ge(s_acc, t * (NS * E1) + (NS * (e - 1) + s + 1))
                        dve.scalar_tensor_tensor(out=acc[:, s, :], in0=pb[:, 5 + e % 2, sub], scalar=gtok[par][:, s, e:e + 1],
                                                 in1=acc[:, s, :], op0=ALU.mult, op1=ALU.add).then_inc(s_acc, 1)

            def tile(t, par, ahead):
                turn(t)
                experts(t, par, ahead)
                if ahead:
                    route(t + 1, 1 - par)

            for stage in range(4):
                mix(0, 0, stage)
            centre(0)
            route(0, 0)
            for i, ready in enumerate((s_w1, s_w1b)):
                dve.wait_ge(ready, 16)
                n = E1 * F1 // 2
                src = ckvT[:, i * (E1 // 2):(i + 1) * (E1 // 2), :].rearrange("p e f -> p (e f)")
                at = slice(n * i, n * (i + 1))
                dve.tensor_copy(w1_hi[:, at], src).then_inc(s_w1s, 1)
                dve.wait_ge(s_w1s, 2 * i + 1)
                dve.tensor_tensor(w1_lo[:, at], src, w1_hi[:, at].bitcast(F32), ALU.subtract).then_inc(s_w1s, 1)
            with dve.Fori(0, NT // 2 - 1) as i:
                tile(i * 2, 0, True)
                tile(i * 2 + 1, 1, True)
            tile(NT - 2, 0, True)
            tile(NT - 1, 1, False)

            def a_unit(b, par, i):
                if BY_ACT[i]:
                    return
                src, u = pb[:, i % 2, :], UNITS[i]
                dve.wait_ge(s_ua, b * NU + (i + 1))
                if u == "q_dve":
                    for g in range(2):
                        q = src[:, N * g:N * (g + 1)].unsqueeze(1).to_broadcast([P, 4, N])
                        last = dve.tensor_tensor(qb[par][:, 4 * g:4 * (g + 1), :], q, over(qmask[:, :], N), ALU.mult)
                    last.then_inc(s_ua_dve, 1)
                    return
                j, k = i - UNITS.index(u), int(u[3])
                src = src.rearrange("p (h n) -> p h n", h=2)[:, :, 0:P * (k + 1)]
                dve.tensor_reduce(mrow[:, k, 2 * j:2 * j + 2], src, AX.X, ALU.max).then_inc(s_ua_dve, 1)
                if i == NU - 3:
                    dve.wait_ge(s_ua_dve, (b + 1) * N_DVE)
                    dve.tensor_copy(mhl[:, :, 0:H1], mrow[:, :, :]).then_inc(s_mc, 1)
                    dve.wait_ge(s_mc, b + 1)
                    dve.tensor_tensor(mhl[:, :, H1:2 * H1], mrow[:, :, :], mhl[:, :, 0:H1].bitcast(F32), ALU.subtract).then_inc(s_mhl, 1)

            def o_unit(b, par, n, i):
                if i == O_NORM:
                    raw_o = pb[:, 6:8, :].rearrange("p k (h c) -> p k h c", h=H1)
                    dve.wait_ge(s_tb, b + 1)
                    dve.reciprocal(rec[:, :, :], raw_o[:, :, :, HD1]).then_inc(s_rec, 1)
                    dve.wait_ge(s_rec, b + 1)
                    o = o_tok.rearrange("p k (h c) -> p k h c", h=H1)
                    for k in range(2):
                        last = dve.tensor_tensor(o[:, k], raw_o[:, k, :, 0:HD1], over(rec[:, k, :], HD1), ALU.mult)
                    last.then_inc(s_ot, 1)
                if i == O_END:
                    dve.wait_ge(s_wo, b + 1)
                    dve.wait_ge(s_g1l[par], n * 16 + 16)
                    dve.tensor_tensor(prodb, pb[:, 7, 0:N].rearrange("p (k c) -> p k c", k=2), g1b[par], ALU.mult).then_inc(s_fin, 1)
                    dve.wait_ge(s_fin, b + 1)
                    dve.wait_ge(s_x2l[par], n * 16 + 16)
                    dve.wait_ge(s_ost, b * 16)
                    dve.tensor_tensor(outb, prodb, x2b[par], ALU.add).then_inc(s_done, 1)

            def both(ba, bo, pa, po, n):
                for i in range(NU):
                    if bo is not None:
                        o_unit(bo, po, n, i)
                    if ba is not None:
                        a_unit(ba, pa, i)

            both(0, None, 0, None, None)
            both(1, None, 1, None, None)
            with dve.Fori(0, B // 2 - 1) as n:
                both(n * 2 + 2, n * 2, 0, 0, n)
                both(n * 2 + 3, n * 2 + 1, 1, 1, n)
            both(None, B - 2, None, 0, B // 2 - 1)
            both(None, B - 1, None, 1, B // 2 - 1)


def build(nc, d, out):
    def scratch(name, *shape):
        return nc.dram_tensor(name, shape, F32).ap()

    z = scratch("z_scratch", NT, NS, BS, H0, TP, ZC)
    y = scratch("y_scratch", NT, P, TP, HD0)
    g0 = scratch("g0_scratch", NT, NS, P, D)
    x2 = scratch("x2_scratch", B, N, D)
    g1 = scratch("g1_scratch", B, N, D)
    with ExitStack() as ctx:
        def sem(name):
            return ctx.enter_context(nc.semaphore(name))

        layer0(nc, d, (z, y, g0), sem)
        layer1(nc, d, (y, g0, x2, g1), out, sem)


def constants():
    f = np.float32
    c = {
        "c_ident": np.eye(P, dtype=f),
        "c_onehot": np.tile(np.eye(E0, dtype=f), (2, 1)),
        "c_tri": np.tril(np.ones((G0, G0), f), -1).reshape(-1),
        "c_rot": np.roll(np.eye(P, dtype=f), D // 2, axis=1) * np.where(np.arange(P) < D // 2, 1, -1).astype(f)[:, None],
        "c_qmask": np.repeat(np.eye(4, dtype=f), P // 4, axis=0),
        "c_mask": np.where(np.arange(P)[None, :] > np.arange(P)[:, None], f(NEG), f(0)),
    }
    freq = (1.0 / 10000.0 ** (np.arange(0, D, 2, dtype=f) / f(D))).astype(f)
    angle = np.arange(N, dtype=f)[:, None] * freq[None, :]
    angle = np.concatenate([angle, angle], -1)
    c["c_cosT"] = np.ascontiguousarray(np.cos(angle).T)
    c["c_sinT"] = np.ascontiguousarray(np.sin(angle).T)
    rep = np.zeros((P, 4, 4, P), f)
    for kind, parts in enumerate(((0, 1), (2,), (0, 2), (1,))):
        for h in range(H1):
            for part in parts:
                for i in range(HD1):
                    rep[h * HD1 + i, kind, h // 4, 32 * (h % 4) + HD1 * part + i] = 1
    c["c_rep"] = rep.reshape(P, -1)
    esel = np.zeros((P // H1, H1, H1, P), f)
    for h in range(H1):
        esel[0:2, h, h, :] = -1
    c["c_esel"] = esel.reshape(P, -1)
    return c


UNUSED = ("L1_attn_wq", "L1_attn_bq", "L1_attn_wqc", "L1_attn_bqc", "L1_attn_wkc", "L1_attn_bkc")


def kernel(**inputs):
    import concourse.bacc as _bacc
    from concourse.bass_utils import run_bass_kernel_spmd as _run

    nc = _bacc.Bacc("TRN2", target_bir_lowering=False, num_devices=1)
    arrays, d = {}, {}
    for name, a in {**inputs, **constants()}.items():
        if name in UNUSED:
            continue
        a = np.ascontiguousarray(a)
        arrays[f"in_{name}_dram"] = a
        d[name] = nc.dram_tensor(f"in_{name}_dram", a.shape, mybir.dt.from_np(a.dtype), kind="ExternalInput").ap()
    out = nc.dram_tensor("out_0_dram", (B, N, D), F32, kind="ExternalOutput").ap()
    build(nc, d, out)
    r = _run(nc, [arrays], core_ids=[0])
    return r.results[0]["out_0_dram"]
```
